# Optimizing a Trainium2 kernel written in Bass

```python
import numpy as np
import jax
import jax.numpy as jnp

def _softmax(x, axis=-1):
    return jax.nn.softmax(x, axis=axis)

def _gelu(x):
    return jax.nn.gelu(x, approximate=True)

def _silu(x):
    return jax.nn.silu(x)

def _sigmoid(x):
    return jax.nn.sigmoid(x)

def _layernorm(x, axis=-1, eps=1e-05):
    m = jnp.mean(x, axis=axis, keepdims=True)
    v = jnp.var(x, axis=axis, keepdims=True)
    return (x - m) / jnp.sqrt(v + eps)

def _scatter_add(tgt, idx, src, axis=0):
    return tgt.at[idx].add(src)

def _segment_sum(src, seg, n):
    return jax.ops.segment_sum(src, seg, n)
kernel_name = 'mk_adaln_d2_jaxref_r8_31ac50'

def setup_inputs(seed: int=0):
    np.random.seed(seed)
    _w = jnp.asarray

    def _L0_attn_setup():
        import jax, jax.numpy as jnp
        import numpy as np
        N_HEADS = 16
        INPUT_DIM = 128
        EMBED_DIM = 128
        KEY_DIM = EMBED_DIM // N_HEADS
        BATCH = 4
        SEQ = 256

        def _uniform(key, shape, bound):
            return jax.random.uniform(key, shape, jnp.float32, -bound, bound)
        key = jax.random.key(seed)
        kq, k1, k2, k3, k4 = jax.random.split(key, 5)
        stdv_k = 1.0 / np.sqrt(KEY_DIM)
        stdv_e = 1.0 / np.sqrt(EMBED_DIM)
        return {'q': jax.random.normal(kq, (BATCH, SEQ, INPUT_DIM), jnp.float32), 'W_query': _uniform(k1, (N_HEADS, INPUT_DIM, KEY_DIM), stdv_k), 'W_key': _uniform(k2, (N_HEADS, INPUT_DIM, KEY_DIM), stdv_k), 'W_val': _uniform(k3, (N_HEADS, INPUT_DIM, KEY_DIM), stdv_k), 'W_out': _uniform(k4, (N_HEADS, KEY_DIM, EMBED_DIM), stdv_e)}
    _L0_attn_in = _L0_attn_setup()

    def _L0_ffn_setup():
        import jax, jax.numpy as jnp
        import numpy as np
        B, S, D = (4, 128, 128)
        I = 64
        E = 32
        TOP_K = 8
        N_GROUP = 8
        TOPK_GROUP = 4

        def _group_topk(scores):
            T = scores.shape[0]
            epg = E // N_GROUP
            group_scores = scores.reshape(T, N_GROUP, epg).sum(axis=-1)
            _, top_groups = jax.lax.top_k(group_scores, TOPK_GROUP)
            group_mask = jnp.zeros((T, N_GROUP), scores.dtype).at[jnp.arange(T)[:, None], top_groups].set(1.0)
            expert_mask = jnp.repeat(group_mask, epg, axis=1)
            masked_scores = scores * expert_mask
            topk_w, topk_i = jax.lax.top_k(masked_scores, TOP_K)
            return (topk_w, topk_i)

        def _reference_tuple_inner(hidden_states, gate_w, expert_gate, expert_up, expert_down, shared_gate_w, shared_up_w, shared_down_w):
            b, s, d = hidden_states.shape
            flat = hidden_states.reshape(-1, d)
            T = flat.shape[0]
            logits = flat @ gate_w.T
            scores = jax.nn.sigmoid(logits)
            topk_w, topk_i = _group_topk(scores)
            topk_w = topk_w / jnp.clip(topk_w.sum(axis=-1, keepdims=True), 1e-12)
            combine = jnp.zeros((T, E), flat.dtype).at[jnp.arange(T)[:, None], topk_i].add(topk_w)

            def body(acc, expert):
                wg, wu, wd, w = expert
                h = jax.nn.silu(flat @ wg.T) * (flat @ wu.T)
                return (acc + w[:, None] * (h @ wd.T), None)
            out, _ = jax.lax.scan(body, jnp.zeros_like(flat), (expert_gate, expert_up, expert_down, combine.T))
            shared = jax.nn.silu(flat @ shared_gate_w.T) * (flat @ shared_up_w.T) @ shared_down_w.T
            out = out + shared
            return (out.reshape(b, s, d), logits)
        key = jax.random.key(seed)
        ks = jax.random.split(key, 8)
        scale = 0.02
        return {'hidden_states': jax.random.normal(ks[0], (B, S, D), jnp.float32), 'gate_w': jax.random.normal(ks[1], (E, D), jnp.float32) * scale, 'expert_gate': jax.random.normal(ks[2], (E, I, D), jnp.float32) * scale, 'expert_up': jax.random.normal(ks[3], (E, I, D), jnp.float32) * scale, 'expert_down': jax.random.normal(ks[4], (E, D, I), jnp.float32) * scale, 'shared_gate_w': jax.random.normal(ks[5], (I, D), jnp.float32) * scale, 'shared_up_w': jax.random.normal(ks[6], (I, D), jnp.float32) * scale, 'shared_down_w': jax.random.normal(ks[7], (D, I), jnp.float32) * scale}
    _L0_ffn_in = _L0_ffn_setup()
    _L0_c = _w((lambda *s: np.random.randn(*s).astype(np.float32) * 0.05)(8, 128))
    _L0_wmod = _w((lambda *s: np.random.randn(*s).astype(np.float32) * 0.05)(128, 6 * 128) * 128 ** (-0.5))

    def _L1_attn_setup():
        import math
        import jax, jax.numpy as jnp
        import numpy as np
        EPS_SUM = 1e-07
        EPS_NORM = 1e-12

        def _l2norm(x, axis):
            n = jnp.sqrt(jnp.sum(x * x, axis=axis, keepdims=True))
            return x / jnp.maximum(n, EPS_NORM)
        key = jax.random.key(seed)
        ks = jax.random.split(key, 5)
        b, N, C = (4, 512, 128)
        x = jax.random.normal(ks[0], (b, N, C), dtype=jnp.float32)
        Wqkv = jax.random.normal(ks[1], (C, 3 * C), dtype=jnp.float32) / math.sqrt(C)
        bqkv = jax.random.normal(ks[2], (3 * C,), dtype=jnp.float32) * 0.01
        Wln = jax.random.normal(ks[3], (C, C), dtype=jnp.float32) / math.sqrt(C)
        bln = jax.random.normal(ks[4], (C,), dtype=jnp.float32) * 0.01
        return {'x': x, 'Wqkv': Wqkv, 'bqkv': bqkv, 'Wln': Wln, 'bln': bln}
    _L1_attn_in = _L1_attn_setup()

    def _L1_ffn_setup():
        import jax, jax.numpy as jnp
        import numpy as np
        EPS = 1e-12

        def rms_norm(t, gamma):
            n = jnp.maximum(jnp.linalg.norm(t, axis=-1, keepdims=True), EPS)
            scale = jnp.sqrt(jnp.asarray(t.shape[-1], t.dtype))
            return t / n * scale * gamma
        key = jax.random.key(seed)
        ks = jax.random.split(key, 4)
        b, s, d = (4, 512, 128)
        e, t = (8, 64)
        hidden = 4 * d
        return {'x': jax.random.normal(ks[0], (b, s, d), dtype=jnp.float32), 'gamma_x': jnp.ones((d,), dtype=jnp.float32), 'gamma_slot': jnp.ones((d,), dtype=jnp.float32), 'slot_embeds': jax.random.normal(ks[1], (e, t, d), dtype=jnp.float32), 'w1': jax.random.normal(ks[2], (d, hidden), dtype=jnp.float32) * (1.0 / np.sqrt(d)), 'w2': jax.random.normal(ks[3], (hidden, d), dtype=jnp.float32) * (1.0 / np.sqrt(hidden))}
    _L1_ffn_in = _L1_ffn_setup()
    _L1_c = _w((lambda *s: np.random.randn(*s).astype(np.float32) * 0.05)(8, 128))
    _L1_wmod = _w((lambda *s: np.random.randn(*s).astype(np.float32) * 0.05)(128, 6 * 128) * 128 ** (-0.5))
    _d = {'L0_attn_q': _L0_attn_in['q'], 'L0_attn_W_query': _L0_attn_in['W_query'], 'L0_attn_W_key': _L0_attn_in['W_key'], 'L0_attn_W_val': _L0_attn_in['W_val'], 'L0_attn_W_out': _L0_attn_in['W_out'], 'L0_ffn_gate_w': _L0_ffn_in['gate_w'], 'L0_ffn_expert_gate': _L0_ffn_in['expert_gate'], 'L0_ffn_expert_up': _L0_ffn_in['expert_up'], 'L0_ffn_expert_down': _L0_ffn_in['expert_down'], 'L0_ffn_shared_gate_w': _L0_ffn_in['shared_gate_w'], 'L0_ffn_shared_up_w': _L0_ffn_in['shared_up_w'], 'L0_ffn_shared_down_w': _L0_ffn_in['shared_down_w'], 'L0_c': _L0_c, 'L0_wmod': _L0_wmod, 'L1_attn_Wqkv': _L1_attn_in['Wqkv'], 'L1_attn_bqkv': _L1_attn_in['bqkv'], 'L1_attn_Wln': _L1_attn_in['Wln'], 'L1_attn_bln': _L1_attn_in['bln'], 'L1_ffn_gamma_x': _L1_ffn_in['gamma_x'], 'L1_ffn_gamma_slot': _L1_ffn_in['gamma_slot'], 'L1_ffn_slot_embeds': _L1_ffn_in['slot_embeds'], 'L1_ffn_w1': _L1_ffn_in['w1'], 'L1_ffn_w2': _L1_ffn_in['w2'], 'L1_c': _L1_c, 'L1_wmod': _L1_wmod}
    _x0 = _d['L0_attn_q']
    _d['L0_attn_q'] = jax.random.normal(jax.random.fold_in(jax.random.key(seed), 1), (8, 256, 128), dtype=_x0.dtype)
    del _x0
    return _d

def reference(L0_attn_q, L0_attn_W_query, L0_attn_W_key, L0_attn_W_val, L0_attn_W_out, L0_ffn_gate_w, L0_ffn_expert_gate, L0_ffn_expert_up, L0_ffn_expert_down, L0_ffn_shared_gate_w, L0_ffn_shared_up_w, L0_ffn_shared_down_w, L0_c, L0_wmod, L1_attn_Wqkv, L1_attn_bqkv, L1_attn_Wln, L1_attn_bln, L1_ffn_gamma_x, L1_ffn_gamma_slot, L1_ffn_slot_embeds, L1_ffn_w1, L1_ffn_w2, L1_c, L1_wmod):

    def _L0_attn_ref(q, W_query, W_key, W_val, W_out):
        import jax, jax.numpy as jnp
        import numpy as np
        N_HEADS = 16
        INPUT_DIM = 128
        EMBED_DIM = 128
        KEY_DIM = EMBED_DIM // N_HEADS
        BATCH = 4
        SEQ = 256

        def _uniform(key, shape, bound):
            return jax.random.uniform(key, shape, jnp.float32, -bound, bound)
        norm = 1.0 / np.sqrt(KEY_DIM)
        Q = jnp.einsum('bsd,hdk->hbsk', q, W_query)
        K = jnp.einsum('bsd,hdk->hbsk', q, W_key)
        V = jnp.einsum('bsd,hdv->hbsv', q, W_val)
        scores = norm * jnp.einsum('hbqk,hbnk->hbqn', Q, K)
        attn = jax.nn.softmax(scores, axis=-1)
        heads = jnp.einsum('hbqn,hbnv->hbqv', attn, V)
        out = jnp.einsum('hbqv,hve->bqe', heads, W_out)
        return out

    def _L0_ffn_ref(hidden_states, gate_w, expert_gate, expert_up, expert_down, shared_gate_w, shared_up_w, shared_down_w):
        import jax, jax.numpy as jnp
        import numpy as np
        B, S, D = (4, 128, 128)
        I = 64
        E = 32
        TOP_K = 8
        N_GROUP = 8
        TOPK_GROUP = 4

        def _group_topk(scores):
            T = scores.shape[0]
            epg = E // N_GROUP
            group_scores = scores.reshape(T, N_GROUP, epg).sum(axis=-1)
            _, top_groups = jax.lax.top_k(group_scores, TOPK_GROUP)
            group_mask = jnp.zeros((T, N_GROUP), scores.dtype).at[jnp.arange(T)[:, None], top_groups].set(1.0)
            expert_mask = jnp.repeat(group_mask, epg, axis=1)
            masked_scores = scores * expert_mask
            topk_w, topk_i = jax.lax.top_k(masked_scores, TOP_K)
            return (topk_w, topk_i)

        def _reference_tuple_inner(hidden_states, gate_w, expert_gate, expert_up, expert_down, shared_gate_w, shared_up_w, shared_down_w):
            b, s, d = hidden_states.shape
            flat = hidden_states.reshape(-1, d)
            T = flat.shape[0]
            logits = flat @ gate_w.T
            scores = jax.nn.sigmoid(logits)
            topk_w, topk_i = _group_topk(scores)
            topk_w = topk_w / jnp.clip(topk_w.sum(axis=-1, keepdims=True), 1e-12)
            combine = jnp.zeros((T, E), flat.dtype).at[jnp.arange(T)[:, None], topk_i].add(topk_w)

            def body(acc, expert):
                wg, wu, wd, w = expert
                h = jax.nn.silu(flat @ wg.T) * (flat @ wu.T)
                return (acc + w[:, None] * (h @ wd.T), None)
            out, _ = jax.lax.scan(body, jnp.zeros_like(flat), (expert_gate, expert_up, expert_down, combine.T))
            shared = jax.nn.silu(flat @ shared_gate_w.T) * (flat @ shared_up_w.T) @ shared_down_w.T
            out = out + shared
            return (out.reshape(b, s, d), logits)
        return _reference_tuple_inner(hidden_states, gate_w, expert_gate, expert_up, expert_down, shared_gate_w, shared_up_w, shared_down_w)[0]

    def _L1_attn_ref(x, Wqkv, bqkv, Wln, bln):
        import math
        import jax, jax.numpy as jnp
        import numpy as np
        EPS_SUM = 1e-07
        EPS_NORM = 1e-12

        def _l2norm(x, axis):
            n = jnp.sqrt(jnp.sum(x * x, axis=axis, keepdims=True))
            return x / jnp.maximum(n, EPS_NORM)
        b, N, C = x.shape
        qkv = x @ Wqkv + bqkv
        q, k, v = jnp.split(qkv, 3, axis=2)
        q = q - q.mean(axis=2, keepdims=True)
        k = k - k.mean(axis=2, keepdims=True)
        q2 = q * q
        k2 = k * k
        q2 = q2 / (q2.sum(axis=2, keepdims=True) + EPS_SUM)
        q2 = _l2norm(q2, axis=-1)
        k2 = k2 / (k2.sum(axis=2, keepdims=True) + EPS_SUM)
        k2 = _l2norm(k2, axis=-2)
        kv = jnp.einsum('bnc,bnd->bcd', k2, v)
        t2 = jnp.einsum('bnc,bcd->bnd', q2, kv) / math.sqrt(N)
        return (v + t2) @ Wln + bln

    def _L1_ffn_ref(x, gamma_x, gamma_slot, slot_embeds, w1, w2):
        import jax, jax.numpy as jnp
        import numpy as np
        EPS = 1e-12

        def rms_norm(t, gamma):
            n = jnp.maximum(jnp.linalg.norm(t, axis=-1, keepdims=True), EPS)
            scale = jnp.sqrt(jnp.asarray(t.shape[-1], t.dtype))
            return t / n * scale * gamma
        b, s, d = x.shape
        e, t, _ = slot_embeds.shape
        xn = rms_norm(x, gamma_x)
        se = rms_norm(slot_embeds, gamma_slot)
        logits = jnp.einsum('bsd,etd->bset', xn, se)
        dispatch = jax.nn.softmax(logits, axis=1)
        slots = jnp.einsum('bsd,bset->betd', xn, dispatch)
        h = jax.nn.gelu(slots @ w1, approximate=False)
        processed = h @ w2
        combine = jax.nn.softmax(logits.reshape(b, s, e * t), axis=-1)
        out = jnp.einsum('bnd,bsn->bsd', processed.reshape(b, e * t, d), combine)
        return out
    x = L0_attn_q
    mod = (_silu(L0_c) @ L0_wmod).reshape(L0_c.shape[0], 6, 1, -1)
    sa, ca, ga, sb, cb, gb = (mod[:, 0], mod[:, 1], mod[:, 2], mod[:, 3], mod[:, 4], mod[:, 5])
    ga = (2 * (ga >= 0) - 1) * jnp.maximum(jnp.abs(ga), 0.25)
    gb = (2 * (gb >= 0) - 1) * jnp.maximum(jnp.abs(gb), 0.25)
    h = _layernorm(x, axis=-1) * (1 + ca) + sa
    x = x + ga * _L0_attn_ref(h, L0_attn_W_query, L0_attn_W_key, L0_attn_W_val, L0_attn_W_out)
    h = _layernorm(x, axis=-1) * (1 + cb) + sb
    x = x + gb * _L0_ffn_ref(h, L0_ffn_gate_w, L0_ffn_expert_gate, L0_ffn_expert_up, L0_ffn_expert_down, L0_ffn_shared_gate_w, L0_ffn_shared_up_w, L0_ffn_shared_down_w)
    mod = (_silu(L1_c) @ L1_wmod).reshape(L1_c.shape[0], 6, 1, -1)
    sa, ca, ga, sb, cb, gb = (mod[:, 0], mod[:, 1], mod[:, 2], mod[:, 3], mod[:, 4], mod[:, 5])
    ga = (2 * (ga >= 0) - 1) * jnp.maximum(jnp.abs(ga), 0.25)
    gb = (2 * (gb >= 0) - 1) * jnp.maximum(jnp.abs(gb), 0.25)
    h = _layernorm(x, axis=-1) * (1 + ca) + sa
    x = x + ga * _L1_attn_ref(h, L1_attn_Wqkv, L1_attn_bqkv, L1_attn_Wln, L1_attn_bln)
    h = _layernorm(x, axis=-1) * (1 + cb) + sb
    x = x + gb * _L1_ffn_ref(h, L1_ffn_gamma_x, L1_ffn_gamma_slot, L1_ffn_slot_embeds, L1_ffn_w1, L1_ffn_w2)
    return x

_drawn_inputs = setup_inputs


def setup_inputs(seed=0):
    import zlib

    import numpy as np

    out = dict(_drawn_inputs(seed))
    spreads = {'L1_ffn_gamma_x': (1.0, 0.2), 'L1_ffn_gamma_slot': (1.0, 0.2)}
    factors = {'L0_ffn_gate_w': 8.0,
     'L0_ffn_expert_gate': 8.0,
     'L0_ffn_expert_up': 8.0,
     'L0_ffn_expert_down': 8.0,
     'L0_ffn_shared_gate_w': 8.0,
     'L0_ffn_shared_up_w': 8.0,
     'L0_ffn_shared_down_w': 8.0,
     'L1_attn_bqkv': 4.365,
     'L1_attn_bln': 27.794}
    for name, (base, spread) in spreads.items():
        noise = np.random.default_rng([zlib.crc32(name.encode()), seed]).standard_normal(out[name].shape)
        drawn = base * np.exp(spread * noise) if base else spread * noise
        out[name] = jnp.asarray(drawn.astype(out[name].dtype))
    for name, factor in factors.items():
        out[name] = (out[name] * factor).astype(out[name].dtype)
    return out
```

```python
from contextlib import ExitStack

import numpy as np
import concourse.bass as bass
from concourse import mybir

F32 = mybir.dt.float32
F32R = mybir.dt.float32r
ALU = mybir.AluOpType
ACT = mybir.ActivationFunctionType
AX = mybir.AxisListType

P = 128
B, S, D = 8, 256, 128
TB = S // P
TILES = B * TB
H, DK = 16, 8
HB = 4
HG = H // HB
STACK = P // HB
M_ROW = 3 * DK
E, I = 32, 64
EP = E // 2
TOPK, GROUPS, TOPG = 8, 8, 4
EPG = E // GROUPS
SB = 2
N2 = SB * S
SLOTS = 512
SC = SLOTS // P
HID = 512
HC = HID // P
LN_EPS = 1e-5
ATTN_SCALE = float(1.0 / np.sqrt(DK))

L0A, L0F, L1A, L1F = range(4)


def row_constants():
    part = np.arange(P) % STACK // DK
    row = np.arange(P) % STACK
    q_low = (part == 1).astype(np.float32)
    k_low = (part == 2).astype(np.float32)
    ones = ((row == M_ROW) | (row == M_ROW + 1)).astype(np.float32)
    return np.ascontiguousarray(np.stack([q_low, 1 - 2 * q_low, k_low, 1 - 2 * k_low, ones], axis=1))


def norm_vector_stats(nc, dve, s, name, x_tiles, stats, mv, n):
    k = len(x_tiles)
    for t, x in enumerate(x_tiles):
        nc.vector.bn_stats(stats[:, t, :], x).then_inc(s[name + "_stats"], 1)
    nc.vector.drain()
    for t in range(k):
        nc.vector.bn_aggr(mv[:, t, :], stats[:, t, :]).then_inc(s[name + "_mv"], 1)


def norm_pool_rstd(nc, pool, s, name, mv, veps, rstd, eps, half, n):
    k = mv.shape[1]
    pool.wait_ge(s[name + "_mv"], k * (n + 1))
    nc.gpsimd.tensor_tensor(veps[:, 0:k], mv[:, :, 1], eps[:, 0:k], ALU.add).then_inc(s[name + "_veps"], 1)
    pool.wait_ge(s[name + "_veps"], n + 1)
    nc.gpsimd.tensor_tensor(rstd[:, 0:k], veps[:, 0:k], half[:, 0:k], ALU.pow).then_inc(s[name + "_rstd"], 1)


def norm_vector_apply(nc, dve, s, name, x_tiles, mv, rstd, h0, n):
    dve.wait_ge(s[name + "_rstd"], n + 1)
    for t, x in enumerate(x_tiles):
        nc.vector.tensor_scalar(h0[:, t, :], x, mv[:, t, 0:1], rstd[:, t:t + 1],
                                ALU.subtract, ALU.mult).then_inc(s[name + "_h0"], 1)


NORM_SEMS = ["stats", "mv", "veps", "rstd", "h0"]


def network(nc, A, out, phases=4):
    with ExitStack() as ctx:
        def sb(name, shape, dt=F32):
            return ctx.enter_context(nc.sbuf_tensor(name, shape, dt))

        def sems(prefix, names, own=ctx):
            made = {n: nc.alloc_semaphore(f"{prefix}_{n}") for n in names}
            own.callback(nc.all_engine_barrier)
            own.callback(nc.clear_and_free_semaphores, list(made.values()))
            return made

        T = {}
        T["x"] = sb("x", [P, TILES, D])
        T["ident"] = sb("ident", [P, P])
        T["ones"] = sb("ones", [P, P])
        T["ones_r"] = sb("ones_r", [P, P], F32R)
        T["mod"] = sb("mod", [P, 4, 3, B])
        T["neg_half"] = sb("neg_half", [P, 8])
        T["half"] = sb("half", [P, 8])
        T["eps"] = sb("eps", [P, 8])
        T["rows"] = sb("rows", [P, 5])
        T["wq"] = sb("wq", [P, H, DK])
        T["wk"] = sb("wk", [P, H, DK])
        T["wv"] = sb("wv", [P, H, DK])
        T["wo"] = sb("wo", [P, D])
        T["wqs"] = sb("wqs", [P, HG, HB, 4, DK])
        T["wks"] = sb("wks", [P, HG, HB, 4, DK])
        T["wqk_hi"] = sb("wqk_hi", [P, 2, HG, P], F32R)
        T["wqk_lo"] = sb("wqk_lo", [P, 2, HG, P], F32R)
        T["gate_t"] = sb("gate_t", [P, E])
        T["gu_hi"] = sb("gu_hi", [P, 2, EP, P], F32R)
        T["gu_lo"] = sb("gu_lo", [P, 2, EP, P], F32R)
        T["down"] = sb("down", [P, EP, P])
        T["sh_hi"] = sb("sh_hi", [P, 2, I], F32R)
        T["sh_lo"] = sb("sh_lo", [P, 2, I], F32R)
        T["sh_down"] = sb("sh_down", [I, P])
        T["sel"] = sb("sel", [2 * E, EP, P], F32R)
        T["wqkv"] = sb("wqkv", [P, 3 * D])
        T["bqkv"] = sb("bqkv", [1, 3 * D])
        T["bv"] = sb("bv", [P, 1])
        T["wln"] = sb("wln", [P, D])
        T["bln"] = sb("bln", [P, 1])
        T["gx"] = sb("gx", [P, 1])
        T["gs"] = sb("gs", [P, 1])
        T["w1"] = sb("w1", [P, HID])
        T["w2"] = sb("w2", [P, HC, D])
        T["se_t"] = sb("se_t", [P, SLOTS])

        prepare(nc, ctx, T, A, sb, sems)
        if phases >= 1:
            attention(nc, T, sems)
        if phases >= 2:
            experts(nc, T, sems)
        if phases >= 3:
            linear_attention(nc, T, sems)
        if phases >= 4:
            slots(nc, T, sems)
        s = sems("end", ["stored"])
        with nc.Block() as block:
            @block.sync
            def _(sp):
                sp.dma_start(out.rearrange("b (t p) d -> p (b t) d", p=P), T["x"][:, :, :]).then_inc(s["stored"], 16)
                sp.wait_ge(s["stored"], 16)


def prepare(nc, ctx, T, A, sb, sems):
    with ExitStack() as own:
        def tmp(name, shape, dt=F32):
            return own.enter_context(nc.sbuf_tensor("p_" + name, shape, dt))

        eg = tmp("eg", [P, EP, D])
        eu = tmp("eu", [P, EP, D])
        ed = tmp("ed", [P, E, I])
        shg = tmp("shg", [I, D])
        shu = tmp("shu", [I, D])
        shd = tmp("shd", [D, I])
        gw = tmp("gw", [E, D])
        c = tmp("c", [B, 2, P])
        cs = tmp("cs", [B, 2, P])
        ct = tmp("ct", [P, 2, B])
        wmod = tmp("wmod", [P, 2, 6 * D])
        slot = tmp("slot", [P, SC, D])
        slot_sq = tmp("slot_sq", [P, SC, D])
        slot_n = tmp("slot_n", [P, SC, D])
        ss = tmp("ss", [P, SC])
        sn = tmp("sn", [P, SC])
        sr = tmp("sr", [P, SC])
        sgn = tmp("sgn", [P, 4, B])
        raw = tmp("raw", [P, 4, B])
        mag = tmp("mag", [P, 4, B])
        sel0 = tmp("sel0", [2 * E, EP, 2, I])
        ps = [own.enter_context(nc.psum_tensor(f"p_ps{i}", [P, 512], F32)) for i in range(8)]
        s = sems("p", ["x", "small", "wqkv", "gate", "up", "downw", "l1", "const", "id0", "cs", "ct_ps", "ct",
                       "mod_ps", "mod", "sgn", "raw", "gates", "stk0", "stk", "stkhi", "stklo", "tr", "hi", "lo", "fr",
                       "ssq", "ss", "sn", "snm", "sr", "slot_n", "sel0", "selm", "sel", "gt", "sh_hi", "sh_lo", "sh_ps"], own)
        x = T["x"]
        rounds = [(k, r) for k in range(3) for r in range(EP // 4)]

        with nc.Block() as block:
            @block.sync
            def _(sp):
                sp.dma_start(c[:, 0, :], A["L0_c"]).then_inc(s["small"], 16)
                sp.dma_start(c[:, 1, :], A["L1_c"]).then_inc(s["small"], 16)
                sp.dma_start(wmod[:, 0, :], A["L0_wmod"]).then_inc(s["small"], 16)
                sp.dma_start(wmod[:, 1, :], A["L1_wmod"]).then_inc(s["small"], 16)
                sp.dma_start(x[:, :, :], A["L0_attn_q"].rearrange("b (t p) d -> p (b t) d", p=P)).then_inc(s["x"], 16)
                sp.dma_start(eg[:, :, :], A["L0_ffn_expert_gate"].rearrange("(p e) i d -> (e i) p d", e=2)).then_inc(s["gate"], 16)
                sp.dma_start(eu[:, :, :], A["L0_ffn_expert_up"].rearrange("(p e) i d -> (e i) p d", e=2)).then_inc(s["up"], 16)
                sp.dma_start(ed[:, :, :], A["L0_ffn_expert_down"].rearrange("e d i -> d e i")).then_inc(s["downw"], 16)
                sp.wait_ge(s["x"], 16)

            @block.gpsimd
            def _(pool):
                nc.gpsimd.memset(T["ident"][:, :], 0.0).then_inc(s["id0"], 1)
                nc.gpsimd.memset(T["ones"][:, :], 1.0).then_inc(s["const"], 1)
                nc.gpsimd.memset(T["neg_half"][:, :], -0.5).then_inc(s["const"], 1)
                nc.gpsimd.memset(T["half"][:, :], 0.5).then_inc(s["const"], 1)
                nc.gpsimd.memset(T["eps"][:, :], LN_EPS).then_inc(s["const"], 1)
                pool.wait_ge(s["id0"], 1)
                nc.gpsimd.affine_select(out=T["ident"][:, :], in_=T["ident"][:, :], compare_op=ALU.not_equal, fill=1.0,
                                        base=0, pattern=[[-1, P]], channel_multiplier=1).then_inc(s["const"], 1)
                nc.gpsimd.memset(sel0[:, :, :, :], 0.0).then_inc(s["sel0"], 1)
                pool.wait_ge(s["sel0"], 1)
                nc.gpsimd.affine_select(out=sel0[:, :, :, :], in_=sel0[:, :, :, :], compare_op=ALU.not_equal, fill=1.0,
                                        base=0, pattern=[[-2, EP], [-1, 2], [0, I]], channel_multiplier=1).then_inc(s["sel0"], 1)
                pool.wait_ge(s["sel0"], 2)
                nc.gpsimd.affine_select(out=sel0[:, :, :, :], in_=sel0[:, :, :, :], compare_op=ALU.not_equal, fill=1.0,
                                        base=-E, pattern=[[-2, EP], [-1, 2], [0, I]], channel_multiplier=1).then_inc(s["selm"], 1)
                nc.gpsimd.memset(T["wqs"][:, :, :, :, :], 0.0).then_inc(s["stk0"], 1)
                nc.gpsimd.memset(T["wks"][:, :, :, :, :], 0.0).then_inc(s["stk0"], 1)
                pool.wait_ge(s["ss"], 1)
                nc.gpsimd.tensor_tensor(sn[:, :], ss[:, :], T["half"][:, 0:SC], ALU.pow).then_inc(s["sn"], 1)

            @block.scalar
            def _(act):
                act.dma_start(T["rows"][:, :], A["rows"]).then_inc(s["wqkv"], 16)
                act.dma_start(T["wq"][:, :, :], A["L0_attn_W_query"].rearrange("h d k -> d h k")).then_inc(s["wqkv"], 16)
                act.dma_start(T["wk"][:, :, :], A["L0_attn_W_key"].rearrange("h d k -> d h k")).then_inc(s["wqkv"], 16)
                act.dma_start(T["wv"][:, :, :], A["L0_attn_W_val"].rearrange("h d k -> d h k")).then_inc(s["wqkv"], 16)
                act.dma_start(T["wo"][:, :], A["L0_attn_W_out"].rearrange("h k e -> (h k) e")).then_inc(s["wqkv"], 16)
                for dst, src in [(gw, A["L0_ffn_gate_w"]), (shg, A["L0_ffn_shared_gate_w"]),
                                 (shu, A["L0_ffn_shared_up_w"]), (shd, A["L0_ffn_shared_down_w"]),
                                 (T["wqkv"], A["L1_attn_Wqkv"]), (T["wln"], A["L1_attn_Wln"]), (T["w1"], A["L1_ffn_w1"])]:
                    act.dma_start(dst[:, :], src).then_inc(s["l1"], 16)
                act.dma_start(T["bqkv"][:, :], A["L1_attn_bqkv"].rearrange("(a n) -> a n", a=1)).then_inc(s["l1"], 16)
                act.dma_start(T["bv"][:, :], A["L1_attn_bqkv"][2 * D:3 * D].rearrange("(n a) -> n a", a=1)).then_inc(s["l1"], 16)
                act.dma_start(T["bln"][:, :], A["L1_attn_bln"].rearrange("(n a) -> n a", a=1)).then_inc(s["l1"], 16)
                act.dma_start(T["gx"][:, :], A["L1_ffn_gamma_x"].rearrange("(n a) -> n a", a=1)).then_inc(s["l1"], 16)
                act.dma_start(T["gs"][:, :], A["L1_ffn_gamma_slot"].rearrange("(n a) -> n a", a=1)).then_inc(s["l1"], 16)
                act.dma_start(T["w2"][:, :, :], A["L1_ffn_w2"].rearrange("(j p) d -> p j d", p=P)).then_inc(s["l1"], 16)
                act.dma_start(slot[:, :, :], A["L1_ffn_slot_embeds"].rearrange("e t d -> (e t) d")
                              .rearrange("(c p) d -> p c d", p=P)).then_inc(s["l1"], 16)
                act.wait_ge(s["small"], 64)
                nc.scalar.activation(cs[:, :, :], c[:, :, :], ACT.Silu).then_inc(s["cs"], 1)
                for n, (k, r) in enumerate(rounds):
                    act.wait_ge(s["tr"], n + 1)
                    if k < 2:
                        nc.scalar.activation(T["gu_hi"][:, k, 4 * r:4 * r + 4, :], ps[n % 4][:, :], ACT.Copy).then_inc(s["hi"], 1)
                    else:
                        nc.scalar.activation(T["down"][:, 4 * r:4 * r + 4, :], ps[n % 4][:, :], ACT.Copy).then_inc(s["fr"], 1)
                act.wait_ge(s["sh_ps"], 1)
                nc.scalar.activation(T["sh_hi"][:, :, :], ps[6][:, 0:2 * I], ACT.Copy).then_inc(s["sh_hi"], 1)
                nc.scalar.activation(T["sh_down"][:, :], ps[6][0:I, 2 * I:2 * I + P], ACT.Copy).then_inc(s["gt"], 1)
                nc.scalar.activation(T["gate_t"][:, :], ps[6][:, 2 * I + P:2 * I + P + E], ACT.Copy).then_inc(s["gt"], 1)
                act.wait_ge(s["l1"], 14 * 16)

            @block.vector
            def _(dve):
                dve.wait_ge(s["wqkv"], 5 * 16)
                dve.wait_ge(s["stk0"], 2)
                for w, st in ((T["wq"], T["wqs"]), (T["wk"], T["wks"])):
                    for k in range(3):
                        nc.vector.tensor_copy(st[:, :, :, k, :], w[:, :, :].rearrange("p (g i) k -> p g i k", i=HB)).then_inc(s["stk"], 1)
                dve.wait_ge(s["stk"], 6)
                for j, st in enumerate((T["wqs"], T["wks"])):
                    nc.vector.tensor_copy(T["wqk_hi"][:, j, :, :], st.rearrange("p g i c k -> p g (i c k)")).then_inc(s["stkhi"], 1)
                dve.wait_ge(s["stkhi"], 2)
                for j, st in enumerate((T["wqs"], T["wks"])):
                    nc.vector.tensor_tensor(T["wqk_lo"][:, j, :, :], st.rearrange("p g i c k -> p g (i c k)"),
                                            T["wqk_hi"][:, j, :, :].bitcast(F32), ALU.subtract).then_inc(s["stklo"], 1)
                dve.wait_ge(s["ct_ps"], 1)
                nc.vector.tensor_copy(ct[:, :, :], ps[4][:, 0:2 * B]).then_inc(s["ct"], 1)
                dve.wait_ge(s["mod_ps"], 1)
                mod_ps = ps[5][:, 0:12 * B].rearrange("p (a k b) -> p a k b", a=4, k=3)
                nc.vector.tensor_copy(T["mod"][:, :, 0, :], mod_ps[:, :, 0, :]).then_inc(s["mod"], 1)
                nc.vector.tensor_scalar(T["mod"][:, :, 1, :], mod_ps[:, :, 1, :], 1.0, None, ALU.add).then_inc(s["mod"], 1)
                nc.vector.tensor_scalar(sgn[:, :, :], mod_ps[:, :, 2, :], 0.0, 2.0, ALU.is_ge, ALU.mult).then_inc(s["sgn"], 1)
                nc.vector.tensor_copy(raw[:, :, :], mod_ps[:, :, 2, :]).then_inc(s["raw"], 1)
                dve.wait_ge(s["raw"], 1)
                nc.vector.scalar_tensor_tensor(mag[:, :, :], raw[:, :, :], -1.0, raw[:, :, :], ALU.mult, ALU.max).then_inc(s["raw"], 1)
                dve.wait_ge(s["raw"], 2)
                nc.vector.tensor_scalar(mag[:, :, :], mag[:, :, :], 0.25, None, ALU.max).then_inc(s["sgn"], 1)
                dve.wait_ge(s["sgn"], 2)
                nc.vector.scalar_tensor_tensor(T["mod"][:, :, 2, :], sgn[:, :, :], -1.0, mag[:, :, :], ALU.add, ALU.mult).then_inc(s["mod"], 1)
                dve.wait_ge(s["const"], 5)
                nc.vector.tensor_copy(T["ones_r"][:, :], T["ones"][:, :]).then_inc(s["const"], 1)
                dve.wait_ge(s["selm"], 1)
                nc.vector.tensor_copy(T["sel"][:, :, :], sel0[:, :, :, :].rearrange("p a j i -> p a (j i)")).then_inc(s["sel"], 1)
                for n, (k, r) in enumerate(rounds):
                    if k < 2:
                        dve.wait_ge(s["hi"], n + 1)
                        nc.vector.tensor_tensor(T["gu_lo"][:, k, 4 * r:4 * r + 4, :].rearrange("p a b -> p (a b)"), ps[n % 4][:, :],
                                                T["gu_hi"][:, k, 4 * r:4 * r + 4, :].bitcast(F32).rearrange("p a b -> p (a b)"),
                                                ALU.subtract).then_inc(s["lo"], 1)
                dve.wait_ge(s["sh_hi"], 1)
                dve.wait_ge(s["gt"], 2)
                nc.vector.tensor_tensor(T["sh_lo"][:, :, :].rearrange("p a b -> p (a b)"), ps[6][:, 0:2 * I],
                                        T["sh_hi"][:, :, :].bitcast(F32).rearrange("p a b -> p (a b)"), ALU.subtract).then_inc(s["sh_lo"], 1)
                dve.wait_ge(s["l1"], 14 * 16)
                nc.vector.tensor_tensor(slot_sq[:, :, :], slot[:, :, :], slot[:, :, :], ALU.mult).then_inc(s["ssq"], 1)
                dve.wait_ge(s["ssq"], 1)
                nc.vector.tensor_reduce(ss[:, :], slot_sq[:, :, :], AX.X, ALU.add).then_inc(s["ss"], 1)
                dve.wait_ge(s["sn"], 1)
                nc.vector.tensor_scalar(sn[:, :], sn[:, :], 1e-12, float(D) ** -0.5, ALU.max, ALU.mult).then_inc(s["snm"], 1)
                dve.wait_ge(s["snm"], 1)
                nc.vector.reciprocal(sr[:, :], sn[:, :]).then_inc(s["sr"], 1)
                dve.wait_ge(s["sr"], 1)
                nc.vector.tensor_tensor(slot_n[:, :, :], slot[:, :, :], sr[:, :].unsqueeze(2).to_broadcast([P, SC, D]),
                                        ALU.mult).then_inc(s["slot_n"], 1)
                dve.wait_ge(s["sh_ps"], 2)
                nc.vector.tensor_scalar(T["se_t"][:, :], ps[7][:, :], T["gs"][:, 0:1], None, ALU.mult).then_inc(s["slot_n"], 1)

            @block.tensor
            def _(pe):
                pe.wait_ge(s["const"], 5)
                pe.wait_ge(s["cs"], 1)
                for l in range(2):
                    last = nc.tensor.transpose(ps[4][:, l * B:(l + 1) * B], cs[:, l, :], T["ident"][0:B, 0:B])
                last.then_inc(s["ct_ps"], 1)
                pe.wait_ge(s["ct"], 1)
                for l in range(2):
                    for k in range(6):
                        last = nc.tensor.matmul(ps[5][:, (l * 6 + k) * B:(l * 6 + k + 1) * B], wmod[:, l, k * D:(k + 1) * D],
                                                ct[:, l, :], start=True, stop=True)
                last.then_inc(s["mod_ps"], 1)
                for n, (k, r) in enumerate(rounds):
                    if r == 0:
                        pe.wait_ge(s[("gate", "up", "downw")[k]], 16)
                    if n >= 4:
                        if n - 4 < 8:
                            pe.wait_ge(s["lo"], n - 3)
                        else:
                            pe.wait_ge(s["fr"], n - 11)
                    for q in range(4):
                        p = 4 * r + q
                        src = (eg[:, p, :], eu[:, p, :], ed[:, 2 * p:2 * p + 2, :].rearrange("d e i -> d (e i)"))[k]
                        last = nc.tensor.transpose(ps[n % 4][:, q * P:(q + 1) * P], src, T["ident"][:, :])
                    last.then_inc(s["tr"], 1)
                pe.wait_ge(s["l1"], 14 * 16)
                nc.tensor.transpose(ps[6][:, 0:I], shg[:, :], T["ident"][0:I, 0:I])
                nc.tensor.transpose(ps[6][:, I:2 * I], shu[:, :], T["ident"][0:I, 0:I])
                nc.tensor.transpose(ps[6][0:I, 2 * I:2 * I + P], shd[:, :], T["ident"][:, :])
                nc.tensor.transpose(ps[6][:, 2 * I + P:2 * I + P + E], gw[:, :], T["ident"][0:E, 0:E]).then_inc(s["sh_ps"], 1)
                pe.wait_ge(s["slot_n"], 1)
                for k in range(SC):
                    last = nc.tensor.transpose(ps[7][:, k * P:(k + 1) * P], slot_n[:, k, :], T["ident"][:, :])
                last.then_inc(s["sh_ps"], 1)


def attention(nc, T, sems):
    with ExitStack() as own:
        def tmp(name, shape, dt=F32):
            return own.enter_context(nc.sbuf_tensor("a_" + name, shape, dt))

        stats = tmp("stats", [P, TB, 6])
        mv = tmp("mv", [P, TB, 2])
        veps = tmp("veps", [P, 8])
        rstd = tmp("rstd", [P, 8])
        h0 = tmp("h0", [P, TB, D])
        ht = tmp("ht", [P, S])
        ht_hi = tmp("ht_hi", [P, S], F32R)
        ht_lo = tmp("ht_lo", [P, S], F32R)
        hs = tmp("hs", [P, 2, 2, S])
        qs = tmp("qs", [P, HG, S], F32R)
        ks = tmp("ks", [P, HG, S], F32R)
        qblk = tmp("qblk", [P, HG, HB, S], F32R)
        vaug = tmp("vaug", [P, TB, H, STACK])
        mx = tmp("mx", [P, TB, HB, HG])
        nm = tmp("nm", [P, TB, HB, HG, 2])
        mt = tmp("mt", [2 * H, S], F32R)
        pt = tmp("pt", [P, 2, TB, HB, S])
        us = tmp("us", [P, HG, S])
        rec = tmp("rec", [P, TB, H])
        o = tmp("o", [P, TB, H, DK])
        ots = tmp("ots", [P, S])
        yts = tmp("yts", [P, S])
        diag = tmp("diag", [P, P])
        ring = [own.enter_context(nc.psum_tensor(f"a_ring{i}", [P, 2, S], F32)) for i in range(2)]
        st = [own.enter_context(nc.psum_tensor(f"a_st{i}", [P, 2, S], F32)) for i in range(2)]
        u = own.enter_context(nc.psum_tensor("a_u", [P, HG, S], F32))
        ma = own.enter_context(nc.psum_tensor("a_ma", [P, 512], F32))
        mb = own.enter_context(nc.psum_tensor("a_mb", [P, 512], F32))
        s = sems("a", ["n_" + n for n in NORM_SEMS] +
                 ["ht_ps", "ht", "ht_hi", "ht_lo", "v_ps", "v", "qk_ps", "qk_hs", "qs", "ks", "ring_free", "qblk",
                  "s_ps", "mx", "nm_hi", "nm", "mt_ps", "mt", "mblk", "st_ps", "pt", "pv", "us", "ut_ps", "rec", "o",
                  "ot_ps", "ots", "yt_ps", "yts", "diag", "xo", "x1", "zero", "vinit"], own)
        FILLS = 4 + 16
        STEPS = [(g, qt, ip) for g in range(HG) for qt in range(TB) for ip in range(2)]

        with nc.Block() as block:
            @block.gpsimd
            def _(pool):
                nc.gpsimd.memset(qblk[:, :, :, :].bitcast(F32), 0.0).then_inc(s["zero"], 1)
                nc.gpsimd.memset(vaug[:, :, :, :], 0.0).then_inc(s["vinit"], 1)
                pool.wait_ge(s["vinit"], 1)
                nc.gpsimd.memset(vaug[:, :, :, DK:DK + 1], 1.0).then_inc(s["zero"], 1)
                with pool.Fori(0, B) as b:
                    norm_pool_rstd(nc, pool, s, "n", mv, veps, rstd, T["eps"], T["neg_half"], b)

            @block.sync
            def _(sp):
                sp.wait_ge(s["zero"], 2)
                with sp.Fori(0, B) as b:
                    sp.wait_ge(s["qs"], 2 * b + 2)
                    for i in range(HB):
                        r = slice(i * STACK, (i + 1) * STACK)
                        sp.dma_start(qblk[r, :, i, :].bitcast(F32), qs[r, :, :].bitcast(F32)).then_inc(s["qblk"], 16)
                sp.wait_ge(s["mblk"], 16 * HG * HB * B)

            @block.vector
            def _(dve):
                dve.sem_inc(s["ring_free"], 1)
                with dve.Fori(0, B) as b:
                    xt = [T["x"][:, bass.ds(TB * b + t, 1), :].rearrange("p a d -> p (a d)") for t in range(TB)]
                    norm_vector_stats(nc, dve, s, "n", xt, stats, mv, b)
                    norm_vector_apply(nc, dve, s, "n", xt, mv, rstd, h0, b)
                    nc.vector.tensor_scalar(diag[:, :], T["ident"][:, :], T["mod"][:, L0A, 2, bass.ds(b, 1)], None,
                                            ALU.mult).then_inc(s["diag"], 1)
                    dve.wait_ge(s["ht_hi"], b + 1)
                    nc.vector.tensor_tensor(ht_lo[:, :], ht[:, :], ht_hi[:, :].bitcast(F32), ALU.subtract).then_inc(s["ht_lo"], 1)
                    dve.wait_ge(s["v_ps"], b + 1)
                    for t in range(TB):
                        nc.vector.tensor_copy(vaug[:, t, :, 0:DK], ma[:, S + t * P:S + (t + 1) * P].rearrange("p (h k) -> p h k", k=DK)).then_inc(s["v"], 1)
                    for k in range(4):
                        dve.wait_ge(s["qk_hs"], 4 * b + k + 1)
                        j, dst, name = (0, qs, "qs") if k < 2 else (1, ks, "ks")
                        g = 2 * (k % 2)
                        nc.vector.scalar_tensor_tensor(dst[:, g:g + 2, :].rearrange("p a n -> p (a n)"),
                                                       ring[k % 2][:, :, :].rearrange("p a n -> p (a n)"), T["rows"][:, 2 * j:2 * j + 1],
                                                       hs[:, k % 2, :, :].rearrange("p a n -> p (a n)"), ALU.mult, ALU.add).then_inc(s[name], 1)
                        dve.wait_ge(s[name], 2 * b + k % 2 + 1)
                        dve.sem_inc(s["ring_free"], 1)
                    for k, (g, qt, ip) in enumerate(STEPS):
                        dve.wait_ge(s["s_ps"], 16 * b + k + 1)
                        nc.vector.tensor_reduce(mx[:, qt, 2 * ip:2 * ip + 2, g], ring[k % 2][:, :, :], AX.X, ALU.max).then_inc(s["ring_free"], 1)
                    dve.wait_ge(s["ring_free"], FILLS * (b + 1) + 1)
                    nc.vector.tensor_scalar(nm[:, :, :, :, 0].bitcast(F32R).rearrange("p t i g -> p t (i g)"),
                                            mx[:, :, :, :].rearrange("p t i g -> p t (i g)"), -1.0, None, ALU.mult).then_inc(s["nm_hi"], 1)
                    dve.wait_ge(s["nm_hi"], b + 1)
                    nc.vector.scalar_tensor_tensor(nm[:, :, :, :, 1].bitcast(F32R).rearrange("p t i g -> p t (i g)"),
                                                   mx[:, :, :, :].rearrange("p t i g -> p t (i g)"), -1.0,
                                                   nm[:, :, :, :, 0].rearrange("p t i g -> p t (i g)"),
                                                   ALU.mult, ALU.subtract).then_inc(s["nm"], 1)
                    for t in range(TB):
                        dve.wait_ge(s["ut_ps"], TB * b + t + 1)
                        ut = (ma, mb)[t][:, :].rearrange("p (h k) -> p h k", k=STACK)
                        nc.vector.reciprocal(rec[:, t, :], ut[:, :, DK]).then_inc(s["rec"], 1)
                        dve.wait_ge(s["rec"], TB * b + t + 1)
                        nc.vector.tensor_tensor(o[:, t, :, :], ut[:, :, 0:DK], rec[:, t, :].unsqueeze(2).to_broadcast([P, H, DK]),
                                                ALU.mult).then_inc(s["o"], 1)
                    dve.wait_ge(s["xo"], b + 1)
                    x2 = T["x"][:, bass.ds(TB * b, TB), :].rearrange("p a d -> p (a d)")
                    nc.vector.tensor_tensor(x2, x2, mb[:, S:2 * S], ALU.add).then_inc(s["x1"], 1)

            @block.scalar
            def _(act):
                with act.Fori(0, B) as b:
                    act.wait_ge(s["ht_ps"], b + 1)
                    nc.scalar.activation(ht[:, :], ma[:, 0:S], ACT.Identity, scale=T["mod"][:, L0A, 1, bass.ds(b, 1)],
                                         bias=T["mod"][:, L0A, 0, bass.ds(b, 1)]).then_inc(s["ht"], 1)
                    act.wait_ge(s["ht"], b + 1)
                    nc.scalar.activation(ht_hi[:, :], ht[:, :], ACT.Copy).then_inc(s["ht_hi"], 1)
                    for k in range(4):
                        act.wait_ge(s["qk_ps"], 4 * b + k + 1)
                        j = k // 2
                        bias = T["rows"][:, 4:5] if j else 0.0
                        nc.scalar.activation(hs[:, k % 2, :, :].bitcast(F32R), ring[k % 2][:, :, :], ACT.Identity, bias=bias,
                                             scale=T["rows"][:, 2 * j + 1:2 * j + 2]).then_inc(s["qk_hs"], 1)
                    act.wait_ge(s["mt_ps"], b + 1)
                    nc.scalar.activation(mt[:, :], mb[0:2 * H, 0:S], ACT.Copy).then_inc(s["mt"], 1)
                    act.wait_ge(s["mt"], b + 1)
                    for i in range(HB):
                        r = i * STACK + M_ROW
                        for g in range(HG):
                            act.dma_start(qblk[r:r + 2, g, i, :].bitcast(F32),
                                          mt[i * 2 * HG + 2 * g:i * 2 * HG + 2 * g + 2, :].bitcast(F32)).then_inc(s["mblk"], 16)
                    for k, (g, nt, ip) in enumerate(STEPS):
                        act.wait_ge(s["st_ps"], 16 * b + k + 1)
                        if nt == 0 and ip == 0:
                            if g >= 2:
                                act.wait_ge(s["pv"], HG * b + g - 1)
                            else:
                                act.wait_ge(s["pv"], HG * b)
                        nc.scalar.activation(pt[:, g % 2, nt, 2 * ip:2 * ip + 2, :], st[k % 2][:, :, :], ACT.Exp,
                                             scale=ATTN_SCALE).then_inc(s["pt"], 1)
                    act.wait_ge(s["pv"], HG * (b + 1))
                    for g in (0, 2):
                        nc.scalar.activation(us[:, g:g + 2, :], u[:, g:g + 2, :], ACT.Copy).then_inc(s["us"], 1)
                    act.wait_ge(s["ot_ps"], b + 1)
                    nc.scalar.activation(ots[:, :], ma[:, 0:S], ACT.Copy).then_inc(s["ots"], 1)
                    act.wait_ge(s["yt_ps"], b + 1)
                    nc.scalar.activation(yts[:, :], mb[:, 0:S], ACT.Copy).then_inc(s["yts"], 1)

            @block.tensor
            def _(pe):
                pe.wait_ge(s["zero"], 2)
                with pe.Fori(0, B) as b:
                    pe.wait_ge(s["n_h0"], TB * (b + 1))
                    pe.wait_ge(s["x1"], b)
                    for t in range(TB):
                        last = nc.tensor.transpose(ma[:, t * P:(t + 1) * P], h0[:, t, :], T["ident"][:, :])
                    last.then_inc(s["ht_ps"], 1)
                    pe.wait_ge(s["ht"], b + 1)
                    for t in range(TB):
                        last = nc.tensor.matmul(ma[:, S + t * P:S + (t + 1) * P], ht[:, t * P:(t + 1) * P],
                                                T["wv"][:, :, :].rearrange("p h k -> p (h k)"), start=True, stop=True)
                    last.then_inc(s["v_ps"], 1)
                    pe.wait_ge(s["ht_lo"], b + 1)
                    for k in range(4):
                        pe.wait_ge(s["ring_free"], FILLS * b + k)
                        j = k // 2
                        for a in range(2):
                            g = 2 * (k % 2) + a
                            dst = ring[k % 2][:, a, :]
                            nc.tensor.matmul(dst, T["wqk_hi"][:, j, g, :], ht_hi[:, :], start=True, stop=False)
                            nc.tensor.matmul(dst, T["wqk_hi"][:, j, g, :], ht_lo[:, :], start=False, stop=False)
                            last = nc.tensor.matmul(dst, T["wqk_lo"][:, j, g, :], ht_hi[:, :], start=False, stop=True)
                        last.then_inc(s["qk_ps"], 1)
                    pe.wait_ge(s["ks"], 2 * b + 2)
                    pe.wait_ge(s["qblk"], 16 * HB * (b + 1))
                    for k, (g, qt, ip) in enumerate(STEPS):
                        pe.wait_ge(s["ring_free"], FILLS * b + 4 + k)
                        for a in range(2):
                            last = nc.tensor.matmul(ring[k % 2][:, a, :], qblk[:, g, 2 * ip + a, qt * P:(qt + 1) * P],
                                                    ks[:, g, :], start=True, stop=True)
                        last.then_inc(s["s_ps"], 1)
                    pe.wait_ge(s["nm"], b + 1)
                    for t in range(TB):
                        last = nc.tensor.transpose(mb[0:2 * H, t * P:(t + 1) * P],
                                                   nm[:, t, :, :, :].rearrange("p i g l -> p (i g l)"), T["ident"][:, :])
                    last.then_inc(s["mt_ps"], 1)
                    pe.wait_ge(s["mblk"], 16 * HB * HG * (b + 1))
                    pe.wait_ge(s["v"], TB * (b + 1))
                    pe.wait_ge(s["us"], 2 * b)

                    def values(g):
                        pe.wait_ge(s["pt"], 16 * b + 4 * (g + 1))
                        for nt in range(TB):
                            for i in range(HB):
                                last = nc.tensor.matmul(u[i * STACK:(i + 1) * STACK, g, :], vaug[:, nt, HB * g + i, :],
                                                        pt[:, g % 2, nt, i, :], start=(nt == 0), stop=(nt == TB - 1),
                                                        skip_group_check=True)
                        last.then_inc(s["pv"], 1)

                    for k, (g, nt, ip) in enumerate(STEPS):
                        if k >= 2:
                            pe.wait_ge(s["pt"], 16 * b + k - 1)
                        else:
                            pe.wait_ge(s["pt"], 16 * b)
                        nc.tensor.matmul(st[k % 2][:, :, :].rearrange("p a n -> p (a n)"), ks[:, g, nt * P:(nt + 1) * P],
                                         qblk[:, g, 2 * ip:2 * ip + 2, :].rearrange("p a n -> p (a n)"),
                                         start=True, stop=True).then_inc(s["st_ps"], 1)
                        if nt == 0 and ip == 1 and g >= 1:
                            values(g - 1)
                    values(HG - 1)
                    for t in range(TB):
                        pe.wait_ge(s["us"], 2 * (b + 1))
                        for g in range(HG):
                            last = nc.tensor.transpose((ma, mb)[t][:, g * P:(g + 1) * P], us[:, g, t * P:(t + 1) * P], T["ident"][:, :])
                        last.then_inc(s["ut_ps"], 1)
                    pe.wait_ge(s["o"], TB * (b + 1))
                    for t in range(TB):
                        last = nc.tensor.transpose(ma[:, t * P:(t + 1) * P], o[:, t, :, :].rearrange("p h k -> p (h k)"), T["ident"][:, :])
                    last.then_inc(s["ot_ps"], 1)
                    pe.wait_ge(s["ots"], b + 1)
                    nc.tensor.matmul(mb[:, 0:S], T["wo"][:, :], ots[:, :], start=True, stop=True).then_inc(s["yt_ps"], 1)
                    pe.wait_ge(s["yts"], b + 1)
                    pe.wait_ge(s["diag"], b + 1)
                    for t in range(TB):
                        last = nc.tensor.matmul(mb[:, S + t * P:S + (t + 1) * P], yts[:, t * P:(t + 1) * P], diag[:, :],
                                                start=True, stop=True)
                    last.then_inc(s["xo"], 1)


def experts(nc, T, sems):
    with ExitStack() as own:
        def tmp(name, shape, dt=F32):
            return own.enter_context(nc.sbuf_tensor("e_" + name, shape, dt))

        h2_hi = tmp("h2_hi", [P, B * S], F32R)
        h2_lo = tmp("h2_lo", [P, B * S], F32R)
        ct_r = tmp("ct_r", [2 * E, B * S], F32R)
        score = tmp("score", [P, TILES, E])
        expert_inputs(nc, T, sems, h2_hi, h2_lo, score)
        routing(nc, T, sems, score, ct_r)
        expert_products(nc, T, sems, h2_hi, h2_lo, ct_r)


def expert_inputs(nc, T, sems, h2_hi, h2_lo, score):
    with ExitStack() as own:
        def tmp(name, shape, dt=F32):
            return own.enter_context(nc.sbuf_tensor("i_" + name, shape, dt))

        stats = tmp("stats", [P, TB, 6])
        mv = tmp("mv", [P, TB, 2])
        veps = tmp("veps", [P, 8])
        rstd = tmp("rstd", [P, 8])
        h0 = tmp("h0", [P, TB, D])
        ht = tmp("ht", [P, S])
        hp = own.enter_context(nc.psum_tensor("i_hp", [P, 512], F32))
        lg = own.enter_context(nc.psum_tensor("i_lg", [P, 512], F32))
        s = sems("i", ["n_" + n for n in NORM_SEMS] + ["ht_ps", "ht", "hi", "lo", "lg", "score"], own)
        with nc.Block() as block:
            @block.gpsimd
            def _(pool):
                with pool.Fori(0, B) as b:
                    norm_pool_rstd(nc, pool, s, "n", mv, veps, rstd, T["eps"], T["neg_half"], b)

            @block.vector
            def _(dve):
                with dve.Fori(0, B) as b:
                    xt = [T["x"][:, bass.ds(TB * b + t, 1), :].rearrange("p a d -> p (a d)") for t in range(TB)]
                    norm_vector_stats(nc, dve, s, "n", xt, stats, mv, b)
                    dve.wait_ge(s["ht_ps"], b)
                    norm_vector_apply(nc, dve, s, "n", xt, mv, rstd, h0, b)
                    dve.wait_ge(s["hi"], b + 1)
                    nc.vector.tensor_tensor(h2_lo[:, bass.ds(S * b, S)], ht[:, :], h2_hi[:, bass.ds(S * b, S)].bitcast(F32),
                                            ALU.subtract).then_inc(s["lo"], 1)

            @block.scalar
            def _(act):
                with act.Fori(0, B) as b:
                    act.wait_ge(s["ht_ps"], b + 1)
                    act.wait_ge(s["lo"], b)
                    nc.scalar.activation(ht[:, :], hp[:, 0:S], ACT.Identity, scale=T["mod"][:, L0F, 1, bass.ds(b, 1)],
                                         bias=T["mod"][:, L0F, 0, bass.ds(b, 1)]).then_inc(s["ht"], 1)
                    act.wait_ge(s["ht"], b + 1)
                    nc.scalar.activation(h2_hi[:, bass.ds(S * b, S)], ht[:, :], ACT.Copy).then_inc(s["hi"], 1)
                    act.wait_ge(s["lg"], b + 1)
                    nc.scalar.activation(score[:, bass.ds(TB * b, TB), :].rearrange("p a e -> p (a e)"), lg[:, 0:TB * E],
                                         ACT.Sigmoid).then_inc(s["score"], 1)

            @block.tensor
            def _(pe):
                with pe.Fori(0, B) as b:
                    pe.wait_ge(s["n_h0"], TB * (b + 1))
                    pe.wait_ge(s["ht"], b)
                    for t in range(TB):
                        last = nc.tensor.transpose(hp[:, t * P:(t + 1) * P], h0[:, t, :], T["ident"][:, :])
                    last.then_inc(s["ht_ps"], 1)
                    pe.wait_ge(s["ht"], b + 1)
                    pe.wait_ge(s["score"], b)
                    for t in range(TB):
                        last = nc.tensor.matmul(lg[:, t * E:(t + 1) * E], ht[:, t * P:(t + 1) * P], T["gate_t"][:, :],
                                                start=True, stop=True)
                    last.then_inc(s["lg"], 1)


def routing(nc, T, sems, score, ct_r):
    with ExitStack() as own:
        def tmp(name, shape, dt=F32):
            return own.enter_context(nc.sbuf_tensor("r_" + name, shape, dt))

        gsum = tmp("gsum", [P, TILES, GROUPS + TOPG])
        best = tmp("best", [P, TILES, GROUPS])
        seek = tmp("seek", [P, TILES, GROUPS])
        left = tmp("left", [P, TILES, GROUPS + TOPG])
        gmask = tmp("gmask", [P, TILES, GROUPS])
        masked = tmp("masked", [P, TILES, E])
        top = tmp("top", [P, TILES, TOPK])
        rest = tmp("rest", [P, TILES, E])
        w = tmp("w", [P, TILES, E])
        total = tmp("total", [P, TILES])
        inv = tmp("inv", [P, TILES])
        cw = tmp("cw", [P, TILES, E])
        c2 = tmp("c2", [P, TILES, 2, E])
        ps = [own.enter_context(nc.psum_tensor(f"r_ps{i}", [P, 512], F32)) for i in range(4)]
        s = sems("r", ["fill", "gsum", "best", "seek", "left", "gmask", "masked", "top", "rest", "w", "total", "tmax", "inv",
                       "cw", "c_hi", "c_lo", "ps", "ct"], own)
        with nc.Block() as block:
            @block.vector
            def _(dve):
                nc.vector.memset(gsum[:, :, GROUPS:], -5.0).then_inc(s["fill"], 1)
                nc.vector.memset(seek[:, :, TOPG:], -5.0).then_inc(s["fill"], 1)
                nc.vector.tensor_reduce(gsum[:, :, 0:GROUPS], score[:, :, :].rearrange("p t (g k) -> p t g k", k=EPG),
                                        AX.X, ALU.add).then_inc(s["gsum"], 1)
                dve.wait_ge(s["gsum"], 1)
                for t in range(TILES):
                    nc.vector.max(best[:, t, :], gsum[:, t, 0:GROUPS]).then_inc(s["best"], 1)
                dve.wait_ge(s["best"], TILES)
                nc.vector.tensor_copy(seek[:, :, 0:TOPG], best[:, :, 0:TOPG]).then_inc(s["seek"], 1)
                dve.wait_ge(s["seek"], 1)
                dve.wait_ge(s["fill"], 2)
                for t in range(TILES):
                    nc.vector.match_replace(left[:, t, :], seek[:, t, :], gsum[:, t, :], -1.0).then_inc(s["left"], 1)
                dve.wait_ge(s["left"], TILES)
                nc.vector.tensor_scalar(gmask[:, :, :], left[:, :, 0:GROUPS], 0.0, None, ALU.is_lt).then_inc(s["gmask"], 1)
                dve.wait_ge(s["gmask"], 1)
                nc.vector.tensor_tensor(masked[:, :, :].rearrange("p t (g k) -> p (t g) k", k=EPG),
                                        score[:, :, :].rearrange("p t (g k) -> p (t g) k", k=EPG),
                                        gmask[:, :, :].rearrange("p t g -> p (t g)").unsqueeze(2).to_broadcast([P, TILES * GROUPS, EPG]),
                                        ALU.mult).then_inc(s["masked"], 1)
                dve.wait_ge(s["masked"], 1)
                for t in range(TILES):
                    nc.vector.max(top[:, t, :], masked[:, t, :]).then_inc(s["top"], 1)
                dve.wait_ge(s["top"], TILES)
                for t in range(TILES):
                    nc.vector.match_replace(rest[:, t, :], top[:, t, :], masked[:, t, :], -1.0).then_inc(s["rest"], 1)
                dve.wait_ge(s["rest"], TILES)
                nc.vector.scalar_tensor_tensor(w[:, :, :].rearrange("p t e -> p (t e)"), rest[:, :, :].rearrange("p t e -> p (t e)"), 0.0,
                                               masked[:, :, :].rearrange("p t e -> p (t e)"), ALU.is_lt, ALU.mult).then_inc(s["w"], 1)
                dve.wait_ge(s["w"], 1)
                nc.vector.tensor_reduce(total[:, :], w[:, :, :], AX.X, ALU.add).then_inc(s["total"], 1)
                dve.wait_ge(s["total"], 1)
                nc.vector.tensor_scalar(total[:, :], total[:, :], 1e-12, None, ALU.max).then_inc(s["tmax"], 1)
                dve.wait_ge(s["tmax"], 1)
                nc.vector.reciprocal(inv[:, :], total[:, :]).then_inc(s["inv"], 1)
                dve.wait_ge(s["inv"], 1)
                nc.vector.tensor_tensor(cw[:, :, :], w[:, :, :], inv[:, :].unsqueeze(2).to_broadcast([P, TILES, E]),
                                        ALU.mult).then_inc(s["cw"], 1)
                dve.wait_ge(s["cw"], 1)
                nc.vector.tensor_copy(c2[:, :, 0, :].bitcast(F32R), cw[:, :, :]).then_inc(s["c_hi"], 1)
                dve.wait_ge(s["c_hi"], 1)
                nc.vector.tensor_tensor(c2[:, :, 1, :].bitcast(F32R), cw[:, :, :], c2[:, :, 0, :], ALU.subtract).then_inc(s["c_lo"], 1)

            @block.tensor
            def _(pe):
                pe.wait_ge(s["c_lo"], 1)
                for t in range(TILES):
                    last = nc.tensor.transpose(ps[t // 4][0:2 * E, t % 4 * P:(t % 4 + 1) * P],
                                               c2[:, t, :, :].rearrange("p l e -> p (l e)"), T["ident"][:, :])
                    if t % 4 == 3:
                        last.then_inc(s["ps"], 1)

            @block.scalar
            def _(act):
                for r in range(4):
                    act.wait_ge(s["ps"], r + 1)
                    nc.scalar.activation(ct_r[:, r * 512:(r + 1) * 512], ps[r][0:2 * E, :], ACT.Copy).then_inc(s["ct"], 1)


def expert_products(nc, T, sems, h2_hi, h2_lo, ct_r):
    with ExitStack() as own:
        def tmp(name, shape, dt=F32):
            return own.enter_context(nc.sbuf_tensor("x_" + name, shape, dt))

        NP = EP + 1
        sg = tmp("sg", [P, 2, N2])
        su = tmp("su", [P, 2, N2])
        act_w = tmp("act_w", [P, 2, N2])
        yts = tmp("yts", [P, N2])
        diag = tmp("diag", [P, SB, P])
        g_ps = [own.enter_context(nc.psum_tensor(f"x_g{i}", [P, N2], F32)) for i in range(2)]
        u_ps = [own.enter_context(nc.psum_tensor(f"x_u{i}", [P, N2], F32)) for i in range(2)]
        w_ps = [own.enter_context(nc.psum_tensor(f"x_w{i}", [P, N2], F32)) for i in range(2)]
        y_ps = own.enter_context(nc.psum_tensor("x_y", [P, N2], F32))
        o_ps = own.enter_context(nc.psum_tensor("x_o", [P, N2], F32))
        s = sems("x", ["g", "u", "silu", "su", "act", "down", "y", "yts", "diag", "o", "res"], own)
        last_of_slot = lambda p: 1 if p == 0 else 2

        with nc.Block() as block:
            @block.tensor
            def _(pe):
                with pe.Fori(0, B // SB) as q:
                    f0 = NP * q
                    cols = bass.ds(N2 * q, N2)

                    def project(p):
                        m = P if p < EP else I
                        w_hi = [T["gu_hi"][:, j, p, :] if p < EP else T["sh_hi"][:, j, :] for j in range(2)]
                        w_lo = [T["gu_lo"][:, j, p, :] if p < EP else T["sh_lo"][:, j, :] for j in range(2)]
                        if p < 2:
                            pe.wait_ge(s["act"], f0)
                        for j, dst in enumerate((g_ps[p % 2], u_ps[p % 2])):
                            nc.tensor.matmul(dst[0:m, :], w_hi[j], h2_hi[:, cols], start=True, stop=False)
                            nc.tensor.matmul(dst[0:m, :], w_hi[j], h2_lo[:, cols], start=False, stop=False)
                            nc.tensor.matmul(dst[0:m, :], w_lo[j], h2_hi[:, cols], start=False, stop=True).then_inc(s[("g", "u")[j]], 1)
                        if p < EP:
                            nc.tensor.matmul(w_ps[p % 2][:, :], T["sel"][:, p, :], ct_r[:, cols], start=True, stop=True).then_inc(s["u"], 1)

                    project(0)
                    for p in range(NP):
                        if p + 1 < NP:
                            project(p + 1)
                        pe.wait_ge(s["act"], f0 + p + 1)
                        if p == 0:
                            pe.wait_ge(s["yts"], q)
                        if p < EP:
                            nc.tensor.matmul(y_ps[:, :], T["down"][:, p, :], act_w[:, p % 2, :], start=(p == 0),
                                             stop=False).then_inc(s["down"], 1)
                        else:
                            nc.tensor.matmul(y_ps[:, :], T["sh_down"][:, :], act_w[0:I, p % 2, :], start=False,
                                             stop=True).then_inc(s["down"], 1)
                    pe.wait_ge(s["yts"], q + 1)
                    pe.wait_ge(s["diag"], SB * (q + 1))
                    pe.wait_ge(s["res"], q)
                    for t in range(TB * SB):
                        last = nc.tensor.matmul(o_ps[:, t * P:(t + 1) * P], yts[:, t * P:(t + 1) * P], diag[:, t // TB, :],
                                                start=True, stop=True)
                    last.then_inc(s["o"], 1)

            @block.scalar
            def _(act):
                with act.Fori(0, B // SB) as q:
                    f0 = NP * q
                    for p in range(NP):
                        m = P if p < EP else I
                        act.wait_ge(s["g"], f0 + p + 1)
                        if p >= 2:
                            act.wait_ge(s["su"], f0 + p - 1)
                        else:
                            act.wait_ge(s["su"], f0)
                        nc.scalar.activation(sg[0:m, p % 2, :], g_ps[p % 2][0:m, :], ACT.Silu).then_inc(s["silu"], 1)
                    act.wait_ge(s["down"], NP * (q + 1))
                    act.wait_ge(s["o"], q)
                    nc.scalar.activation(yts[:, :], y_ps[:, :], ACT.Copy).then_inc(s["yts"], 1)

            @block.vector
            def _(dve):
                with dve.Fori(0, B // SB) as q:
                    f0 = NP * q
                    dve.wait_ge(s["o"], q)
                    for k in range(SB):
                        nc.vector.tensor_scalar(diag[:, k, :], T["ident"][:, :], T["mod"][:, L0F, 2, bass.ds(SB * q + k, 1)], None,
                                                ALU.mult).then_inc(s["diag"], 1)
                    for p in range(NP):
                        dve.wait_ge(s["silu"], f0 + p + 1)
                        dve.wait_ge(s["u"], (2 * EP + 1) * q + (2 * p + 2 if p < EP else 2 * EP + 1))
                        if p < EP:
                            nc.vector.tensor_tensor(su[:, p % 2, :], sg[:, p % 2, :], u_ps[p % 2][:, :], ALU.mult).then_inc(s["su"], 1)
                            dve.wait_ge(s["su"], f0 + p + 1)
                            if p >= 2:
                                dve.wait_ge(s["down"], f0 + p - 1)
                            else:
                                dve.wait_ge(s["down"], f0)
                            nc.vector.tensor_tensor(act_w[:, p % 2, :], su[:, p % 2, :], w_ps[p % 2][:, :], ALU.mult).then_inc(s["act"], 1)
                        else:
                            dve.wait_ge(s["down"], f0 + p - 1)
                            nc.vector.tensor_tensor(act_w[0:I, p % 2, :], sg[0:I, p % 2, :], u_ps[p % 2][0:I, :], ALU.mult).then_inc(s["act"], 1)
                            dve.wait_ge(s["act"], f0 + p + 1)
                            dve.sem_inc(s["su"], 1)
                    dve.wait_ge(s["o"], q + 1)
                    xq = T["x"][:, bass.ds(TB * SB * q, TB * SB), :].rearrange("p a d -> p (a d)")
                    nc.vector.tensor_tensor(xq, xq, o_ps[:, :], ALU.add).then_inc(s["res"], 1)


def linear_attention(nc, T, sems):
    with ExitStack() as own:
        def tmp(name, shape, dt=F32):
            return own.enter_context(nc.sbuf_tensor("l_" + name, shape, dt))

        NT = TB * SB
        stats = tmp("stats", [P, NT, 6])
        mv = tmp("mv", [P, NT, 2])
        veps = tmp("veps", [P, 8])
        rstd = tmp("rstd", [P, 8])
        h0 = tmp("h0", [P, NT, D])
        ht = tmp("ht", [P, N2])
        qk_stats = tmp("qk_stats", [P, 2 * NT, 6])
        qk_mv = tmp("qk_mv", [P, NT, 2, 2])
        den = tmp("den", [P, NT, 2])
        r1 = tmp("r1", [P, NT, 2])
        cen = tmp("cen", [P, 2 * NT, D])
        sq = tmp("sq", [P, NT, 2, D])
        q4 = tmp("q4", [P, NT, D])
        q4s = tmp("q4s", [P, NT])
        r1q = tmp("r1q", [P, NT])
        n2 = tmp("n2", [P, NT])
        nq = tmp("nq", [P, NT])
        rq = tmp("rq", [P, NT])
        q2n = tmp("q2n", [P, NT, D])
        k2 = tmp("k2", [P, NT, D])
        k4 = tmp("k4", [P, NT, D])
        v = tmp("v", [P, NT, D])
        q2t = tmp("q2t", [P, N2])
        kn = tmp("kn", [P, SB])
        knr = tmp("knr", [P, SB])
        rk = tmp("rk", [P, SB])
        kvs = tmp("kvs", [P, SB, D])
        zts = tmp("zts", [P, N2])
        yts = tmp("yts", [P, N2])
        diag = tmp("diag", [P, SB, P])
        ht_ps = own.enter_context(nc.psum_tensor("l_ht_ps", [P, 512], F32))
        qk_ps = own.enter_context(nc.psum_tensor("l_qk", [P, NT, 2 * D], F32))
        v_ps = own.enter_context(nc.psum_tensor("l_v_ps", [P, NT, D], F32))
        kv_ps = own.enter_context(nc.psum_tensor("l_kv", [P, 512], F32))
        qt_ps = own.enter_context(nc.psum_tensor("l_qt", [P, 512], F32))
        z_ps = own.enter_context(nc.psum_tensor("l_z", [P, 512], F32))
        y_ps = own.enter_context(nc.psum_tensor("l_y", [P, 512], F32))
        s = sems("l", ["n_" + n for n in NORM_SEMS] +
                 ["ht_ps", "ht", "qk", "v_ps", "v", "qk_stats", "qk_mv", "den", "r1", "cen", "sq", "q4", "q4s", "r1q", "n2", "nq",
                  "nqm", "rq", "rq2", "q2n", "k2", "k4", "kv", "kn", "knr", "knm", "rk", "kvs", "qt", "q2t", "z", "zts", "y", "yts",
                  "diag", "o", "res"], own)
        with nc.Block() as block:
            @block.gpsimd
            def _(pool):
                with pool.Fori(0, B // SB) as q:
                    norm_pool_rstd(nc, pool, s, "n", mv, veps, rstd, T["eps"], T["neg_half"], q)
                    pool.wait_ge(s["n2"], q + 1)
                    nc.gpsimd.tensor_tensor(nq[:, :], n2[:, :], T["half"][:, 0:NT], ALU.pow).then_inc(s["nq"], 1)
                    pool.wait_ge(s["kn"], q + 1)
                    nc.gpsimd.tensor_tensor(knr[:, :], kn[:, :], T["half"][:, 0:SB], ALU.pow).then_inc(s["knr"], 1)

            @block.vector
            def _(dve):
                with dve.Fori(0, B // SB) as q:
                    xt = [T["x"][:, bass.ds(NT * q + t, 1), :].rearrange("p a d -> p (a d)") for t in range(NT)]
                    norm_vector_stats(nc, dve, s, "n", xt, stats, mv, q)
                    norm_vector_apply(nc, dve, s, "n", xt, mv, rstd, h0, q)
                    for k in range(SB):
                        nc.vector.tensor_scalar(diag[:, k, :], T["ident"][:, :], T["mod"][:, L1A, 2, bass.ds(SB * q + k, 1)], None,
                                                ALU.mult).then_inc(s["diag"], 1)
                    dve.wait_ge(s["qk"], q + 1)
                    for t in range(NT):
                        for j in range(2):
                            nc.vector.bn_stats(qk_stats[:, 2 * t + j, :], qk_ps[:, t, j * D:(j + 1) * D]).then_inc(s["qk_stats"], 1)
                    nc.vector.drain()
                    for t in range(NT):
                        for j in range(2):
                            nc.vector.bn_aggr(qk_mv[:, t, j, :], qk_stats[:, 2 * t + j, :]).then_inc(s["qk_mv"], 1)
                    dve.wait_ge(s["qk_mv"], 2 * NT * (q + 1))
                    nc.vector.tensor_tensor(cen[:, :, :], qk_ps[:, :, :].rearrange("p t (j d) -> p (t j) d", j=2),
                                            qk_mv[:, :, :, 0].rearrange("p t j -> p (t j)").unsqueeze(2).to_broadcast([P, 2 * NT, D]),
                                            ALU.subtract).then_inc(s["cen"], 1)
                    nc.vector.tensor_scalar(den[:, :, :], qk_mv[:, :, :, 1], float(D), 1e-7, ALU.mult, ALU.add).then_inc(s["den"], 1)
                    dve.wait_ge(s["den"], q + 1)
                    nc.vector.reciprocal(r1[:, :, :], den[:, :, :]).then_inc(s["r1"], 1)
                    dve.wait_ge(s["r1"], q + 1)
                    nc.vector.tensor_tensor(r1q[:, :], r1[:, :, 0], r1[:, :, 0], ALU.mult).then_inc(s["r1q"], 1)
                    dve.wait_ge(s["sq"], q + 1)
                    nc.vector.tensor_tensor(k2[:, :, :], sq[:, :, 1, :], r1[:, :, 1].unsqueeze(2).to_broadcast([P, NT, D]),
                                            ALU.mult).then_inc(s["k2"], 1)
                    nc.vector.tensor_tensor(q4[:, :, :], sq[:, :, 0, :], sq[:, :, 0, :], ALU.mult).then_inc(s["q4"], 1)
                    dve.wait_ge(s["q4"], q + 1)
                    nc.vector.tensor_reduce(q4s[:, :], q4[:, :, :], AX.X, ALU.add).then_inc(s["q4s"], 1)
                    dve.wait_ge(s["q4s"], q + 1)
                    dve.wait_ge(s["r1q"], q + 1)
                    nc.vector.tensor_tensor(n2[:, :], q4s[:, :], r1q[:, :], ALU.mult).then_inc(s["n2"], 1)
                    dve.wait_ge(s["nq"], q + 1)
                    nc.vector.tensor_scalar(nq[:, :], nq[:, :], 1e-12, None, ALU.max).then_inc(s["nqm"], 1)
                    dve.wait_ge(s["nqm"], q + 1)
                    nc.vector.reciprocal(rq[:, :], nq[:, :]).then_inc(s["rq"], 1)
                    dve.wait_ge(s["rq"], q + 1)
                    nc.vector.tensor_tensor(rq[:, :], rq[:, :], r1[:, :, 0], ALU.mult).then_inc(s["rq2"], 1)
                    dve.wait_ge(s["rq2"], q + 1)
                    nc.vector.tensor_tensor(q2n[:, :, :], sq[:, :, 0, :], rq[:, :].unsqueeze(2).to_broadcast([P, NT, D]),
                                            ALU.mult).then_inc(s["q2n"], 1)
                    dve.wait_ge(s["kv"], q + 1)
                    nc.vector.tensor_copy(kn[:, :], kv_ps[:, SB * D:SB * D + SB]).then_inc(s["kn"], 1)
                    dve.wait_ge(s["knr"], q + 1)
                    nc.vector.tensor_scalar(knr[:, :], knr[:, :], 1e-12, float(S) ** 0.5, ALU.max, ALU.mult).then_inc(s["knm"], 1)
                    dve.wait_ge(s["knm"], q + 1)
                    nc.vector.reciprocal(rk[:, :], knr[:, :]).then_inc(s["rk"], 1)
                    dve.wait_ge(s["rk"], q + 1)
                    for k in range(SB):
                        nc.vector.tensor_scalar(kvs[:, k, :], kv_ps[:, k * D:(k + 1) * D], rk[:, k:k + 1], None,
                                                ALU.mult).then_inc(s["kvs"], 1)
                    dve.wait_ge(s["o"], q + 1)
                    xq = T["x"][:, bass.ds(NT * q, NT), :].rearrange("p a d -> p (a d)")
                    nc.vector.tensor_tensor(xq, xq, ht_ps[:, :], ALU.add).then_inc(s["res"], 1)

            @block.scalar
            def _(act):
                with act.Fori(0, B // SB) as q:
                    act.wait_ge(s["ht_ps"], q + 1)
                    for k in range(SB):
                        nc.scalar.activation(ht[:, k * S:(k + 1) * S], ht_ps[:, k * S:(k + 1) * S], ACT.Identity,
                                             scale=T["mod"][:, L1A, 1, bass.ds(SB * q + k, 1)],
                                             bias=T["mod"][:, L1A, 0, bass.ds(SB * q + k, 1)]).then_inc(s["ht"], 1)
                    act.wait_ge(s["v_ps"], q + 1)
                    nc.scalar.activation(v[:, :, :], v_ps[:, :, :], ACT.Copy).then_inc(s["v"], 1)
                    act.wait_ge(s["cen"], q + 1)
                    nc.scalar.activation(sq[:, :, :, :].rearrange("p t j d -> p (t j) d"), cen[:, :, :], ACT.Square).then_inc(s["sq"], 1)
                    act.wait_ge(s["k2"], q + 1)
                    nc.scalar.activation(k4[:, :, :], k2[:, :, :], ACT.Square).then_inc(s["k4"], 1)
                    act.wait_ge(s["qt"], q + 1)
                    nc.scalar.activation(q2t[:, :], qt_ps[:, :], ACT.Copy).then_inc(s["q2t"], 1)
                    act.wait_ge(s["z"], q + 1)
                    nc.scalar.activation(zts[:, :], z_ps[:, :], ACT.Identity, bias=T["bv"][:, 0:1]).then_inc(s["zts"], 1)
                    act.wait_ge(s["y"], q + 1)
                    nc.scalar.activation(yts[:, :], y_ps[:, :], ACT.Identity, bias=T["bln"][:, 0:1]).then_inc(s["yts"], 1)

            @block.tensor
            def _(pe):
                with pe.Fori(0, B // SB) as q:
                    pe.wait_ge(s["n_h0"], NT * (q + 1))
                    for t in range(NT):
                        last = nc.tensor.transpose(ht_ps[:, t * P:(t + 1) * P], h0[:, t, :], T["ident"][:, :])
                    last.then_inc(s["ht_ps"], 1)
                    pe.wait_ge(s["ht"], SB * (q + 1))
                    for t in range(NT):
                        nc.tensor.matmul(qk_ps[:, t, :], ht[:, t * P:(t + 1) * P], T["wqkv"][:, 0:2 * D], start=True, stop=False)
                        last = nc.tensor.matmul(qk_ps[:, t, :], T["ones"][0:1, :], T["bqkv"][:, 0:2 * D], start=False, stop=True)
                    last.then_inc(s["qk"], 1)
                    for t in range(NT):
                        nc.tensor.matmul(v_ps[:, t, :], ht[:, t * P:(t + 1) * P], T["wqkv"][:, 2 * D:3 * D], start=True, stop=False)
                        last = nc.tensor.matmul(v_ps[:, t, :], T["ones"][0:1, :], T["bqkv"][:, 2 * D:3 * D], start=False, stop=True)
                    last.then_inc(s["v_ps"], 1)
                    pe.wait_ge(s["v"], q + 1)
                    pe.wait_ge(s["k4"], q + 1)
                    for k in range(SB):
                        for t in range(TB):
                            nc.tensor.matmul(kv_ps[:, k * D:(k + 1) * D], k2[:, TB * k + t, :], v[:, TB * k + t, :],
                                             start=(t == 0), stop=(t == TB - 1))
                    for k in range(SB):
                        for t in range(TB):
                            last = nc.tensor.matmul(kv_ps[:, SB * D + k:SB * D + k + 1], k4[:, TB * k + t, :], T["ones"][:, 0:1],
                                                    start=(t == 0), stop=(t == TB - 1))
                    last.then_inc(s["kv"], 1)
                    pe.wait_ge(s["q2n"], q + 1)
                    for t in range(NT):
                        last = nc.tensor.transpose(qt_ps[:, t * P:(t + 1) * P], q2n[:, t, :], T["ident"][:, :])
                    last.then_inc(s["qt"], 1)
                    pe.wait_ge(s["kvs"], SB * (q + 1))
                    pe.wait_ge(s["q2t"], q + 1)
                    for k in range(SB):
                        z = z_ps[:, k * S:(k + 1) * S]
                        nc.tensor.matmul(z, T["wqkv"][:, 2 * D:3 * D], ht[:, k * S:(k + 1) * S], start=True, stop=False)
                        last = nc.tensor.matmul(z, kvs[:, k, :], q2t[:, k * S:(k + 1) * S], start=False, stop=True)
                    last.then_inc(s["z"], 1)
                    pe.wait_ge(s["zts"], q + 1)
                    nc.tensor.matmul(y_ps[:, :], T["wln"][:, :], zts[:, :], start=True, stop=True).then_inc(s["y"], 1)
                    pe.wait_ge(s["yts"], q + 1)
                    pe.wait_ge(s["diag"], SB * (q + 1))
                    for t in range(NT):
                        last = nc.tensor.matmul(ht_ps[:, t * P:(t + 1) * P], yts[:, t * P:(t + 1) * P], diag[:, t // TB, :],
                                                start=True, stop=True)
                    last.then_inc(s["o"], 1)


def slots(nc, T, sems):
    with ExitStack() as own:
        def tmp(name, shape, dt=F32):
            return own.enter_context(nc.sbuf_tensor("s_" + name, shape, dt))

        stats = tmp("stats", [P, TB, 6])
        mv = tmp("mv", [P, TB, 2])
        veps = tmp("veps", [P, 8])
        rstd = tmp("rstd", [P, 8])
        h0 = tmp("h0", [P, TB, D])
        ht = tmp("ht", [P, S])
        hsq = tmp("hsq", [P, S])
        gdiag = tmp("gdiag", [P, P])
        bdiag = tmp("bdiag", [P, P])
        gb = tmp("gb", [P, P])
        ssum = tmp("ssum", [P, TB])
        norm = tmp("norm", [P, TB])
        rnorm = tmp("rnorm", [P, TB])
        xn = tmp("xn", [P, TB, D + 1])
        xnt = tmp("xnt", [P, S])
        m_slot = tmp("m_slot", [P, SC])
        m_tok = tmp("m_tok", [P, TB])
        d_slot = tmp("d_slot", [P, SC, P], F32R)
        d_tok = tmp("d_tok", [P, TB, P], F32R)
        disp = tmp("disp", [P, TB, SLOTS])
        comb = tmp("comb", [P, SC, S])
        rz = tmp("rz", [P, SC])
        sl = tmp("sl", [P, SC, D])
        slt = tmp("slt", [P, SLOTS])
        hid = tmp("hid", [P, HC, SLOTS])
        proc = tmp("proc", [P, SC, D + 1])
        ru = tmp("ru", [P, TB])
        yo = tmp("yo", [P, TB, D])
        pa = own.enter_context(nc.psum_tensor("s_a", [P, TB, SLOTS], F32))
        pb = own.enter_context(nc.psum_tensor("s_b", [P, SC, S], F32))
        pc = own.enter_context(nc.psum_tensor("s_c", [P, 2, 512], F32))
        pd = own.enter_context(nc.psum_tensor("s_d", [P, 512], F32))
        pe_ = own.enter_context(nc.psum_tensor("s_e", [P, 512], F32))
        s = sems("s", ["n_" + n for n in NORM_SEMS] +
                 ["one", "gdiag", "bdiag", "ht_ps", "ht", "hsq", "ss", "ssum", "norm", "nm", "rn", "xt_ps", "gb", "xn", "xnt_ps", "xnt",
                  "la", "lb", "m_tok", "m_slot", "d", "fa", "fb", "disp", "comb", "sl_ps", "rz", "sl", "slt_ps", "slt", "h_ps",
                  "hid", "pr_ps", "proc", "u_ps", "ru", "yo", "yg", "res"], own)
        banks = [pa[:, 0, :], pa[:, 1, :], pb[:, 0:2, :].rearrange("p a n -> p (a n)"), pb[:, 2:4, :].rearrange("p a n -> p (a n)")]
        slot_out = lambda c, n: pc[:, c // 2, c % 2 * (D + 1):c % 2 * (D + 1) + n]
        with nc.Block() as block:
            @block.gpsimd
            def _(pool):
                nc.gpsimd.memset(xn[:, :, D:D + 1], 1.0).then_inc(s["one"], 1)
                nc.gpsimd.memset(proc[:, :, D:D + 1], 1.0).then_inc(s["one"], 1)
                with pool.Fori(0, B) as b:
                    norm_pool_rstd(nc, pool, s, "n", mv, veps, rstd, T["eps"], T["neg_half"], b)
                    pool.wait_ge(s["ssum"], b + 1)
                    nc.gpsimd.tensor_tensor(norm[:, :], ssum[:, :], T["half"][:, 0:TB], ALU.pow).then_inc(s["norm"], 1)

            @block.vector
            def _(dve):
                nc.vector.tensor_scalar(gdiag[:, :], T["ident"][:, :], T["gx"][:, 0:1], float(D) ** 0.5,
                                        ALU.mult, ALU.mult).then_inc(s["gdiag"], 1)
                with dve.Fori(0, B) as b:
                    xt = [T["x"][:, bass.ds(TB * b + t, 1), :].rearrange("p a d -> p (a d)") for t in range(TB)]
                    norm_vector_stats(nc, dve, s, "n", xt, stats, mv, b)
                    norm_vector_apply(nc, dve, s, "n", xt, mv, rstd, h0, b)
                    nc.vector.tensor_scalar(bdiag[:, :], T["ident"][:, :], T["mod"][:, L1F, 2, bass.ds(b, 1)], None,
                                            ALU.mult).then_inc(s["bdiag"], 1)
                    dve.wait_ge(s["ss"], b + 1)
                    nc.vector.tensor_copy(ssum[:, :], pe_[:, 0:TB]).then_inc(s["ssum"], 1)
                    dve.wait_ge(s["norm"], b + 1)
                    nc.vector.tensor_scalar(norm[:, :], norm[:, :], 1e-12, None, ALU.max).then_inc(s["nm"], 1)
                    dve.wait_ge(s["nm"], b + 1)
                    nc.vector.reciprocal(rnorm[:, :], norm[:, :]).then_inc(s["rn"], 1)
                    dve.wait_ge(s["rn"], b + 1)
                    dve.wait_ge(s["xt_ps"], b + 1)
                    nc.vector.tensor_tensor(xn[:, :, 0:D], pe_[:, S:2 * S].rearrange("p (t d) -> p t d", t=TB),
                                            rnorm[:, :].unsqueeze(2).to_broadcast([P, TB, D]), ALU.mult).then_inc(s["xn"], 1)
                    nc.vector.tensor_copy(gb[:, :], pe_[:, P:2 * P]).then_inc(s["gb"], 1)
                    dve.wait_ge(s["la"], b + 1)
                    nc.vector.tensor_reduce(m_tok[:, :], pa[:, :, :], AX.X, ALU.max).then_inc(s["m_tok"], 1)
                    dve.wait_ge(s["lb"], b + 1)
                    nc.vector.tensor_reduce(m_slot[:, :], pb[:, :, :], AX.X, ALU.max).then_inc(s["m_slot"], 1)
                    dve.wait_ge(s["m_slot"], b + 1)
                    for k in range(SC):
                        nc.vector.tensor_scalar(d_slot[:, k, :], T["ident"][:, :], m_slot[:, k:k + 1], -1.0,
                                                ALU.mult, ALU.mult).then_inc(s["d"], 1)
                    for t in range(TB):
                        nc.vector.tensor_scalar(d_tok[:, t, :], T["ident"][:, :], m_tok[:, t:t + 1], -1.0,
                                                ALU.mult, ALU.mult).then_inc(s["d"], 1)
                    dve.wait_ge(s["sl_ps"], b + 1)
                    for k in range(SC):
                        nc.vector.reciprocal(rz[:, k:k + 1], slot_out(k, D + 1)[:, D:D + 1]).then_inc(s["rz"], 1)
                    dve.wait_ge(s["rz"], SC * (b + 1))
                    for k in range(SC):
                        nc.vector.tensor_scalar(sl[:, k, :], slot_out(k, D), rz[:, k:k + 1], None, ALU.mult).then_inc(s["sl"], 1)
                    dve.wait_ge(s["slt_ps"], b + 1)
                    nc.vector.tensor_copy(slt[:, :], pd[:, :]).then_inc(s["slt"], 1)
                    dve.wait_ge(s["pr_ps"], b + 1)
                    nc.vector.tensor_copy(proc[:, :, 0:D], pe_[:, :].rearrange("p (c d) -> p c d", c=SC)).then_inc(s["proc"], 1)
                    dve.wait_ge(s["u_ps"], b + 1)
                    uo = pd[:, 0:TB * (D + 1)].rearrange("p (t d) -> p t d", t=TB)
                    nc.vector.reciprocal(ru[:, :], uo[:, :, D]).then_inc(s["ru"], 1)
                    dve.wait_ge(s["ru"], b + 1)
                    for t in range(TB):
                        nc.vector.scalar_tensor_tensor(yo[:, t, :], uo[:, t, 0:D], ru[:, t:t + 1], gb[:, :],
                                                       ALU.mult, ALU.mult).then_inc(s["yo"], 1)
                    dve.wait_ge(s["yo"], TB * (b + 1))
                    xb = T["x"][:, bass.ds(TB * b, TB), :]
                    nc.vector.tensor_tensor(xb, xb, yo[:, :, :], ALU.add).then_inc(s["res"], 1)

            @block.scalar
            def _(act):
                with act.Fori(0, B) as b:
                    act.wait_ge(s["ht_ps"], b + 1)
                    nc.scalar.activation(ht[:, :], pd[:, 0:S], ACT.Identity, scale=T["mod"][:, L1F, 1, bass.ds(b, 1)],
                                         bias=T["mod"][:, L1F, 0, bass.ds(b, 1)]).then_inc(s["ht"], 1)
                    act.wait_ge(s["ht"], b + 1)
                    nc.scalar.activation(hsq[:, :], ht[:, :], ACT.Square).then_inc(s["hsq"], 1)
                    act.wait_ge(s["xnt_ps"], b + 1)
                    nc.scalar.activation(xnt[:, :], pd[:, S:2 * S], ACT.Copy).then_inc(s["xnt"], 1)
                    act.wait_ge(s["fa"], b + 1)
                    nc.scalar.activation(disp[:, :, :], pa[:, :, :], ACT.Exp).then_inc(s["disp"], 1)
                    act.wait_ge(s["fb"], b + 1)
                    nc.scalar.activation(comb[:, :, :], pb[:, :, :], ACT.Exp).then_inc(s["comb"], 1)
                    for j in range(HC):
                        act.wait_ge(s["h_ps"], HC * b + j + 1)
                        nc.scalar.activation(hid[:, j, :], banks[j], ACT.Gelu).then_inc(s["hid"], 1)

            @block.tensor
            def _(pe):
                pe.wait_ge(s["one"], 2)
                pe.wait_ge(s["gdiag"], 1)
                with pe.Fori(0, B) as b:
                    pe.wait_ge(s["n_h0"], TB * (b + 1))
                    pe.wait_ge(s["res"], b)
                    for t in range(TB):
                        last = nc.tensor.transpose(pd[:, t * P:(t + 1) * P], h0[:, t, :], T["ident"][:, :])
                    last.then_inc(s["ht_ps"], 1)
                    pe.wait_ge(s["hsq"], b + 1)
                    for t in range(TB):
                        last = nc.tensor.matmul(pe_[:, t:t + 1], hsq[:, t * P:(t + 1) * P], T["ones"][:, 0:1], start=True, stop=True)
                    last.then_inc(s["ss"], 1)
                    pe.wait_ge(s["bdiag"], b + 1)
                    pe.wait_ge(s["ssum"], b + 1)
                    nc.tensor.matmul(pe_[:, P:2 * P], T["ones"][:, :], bdiag[:, :], start=True, stop=True)
                    for t in range(TB):
                        last = nc.tensor.matmul(pe_[:, S + t * P:S + (t + 1) * P], ht[:, t * P:(t + 1) * P], gdiag[:, :],
                                                start=True, stop=True)
                    last.then_inc(s["xt_ps"], 1)
                    pe.wait_ge(s["xn"], b + 1)
                    for t in range(TB):
                        last = nc.tensor.transpose(pd[:, S + t * P:S + (t + 1) * P], xn[:, t, 0:D], T["ident"][:, :])
                    last.then_inc(s["xnt_ps"], 1)
                    pe.wait_ge(s["xnt"], b + 1)
                    pe.wait_ge(s["hid"], HC * b)
                    for t in range(TB):
                        last = nc.tensor.matmul(pa[:, t, :], xnt[:, t * P:(t + 1) * P], T["se_t"][:, :], start=True, stop=False,
                                                skip_group_check=True)
                    last.then_inc(s["la"], 1)
                    for k in range(SC):
                        last = nc.tensor.matmul(pb[:, k, :], T["se_t"][:, k * P:(k + 1) * P], xnt[:, :], start=(k % 2 == 0), stop=False,
                                                skip_group_check=True)
                    last.then_inc(s["lb"], 1)
                    pe.wait_ge(s["d"], (SC + TB) * (b + 1))
                    for t in range(TB):
                        last = nc.tensor.matmul(pa[:, t, :], T["ones_r"][:, :], d_slot[:, :, :].rearrange("p c n -> p (c n)"),
                                                start=False, stop=True, skip_group_check=True)
                    last.then_inc(s["fa"], 1)
                    for k in range(SC):
                        last = nc.tensor.matmul(pb[:, k, :], T["ones_r"][:, :], d_tok[:, :, :].rearrange("p t n -> p (t n)"),
                                                start=False, stop=True, skip_group_check=True)
                    last.then_inc(s["fb"], 1)
                    pe.wait_ge(s["disp"], b + 1)
                    for k in range(SC):
                        for t in range(TB):
                            last = nc.tensor.matmul(slot_out(k, D + 1), disp[:, t, k * P:(k + 1) * P], xn[:, t, :],
                                                    start=(t == 0), stop=(t == TB - 1), skip_group_check=True)
                    last.then_inc(s["sl_ps"], 1)
                    pe.wait_ge(s["sl"], SC * (b + 1))
                    for k in range(SC):
                        last = nc.tensor.transpose(pd[:, k * P:(k + 1) * P], sl[:, k, :], T["ident"][:, :])
                    last.then_inc(s["slt_ps"], 1)
                    pe.wait_ge(s["slt"], b + 1)
                    pe.wait_ge(s["comb"], b + 1)
                    for j in range(HC):
                        nc.tensor.matmul(banks[j], T["w1"][:, j * P:(j + 1) * P], slt[:, :], start=True, stop=True,
                                         skip_group_check=True).then_inc(s["h_ps"], 1)
                    pe.wait_ge(s["hid"], HC * (b + 1))
                    for k in range(SC):
                        for j in range(HC):
                            last = nc.tensor.matmul(pe_[:, k * P:(k + 1) * P], hid[:, j, k * P:(k + 1) * P], T["w2"][:, j, :],
                                                    start=(j == 0), stop=(j == HC - 1))
                    last.then_inc(s["pr_ps"], 1)
                    pe.wait_ge(s["proc"], b + 1)
                    for t in range(TB):
                        for k in range(SC):
                            last = nc.tensor.matmul(pd[:, t * (D + 1):(t + 1) * (D + 1)], comb[:, k, t * P:(t + 1) * P], proc[:, k, :],
                                                    start=(k == 0), stop=(k == SC - 1))
                    last.then_inc(s["u_ps"], 1)


_INS = ['L0_attn_q', 'L0_attn_W_query', 'L0_attn_W_key', 'L0_attn_W_val', 'L0_attn_W_out', 'L0_ffn_gate_w',
        'L0_ffn_expert_gate', 'L0_ffn_expert_up', 'L0_ffn_expert_down', 'L0_ffn_shared_gate_w', 'L0_ffn_shared_up_w',
        'L0_ffn_shared_down_w', 'L0_c', 'L0_wmod', 'L1_attn_Wqkv', 'L1_attn_bqkv', 'L1_attn_Wln', 'L1_attn_bln',
        'L1_ffn_gamma_x', 'L1_ffn_gamma_slot', 'L1_ffn_slot_embeds', 'L1_ffn_w1', 'L1_ffn_w2', 'L1_c', 'L1_wmod']


def kernel(**inputs):
    import numpy as _np
    import concourse.bacc as _bacc
    from concourse import mybir as _mybir
    from concourse.bass_utils import run_bass_kernel_spmd as _run

    nc = _bacc.Bacc("TRN2", target_bir_lowering=False, num_devices=1)
    arrays, aps = {}, {}
    for name in _INS:
        a = _np.ascontiguousarray(inputs[name])
        arrays[f"in_{name}_dram"] = a
        aps[name] = nc.dram_tensor(f"in_{name}_dram", a.shape, _mybir.dt.from_np(a.dtype), kind="ExternalInput").ap()
    rows = row_constants()
    arrays["rows_dram"] = rows
    aps["rows"] = nc.dram_tensor("rows_dram", rows.shape, _mybir.dt.from_np(rows.dtype), kind="ExternalInput").ap()
    out = nc.dram_tensor("out_dram", (B, S, D), F32, kind="ExternalOutput").ap()
    network(nc, aps, out)
    r = _run(nc, [arrays], core_ids=[0])
    return r.results[0]["out_dram"]
```

```python
from contextlib import ExitStack

import numpy as np
import concourse.bass as bass
from concourse import mybir

F32 = mybir.dt.float32
F32R = mybir.dt.float32r
ALU = mybir.AluOpType
ACT = mybir.ActivationFunctionType
AX = mybir.AxisListType

P = 128
B, S, D = 8, 256, 128
TB = S // P
TILES = B * TB
H, DK = 16, 8
HB = 4
HG = H // HB
STACK = P // HB
M_ROW = 3 * DK
E, I = 32, 64
EP = E // 2
TOPK, GROUPS, TOPG = 8, 8, 4
EPG = E // GROUPS
SB = 2
N2 = SB * S
SLOTS = 512
SC = SLOTS // P
HID = 512
HC = HID // P
LN_EPS = 1e-5
ATTN_SCALE = float(1.0 / np.sqrt(DK))

L0A, L0F, L1A, L1F = range(4)


def row_constants():
    part = np.arange(P) % STACK // DK
    row = np.arange(P) % STACK
    q_low = (part == 1).astype(np.float32)
    k_low = (part == 2).astype(np.float32)
    ones = ((row == M_ROW) | (row == M_ROW + 1)).astype(np.float32)
    return np.ascontiguousarray(np.stack([q_low, 1 - 2 * q_low, k_low, 1 - 2 * k_low, ones], axis=1))


def norm_vector_stats(nc, dve, s, name, x_tiles, stats, mv, n):
    k = len(x_tiles)
    for t, x in enumerate(x_tiles):
        nc.vector.bn_stats(stats[:, t, :], x).then_inc(s[name + "_stats"], 1)
    nc.vector.drain()
    for t in range(k):
        nc.vector.bn_aggr(mv[:, t, :], stats[:, t, :]).then_inc(s[name + "_mv"], 1)


def norm_pool_rstd(nc, pool, s, name, mv, veps, rstd, eps, half, n):
    k = mv.shape[1]
    pool.wait_ge(s[name + "_mv"], k * (n + 1))
    nc.gpsimd.tensor_tensor(veps[:, 0:k], mv[:, :, 1], eps[:, 0:k], ALU.add).then_inc(s[name + "_veps"], 1)
    pool.wait_ge(s[name + "_veps"], n + 1)
    nc.gpsimd.tensor_tensor(rstd[:, 0:k], veps[:, 0:k], half[:, 0:k], ALU.pow).then_inc(s[name + "_rstd"], 1)


def norm_vector_apply(nc, dve, s, name, x_tiles, mv, rstd, h0, n):
    dve.wait_ge(s[name + "_rstd"], n + 1)
    for t, x in enumerate(x_tiles):
        nc.vector.tensor_scalar(h0[:, t, :], x, mv[:, t, 0:1], rstd[:, t:t + 1],
                                ALU.subtract, ALU.mult).then_inc(s[name + "_h0"], 1)


NORM_SEMS = ["stats", "mv", "veps", "rstd", "h0"]


def network(nc, A, out, phases=4):
    with ExitStack() as ctx:
        def sb(name, shape, dt=F32):
            return ctx.enter_context(nc.sbuf_tensor(name, shape, dt))

        def sems(prefix, names, own=ctx):
            made = {n: nc.alloc_semaphore(f"{prefix}_{n}") for n in names}
            own.callback(nc.all_engine_barrier)
            own.callback(nc.clear_and_free_semaphores, list(made.values()))
            return made

        T = {}
        T["x"] = sb("x", [P, TILES, D])
        T["ident"] = sb("ident", [P, P])
        T["ones"] = sb("ones", [P, P])
        T["ones_r"] = sb("ones_r", [P, P], F32R)
        T["mod"] = sb("mod", [P, 4, 3, B])
        T["neg_half"] = sb("neg_half", [P, 8])
        T["half"] = sb("half", [P, 8])
        T["eps"] = sb("eps", [P, 8])
        T["rows"] = sb("rows", [P, 5])
        T["wq"] = sb("wq", [P, H, DK])
        T["wk"] = sb("wk", [P, H, DK])
        T["wv"] = sb("wv", [P, H, DK])
        T["wo"] = sb("wo", [P, D])
        T["diag"] = sb("diag", [P, 4, B, P])
        T["wo_b"] = sb("wo_b", [P, B, D])
        T["wqs"] = sb("wqs", [P, HG, HB, 4, DK])
        T["wks"] = sb("wks", [P, HG, HB, 4, DK])
        T["wqk_hi"] = sb("wqk_hi", [P, 2, HG, P], F32R)
        T["wqk_lo"] = sb("wqk_lo", [P, 2, HG, P], F32R)
        T["gate_t"] = sb("gate_t", [P, E])
        T["gu_hi"] = sb("gu_hi", [P, 2, EP, P], F32R)
        T["gu_lo"] = sb("gu_lo", [P, 2, EP, P], F32R)
        T["down"] = sb("down", [P, EP, P])
        T["sh_hi"] = sb("sh_hi", [P, 2, I], F32R)
        T["sh_lo"] = sb("sh_lo", [P, 2, I], F32R)
        T["sh_down"] = sb("sh_down", [I, P])
        T["sel"] = sb("sel", [2 * E, EP, P], F32R)
        T["wqkv"] = sb("wqkv", [P, 3 * D])
        T["bqkv"] = sb("bqkv", [1, 3 * D])
        T["bv"] = sb("bv", [P, 1])
        T["wln"] = sb("wln", [P, D])
        T["bln"] = sb("bln", [P, 1])
        T["gx"] = sb("gx", [P, 1])
        T["gs"] = sb("gs", [P, 1])
        T["w1_hi"] = sb("w1_hi", [P, HID], F32R)
        T["w1_lo"] = sb("w1_lo", [P, HID], F32R)
        T["w2"] = sb("w2", [P, HC, D])
        T["se_hi"] = sb("se_hi", [P, SLOTS], F32R)
        T["se_lo"] = sb("se_lo", [P, SLOTS], F32R)
        T["gb"] = sb("gb", [P, B, D])

        prepare(nc, ctx, T, A, sb, sems)
        if phases >= 1:
            attention(nc, T, sems)
        if phases >= 2:
            experts(nc, T, sems)
        if phases >= 3:
            linear_attention(nc, T, sems)
        if phases >= 4:
            slots(nc, T, sems)
        s = sems("end", ["stored"])
        with nc.Block() as block:
            @block.sync
            def _(sp):
                sp.dma_start(out.rearrange("b (t p) d -> p (b t) d", p=P), T["x"][:, :, :]).then_inc(s["stored"], 16)
                sp.wait_ge(s["stored"], 16)


def prepare(nc, ctx, T, A, sb, sems):
    with ExitStack() as own:
        def tmp(name, shape, dt=F32):
            return own.enter_context(nc.sbuf_tensor("p_" + name, shape, dt))

        eg = tmp("eg", [P, EP, D])
        eu = tmp("eu", [P, EP, D])
        ed = tmp("ed", [P, E, I])
        shg = tmp("shg", [I, D])
        shu = tmp("shu", [I, D])
        shd = tmp("shd", [D, I])
        gw = tmp("gw", [E, D])
        c = tmp("c", [B, 2, P])
        cs = tmp("cs", [B, 2, P])
        ct = tmp("ct", [P, 2, B])
        wmod = tmp("wmod", [P, 2, 6 * D])
        w1 = tmp("w1", [P, HID])
        se_t = tmp("se_t", [P, SLOTS])
        slot = tmp("slot", [P, SC, D])
        slot_sq = tmp("slot_sq", [P, SC, D])
        slot_n = tmp("slot_n", [P, SC, D])
        ss = tmp("ss", [P, SC])
        sn = tmp("sn", [P, SC])
        sr = tmp("sr", [P, SC])
        sgn = tmp("sgn", [P, 4, B])
        wot = tmp("wot", [P, P])
        raw = tmp("raw", [P, 4, B])
        mag = tmp("mag", [P, 4, B])
        sel0 = tmp("sel0", [2 * E, EP, 2, I])
        ps = [own.enter_context(nc.psum_tensor(f"p_ps{i}", [P, 512], F32)) for i in range(8)]
        s = sems("p", ["x", "small", "wqkv", "gate", "up", "downw", "l1", "const", "id0", "cs", "ct_ps", "ct",
                       "mod_ps", "mod", "sgn", "raw", "gates", "stk0", "stk", "stkhi", "stklo", "tr", "hi", "lo", "fr",
                       "ssq", "ss", "sn", "snm", "sr", "slot_n", "sel0", "selm", "sel", "gt", "sh_hi", "sh_lo", "sh_ps", "diag", "wot_ps", "wot", "wob_ps", "wob", "split", "gb_ps", "gb"], own)
        x = T["x"]
        rounds = [(k, r) for k in range(3) for r in range(EP // 4)]

        with nc.Block() as block:
            @block.sync
            def _(sp):
                sp.dma_start(c[:, 0, :], A["L0_c"]).then_inc(s["small"], 16)
                sp.dma_start(c[:, 1, :], A["L1_c"]).then_inc(s["small"], 16)
                sp.dma_start(wmod[:, 0, :], A["L0_wmod"]).then_inc(s["small"], 16)
                sp.dma_start(wmod[:, 1, :], A["L1_wmod"]).then_inc(s["small"], 16)
                sp.dma_start(x[:, :, :], A["L0_attn_q"].rearrange("b (t p) d -> p (b t) d", p=P)).then_inc(s["x"], 16)
                sp.dma_start(eg[:, :, :], A["L0_ffn_expert_gate"].rearrange("(p e) i d -> (e i) p d", e=2)).then_inc(s["gate"], 16)
                sp.dma_start(eu[:, :, :], A["L0_ffn_expert_up"].rearrange("(p e) i d -> (e i) p d", e=2)).then_inc(s["up"], 16)
                sp.dma_start(ed[:, :, :], A["L0_ffn_expert_down"].rearrange("e d i -> d e i")).then_inc(s["downw"], 16)
                sp.wait_ge(s["x"], 16)

            @block.gpsimd
            def _(pool):
                nc.gpsimd.memset(T["ident"][:, :], 0.0).then_inc(s["id0"], 1)
                nc.gpsimd.memset(T["ones"][:, :], 1.0).then_inc(s["const"], 1)
                nc.gpsimd.memset(T["neg_half"][:, :], -0.5).then_inc(s["const"], 1)
                nc.gpsimd.memset(T["half"][:, :], 0.5).then_inc(s["const"], 1)
                nc.gpsimd.memset(T["eps"][:, :], LN_EPS).then_inc(s["const"], 1)
                pool.wait_ge(s["id0"], 1)
                nc.gpsimd.affine_select(out=T["ident"][:, :], in_=T["ident"][:, :], compare_op=ALU.not_equal, fill=1.0,
                                        base=0, pattern=[[-1, P]], channel_multiplier=1).then_inc(s["const"], 1)
                nc.gpsimd.memset(sel0[:, :, :, :], 0.0).then_inc(s["sel0"], 1)
                pool.wait_ge(s["sel0"], 1)
                nc.gpsimd.affine_select(out=sel0[:, :, :, :], in_=sel0[:, :, :, :], compare_op=ALU.not_equal, fill=1.0,
                                        base=0, pattern=[[-2, EP], [-1, 2], [0, I]], channel_multiplier=1).then_inc(s["sel0"], 1)
                pool.wait_ge(s["sel0"], 2)
                nc.gpsimd.affine_select(out=sel0[:, :, :, :], in_=sel0[:, :, :, :], compare_op=ALU.not_equal, fill=1.0,
                                        base=-E, pattern=[[-2, EP], [-1, 2], [0, I]], channel_multiplier=1).then_inc(s["selm"], 1)
                nc.gpsimd.memset(T["wqs"][:, :, :, :, :], 0.0).then_inc(s["stk0"], 1)
                nc.gpsimd.memset(T["wks"][:, :, :, :, :], 0.0).then_inc(s["stk0"], 1)
                pool.wait_ge(s["mod"], 3)
                for site in range(4):
                    nc.gpsimd.tensor_tensor(T["diag"][:, site, :, :], T["ident"][:, :].unsqueeze(1).to_broadcast([P, B, P]),
                                            T["mod"][:, site, 2, :].unsqueeze(2).to_broadcast([P, B, P]), ALU.mult).then_inc(s["diag"], 1)
                pool.wait_ge(s["ss"], 1)
                nc.gpsimd.tensor_tensor(sn[:, :], ss[:, :], T["half"][:, 0:SC], ALU.pow).then_inc(s["sn"], 1)

            @block.scalar
            def _(act):
                act.dma_start(T["rows"][:, :], A["rows"]).then_inc(s["wqkv"], 16)
                act.dma_start(T["wq"][:, :, :], A["L0_attn_W_query"].rearrange("h d k -> d h k")).then_inc(s["wqkv"], 16)
                act.dma_start(T["wk"][:, :, :], A["L0_attn_W_key"].rearrange("h d k -> d h k")).then_inc(s["wqkv"], 16)
                act.dma_start(T["wv"][:, :, :], A["L0_attn_W_val"].rearrange("h d k -> d h k")).then_inc(s["wqkv"], 16)
                act.dma_start(T["wo"][:, :], A["L0_attn_W_out"].rearrange("h k e -> (h k) e")).then_inc(s["wqkv"], 16)
                for dst, src in [(gw, A["L0_ffn_gate_w"]), (shg, A["L0_ffn_shared_gate_w"]),
                                 (shu, A["L0_ffn_shared_up_w"]), (shd, A["L0_ffn_shared_down_w"]),
                                 (T["wqkv"], A["L1_attn_Wqkv"]), (T["wln"], A["L1_attn_Wln"]), (w1, A["L1_ffn_w1"])]:
                    act.dma_start(dst[:, :], src).then_inc(s["l1"], 16)
                act.dma_start(T["bqkv"][:, :], A["L1_attn_bqkv"].rearrange("(a n) -> a n", a=1)).then_inc(s["l1"], 16)
                act.dma_start(T["bv"][:, :], A["L1_attn_bqkv"][2 * D:3 * D].rearrange("(n a) -> n a", a=1)).then_inc(s["l1"], 16)
                act.dma_start(T["bln"][:, :], A["L1_attn_bln"].rearrange("(n a) -> n a", a=1)).then_inc(s["l1"], 16)
                act.dma_start(T["gx"][:, :], A["L1_ffn_gamma_x"].rearrange("(n a) -> n a", a=1)).then_inc(s["l1"], 16)
                act.dma_start(T["gs"][:, :], A["L1_ffn_gamma_slot"].rearrange("(n a) -> n a", a=1)).then_inc(s["l1"], 16)
                act.dma_start(T["w2"][:, :, :], A["L1_ffn_w2"].rearrange("(j p) d -> p j d", p=P)).then_inc(s["l1"], 16)
                act.dma_start(slot[:, :, :], A["L1_ffn_slot_embeds"].rearrange("e t d -> (e t) d")
                              .rearrange("(c p) d -> p c d", p=P)).then_inc(s["l1"], 16)
                act.wait_ge(s["small"], 64)
                nc.scalar.activation(cs[:, :, :], c[:, :, :], ACT.Silu).then_inc(s["cs"], 1)
                for n, (k, r) in enumerate(rounds):
                    act.wait_ge(s["tr"], n + 1)
                    if k < 2:
                        nc.scalar.activation(T["gu_hi"][:, k, 4 * r:4 * r + 4, :], ps[n % 4][:, :], ACT.Copy).then_inc(s["hi"], 1)
                    else:
                        nc.scalar.activation(T["down"][:, 4 * r:4 * r + 4, :], ps[n % 4][:, :], ACT.Copy).then_inc(s["fr"], 1)
                act.wait_ge(s["sh_ps"], 1)
                nc.scalar.activation(T["sh_hi"][:, :, :], ps[6][:, 0:2 * I], ACT.Copy).then_inc(s["sh_hi"], 1)
                nc.scalar.activation(T["sh_down"][:, :], ps[6][0:I, 2 * I:2 * I + P], ACT.Copy).then_inc(s["gt"], 1)
                nc.scalar.activation(T["gate_t"][:, :], ps[6][:, 2 * I + P:2 * I + P + E], ACT.Copy).then_inc(s["gt"], 1)
                act.wait_ge(s["wot_ps"], 1)
                nc.scalar.activation(wot[:, :], ps[0][:, 0:P], ACT.Copy).then_inc(s["wot"], 1)
                for k in range(2):
                    act.wait_ge(s["wob_ps"], k + 1)
                    nc.scalar.activation(T["wo_b"][:, 4 * k:4 * k + 4, :], ps[1 + k][:, :], ACT.Copy).then_inc(s["wob"], 1)
                act.wait_ge(s["l1"], 14 * 16)

            @block.vector
            def _(dve):
                dve.wait_ge(s["wqkv"], 5 * 16)
                dve.wait_ge(s["stk0"], 2)
                for w, st in ((T["wq"], T["wqs"]), (T["wk"], T["wks"])):
                    for k in range(3):
                        nc.vector.tensor_copy(st[:, :, :, k, :], w[:, :, :].rearrange("p (g i) k -> p g i k", i=HB)).then_inc(s["stk"], 1)
                dve.wait_ge(s["stk"], 6)
                for j, st in enumerate((T["wqs"], T["wks"])):
                    nc.vector.tensor_copy(T["wqk_hi"][:, j, :, :], st.rearrange("p g i c k -> p g (i c k)")).then_inc(s["stkhi"], 1)
                dve.wait_ge(s["stkhi"], 2)
                for j, st in enumerate((T["wqs"], T["wks"])):
                    nc.vector.tensor_tensor(T["wqk_lo"][:, j, :, :], st.rearrange("p g i c k -> p g (i c k)"),
                                            T["wqk_hi"][:, j, :, :].bitcast(F32), ALU.subtract).then_inc(s["stklo"], 1)
                dve.wait_ge(s["ct_ps"], 1)
                nc.vector.tensor_copy(ct[:, :, :], ps[4][:, 0:2 * B]).then_inc(s["ct"], 1)
                dve.wait_ge(s["mod_ps"], 1)
                mod_ps = ps[5][:, 0:12 * B].rearrange("p (a k b) -> p a k b", a=4, k=3)
                nc.vector.tensor_copy(T["mod"][:, :, 0, :], mod_ps[:, :, 0, :]).then_inc(s["mod"], 1)
                nc.vector.tensor_scalar(T["mod"][:, :, 1, :], mod_ps[:, :, 1, :], 1.0, None, ALU.add).then_inc(s["mod"], 1)
                nc.vector.tensor_scalar(sgn[:, :, :], mod_ps[:, :, 2, :], 0.0, 2.0, ALU.is_ge, ALU.mult).then_inc(s["sgn"], 1)
                nc.vector.tensor_copy(raw[:, :, :], mod_ps[:, :, 2, :]).then_inc(s["raw"], 1)
                dve.wait_ge(s["raw"], 1)
                nc.vector.scalar_tensor_tensor(mag[:, :, :], raw[:, :, :], -1.0, raw[:, :, :], ALU.mult, ALU.max).then_inc(s["raw"], 1)
                dve.wait_ge(s["raw"], 2)
                nc.vector.tensor_scalar(mag[:, :, :], mag[:, :, :], 0.25, None, ALU.max).then_inc(s["sgn"], 1)
                dve.wait_ge(s["sgn"], 2)
                nc.vector.scalar_tensor_tensor(T["mod"][:, :, 2, :], sgn[:, :, :], -1.0, mag[:, :, :], ALU.add, ALU.mult).then_inc(s["mod"], 1)
                dve.wait_ge(s["const"], 5)
                nc.vector.tensor_copy(T["ones_r"][:, :], T["ones"][:, :]).then_inc(s["const"], 1)
                dve.wait_ge(s["selm"], 1)
                nc.vector.tensor_copy(T["sel"][:, :, :], sel0[:, :, :, :].rearrange("p a j i -> p a (j i)")).then_inc(s["sel"], 1)
                for n, (k, r) in enumerate(rounds):
                    if k < 2:
                        dve.wait_ge(s["hi"], n + 1)
                        nc.vector.tensor_tensor(T["gu_lo"][:, k, 4 * r:4 * r + 4, :].rearrange("p a b -> p (a b)"), ps[n % 4][:, :],
                                                T["gu_hi"][:, k, 4 * r:4 * r + 4, :].bitcast(F32).rearrange("p a b -> p (a b)"),
                                                ALU.subtract).then_inc(s["lo"], 1)
                dve.wait_ge(s["sh_hi"], 1)
                dve.wait_ge(s["gt"], 2)
                nc.vector.tensor_tensor(T["sh_lo"][:, :, :].rearrange("p a b -> p (a b)"), ps[6][:, 0:2 * I],
                                        T["sh_hi"][:, :, :].bitcast(F32).rearrange("p a b -> p (a b)"), ALU.subtract).then_inc(s["sh_lo"], 1)
                dve.wait_ge(s["l1"], 14 * 16)
                nc.vector.tensor_tensor(slot_sq[:, :, :], slot[:, :, :], slot[:, :, :], ALU.mult).then_inc(s["ssq"], 1)
                dve.wait_ge(s["ssq"], 1)
                nc.vector.tensor_reduce(ss[:, :], slot_sq[:, :, :], AX.X, ALU.add).then_inc(s["ss"], 1)
                dve.wait_ge(s["sn"], 1)
                nc.vector.tensor_scalar(sn[:, :], sn[:, :], 1e-12, float(D) ** -0.5, ALU.max, ALU.mult).then_inc(s["snm"], 1)
                dve.wait_ge(s["snm"], 1)
                nc.vector.reciprocal(sr[:, :], sn[:, :]).then_inc(s["sr"], 1)
                dve.wait_ge(s["sr"], 1)
                nc.vector.tensor_tensor(slot_n[:, :, :], slot[:, :, :], sr[:, :].unsqueeze(2).to_broadcast([P, SC, D]),
                                        ALU.mult).then_inc(s["slot_n"], 1)
                dve.wait_ge(s["sh_ps"], 2)
                nc.vector.tensor_scalar(se_t[:, :], ps[7][:, :], T["gs"][:, 0:1], None, ALU.mult).then_inc(s["slot_n"], 1)
                nc.vector.tensor_copy(T["w1_hi"][:, :], w1[:, :]).then_inc(s["split"], 1)
                dve.wait_ge(s["slot_n"], 2)
                nc.vector.tensor_copy(T["se_hi"][:, :], se_t[:, :]).then_inc(s["split"], 1)
                dve.wait_ge(s["split"], 2)
                for whole, hi, lo in ((w1, T["w1_hi"], T["w1_lo"]), (se_t, T["se_hi"], T["se_lo"])):
                    nc.vector.tensor_tensor(lo[:, :], whole[:, :], hi[:, :].bitcast(F32), ALU.subtract).then_inc(s["split"], 1)
                for k in range(2):
                    dve.wait_ge(s["gb_ps"], k + 1)
                    nc.vector.tensor_copy(T["gb"][:, 4 * k:4 * k + 4, :], ps[3 + k][:, :]).then_inc(s["gb"], 1)

            @block.tensor
            def _(pe):
                pe.wait_ge(s["const"], 5)
                pe.wait_ge(s["cs"], 1)
                for l in range(2):
                    last = nc.tensor.transpose(ps[4][:, l * B:(l + 1) * B], cs[:, l, :], T["ident"][0:B, 0:B])
                last.then_inc(s["ct_ps"], 1)
                pe.wait_ge(s["ct"], 1)
                for l in range(2):
                    for k in range(6):
                        last = nc.tensor.matmul(ps[5][:, (l * 6 + k) * B:(l * 6 + k + 1) * B], wmod[:, l, k * D:(k + 1) * D],
                                                ct[:, l, :], start=True, stop=True)
                last.then_inc(s["mod_ps"], 1)
                for n, (k, r) in enumerate(rounds):
                    if r == 0:
                        pe.wait_ge(s[("gate", "up", "downw")[k]], 16)
                    if n >= 4:
                        if n - 4 < 8:
                            pe.wait_ge(s["lo"], n - 3)
                        else:
                            pe.wait_ge(s["fr"], n - 11)
                    for q in range(4):
                        p = 4 * r + q
                        src = (eg[:, p, :], eu[:, p, :], ed[:, 2 * p:2 * p + 2, :].rearrange("d e i -> d (e i)"))[k]
                        last = nc.tensor.transpose(ps[n % 4][:, q * P:(q + 1) * P], src, T["ident"][:, :])
                    last.then_inc(s["tr"], 1)
                pe.wait_ge(s["l1"], 14 * 16)
                nc.tensor.transpose(ps[6][:, 0:I], shg[:, :], T["ident"][0:I, 0:I])
                nc.tensor.transpose(ps[6][:, I:2 * I], shu[:, :], T["ident"][0:I, 0:I])
                nc.tensor.transpose(ps[6][0:I, 2 * I:2 * I + P], shd[:, :], T["ident"][:, :])
                nc.tensor.transpose(ps[6][:, 2 * I + P:2 * I + P + E], gw[:, :], T["ident"][0:E, 0:E]).then_inc(s["sh_ps"], 1)
                pe.wait_ge(s["slot_n"], 1)
                for k in range(SC):
                    last = nc.tensor.transpose(ps[7][:, k * P:(k + 1) * P], slot_n[:, k, :], T["ident"][:, :])
                last.then_inc(s["sh_ps"], 1)
                pe.wait_ge(s["wqkv"], 5 * 16)
                pe.wait_ge(s["fr"], 4)
                nc.tensor.transpose(ps[0][:, 0:P], T["wo"][:, :], T["ident"][:, :]).then_inc(s["wot_ps"], 1)
                pe.wait_ge(s["wot"], 1)
                pe.wait_ge(s["diag"], 1)
                for k in range(2):
                    nc.tensor.matmul(ps[1 + k][:, :], wot[:, :], T["diag"][:, L0A, 4 * k:4 * k + 4, :].rearrange("p b n -> p (b n)"),
                                     start=True, stop=True).then_inc(s["wob_ps"], 1)
                pe.wait_ge(s["diag"], 4)
                for k in range(2):
                    nc.tensor.matmul(ps[3 + k][:, :], T["ones"][:, :], T["diag"][:, L1F, 4 * k:4 * k + 4, :].rearrange("p b n -> p (b n)"),
                                     start=True, stop=True).then_inc(s["gb_ps"], 1)


def need(eng, sem, n):
    if not isinstance(n, int) or n > 0:
        eng.wait_ge(sem, n)


def attention(nc, T, sems):
    with ExitStack() as own:
        def tmp(name, shape, dt=F32):
            return own.enter_context(nc.sbuf_tensor("a_" + name, shape, dt))

        stats = tmp("stats", [P, TB, 6])
        mv = tmp("mv", [P, TB, 2])
        veps = tmp("veps", [P, 8])
        rstd = tmp("rstd", [P, 8])
        h0 = tmp("h0", [P, TB, D])
        ht = tmp("ht", [P, S])
        ht_hi = tmp("ht_hi", [P, S], F32R)
        ht_lo = tmp("ht_lo", [P, S], F32R)
        hs = tmp("hs", [P, 2, 2, S])
        qs = tmp("qs", [P, HG, S], F32R)
        ks = [tmp(f"ks{i}", [P, HG, S], F32R) for i in range(2)]
        qblk = [tmp(f"qblk{i}", [P, HG, HB, S], F32R) for i in range(2)]
        vaug = [tmp(f"vaug{i}", [P, TB, H, STACK]) for i in range(2)]
        mx = tmp("mx", [P, TB, HG, HB])
        nm = tmp("nm", [P, TB, HG, HB, 2])
        mt = [tmp(f"mt{i}", [2 * HB, 2, S]) for i in range(2)]
        pt = tmp("pt", [P, 2, TB, HB, S])
        us = tmp("us", [P, HG, S])
        rec = tmp("rec", [P, TB, H])
        o = tmp("o", [P, TB, H, DK])
        ots = tmp("ots", [P, S])
        ring = [own.enter_context(nc.psum_tensor(f"a_ring{i}", [P, 2, S], F32)) for i in range(2)]
        st = [own.enter_context(nc.psum_tensor(f"a_st{i}", [P, 2, S], F32)) for i in range(2)]
        u = own.enter_context(nc.psum_tensor("a_u", [P, HG, S], F32))
        ma = own.enter_context(nc.psum_tensor("a_ma", [P, 512], F32))
        mb = own.enter_context(nc.psum_tensor("a_mb", [P, 512], F32))
        s = sems("a", ["n_" + n for n in NORM_SEMS] +
                 ["ht_ps", "ht", "ht_hi", "ht_lo", "v_ps", "v", "qk_ps", "qk_hs", "qs", "ks", "ring_free", "qblk",
                  "s_ps", "nm_hi", "nm", "mt_ps", "mt", "mblk0", "mblk1", "st_ps", "pt", "pv", "us", "ut_ps", "rec", "o",
                  "ot_ps", "ots", "xo", "x1", "zero", "vinit"], own)
        FILLS = 4 + 16
        STEPS = [(g, t, ip) for g in range(HG) for t in range(TB) for ip in range(2)]

        def windows(eng, window):
            for b in (0, 1):
                window(b, b % 2)
            with eng.Fori(0, (B - 4) // 2) as turn:
                window(2 * turn + 2, 0, True)
                window(2 * turn + 3, 1, True)
            for b in range(B - 2, B + 2):
                window(b, b % 2)

        def parts(b, inner):
            if inner:
                return True, True, True, True
            return b < B, 1 <= b <= B, 2 <= b, b + 1 < B

        with nc.Block() as block:
            @block.gpsimd
            def _(pool):
                for i in range(2):
                    nc.gpsimd.memset(qblk[i][:, :, :, :].bitcast(F32), 0.0).then_inc(s["zero"], 1)
                    nc.gpsimd.memset(vaug[i][:, :, :, :], 0.0).then_inc(s["vinit"], 1)
                    pool.wait_ge(s["vinit"], i + 1)
                    nc.gpsimd.memset(vaug[i][:, :, :, DK:DK + 1], 1.0).then_inc(s["zero"], 1)
                with pool.Fori(0, B) as b:
                    norm_pool_rstd(nc, pool, s, "n", mv, veps, rstd, T["eps"], T["neg_half"], b)
                    pool.wait_ge(s["ht_hi"], b + 1)
                    nc.gpsimd.tensor_tensor(ht_lo[:, :], ht[:, :], ht_hi[:, :].bitcast(F32), ALU.subtract).then_inc(s["ht_lo"], 1)

            @block.sync
            def _(sp):
                def maxima(b, half, par):
                    sp.wait_ge(s["mt"], 2 * b + half + 1)
                    for i in range(HB):
                        r = i * STACK + M_ROW
                        sp.dma_start(qblk[par][r:r + 2, 2 * half:2 * half + 2, i, :].bitcast(F32),
                                     mt[half][2 * i:2 * i + 2, :, :]).then_inc(s[f"mblk{half}"], 16)

                def window(b, par, inner=False):
                    front, back, tail, nxt = parts(b, inner)
                    if front:
                        sp.wait_ge(s["qs"], 2 * b + 2)
                        for i in range(HB):
                            r = slice(i * STACK, (i + 1) * STACK)
                            sp.dma_start(qblk[par][r, :, i, :].bitcast(F32), qs[r, :, :].bitcast(F32)).then_inc(s["qblk"], 16)
                    if back:
                        maxima(b - 1, 1, 1 - par)
                    if front:
                        maxima(b, 0, par)

                sp.wait_ge(s["zero"], 4)
                windows(sp, window)

            @block.vector
            def _(dve):
                def tiles(b):
                    if isinstance(b, int):
                        return [T["x"][:, TB * b + t, :] for t in range(TB)]
                    return [T["x"][:, bass.ds(TB * b + t, 1), :].rearrange("p a d -> p (a d)") for t in range(TB)]

                def stack(b, k, par):
                    dve.wait_ge(s["qk_hs"], 4 * b + k + 1)
                    j, dst, name = (0, qs, "qs") if k < 2 else (1, ks[par], "ks")
                    g = 2 * (k % 2)
                    if k == 0:
                        need(dve, s["qblk"], 16 * HB * b)
                    nc.vector.scalar_tensor_tensor(dst[:, g:g + 2, :].rearrange("p a n -> p (a n)"),
                                                   ring[k % 2][:, :, :].rearrange("p a n -> p (a n)"), T["rows"][:, 2 * j:2 * j + 1],
                                                   hs[:, k % 2, :, :].rearrange("p a n -> p (a n)"), ALU.mult, ALU.add).then_inc(s[name], 1)

                def output(b, t):
                    dve.wait_ge(s["ut_ps"], TB * b + t + 1)
                    ut = mb[:, :].rearrange("p (h k) -> p h k", k=STACK)
                    nc.vector.reciprocal(rec[:, t, :], ut[:, :, DK]).then_inc(s["rec"], 1)
                    dve.wait_ge(s["rec"], TB * b + t + 1)
                    nc.vector.tensor_tensor(o[:, t, :, :], ut[:, :, 0:DK], rec[:, t, :].unsqueeze(2).to_broadcast([P, H, DK]),
                                            ALU.mult).then_inc(s["o"], 1)

                def negate(b, half):
                    dve.wait_ge(s["ring_free"], FILLS * b + 12 + 8 * half)
                    need(dve, s["mt_ps"], 2 * b + half - 1)
                    g = slice(2 * half, 2 * half + 2)
                    m, hi, lo = (a.rearrange("p t g i -> p t (g i)") for a in
                                 (mx[:, :, g, :], nm[:, :, g, :, 0], nm[:, :, g, :, 1]))
                    nc.vector.tensor_scalar(hi.bitcast(F32R), m, -1.0, None, ALU.mult).then_inc(s["nm_hi"], 1)
                    dve.wait_ge(s["nm_hi"], 2 * b + half + 1)
                    nc.vector.scalar_tensor_tensor(lo.bitcast(F32R), m, -1.0, hi, ALU.mult, ALU.subtract).then_inc(s["nm"], 1)

                def window(b, par, inner=False):
                    front, back, tail, nxt = parts(b, inner)
                    if isinstance(b, int) and b == 0:
                        norm_vector_stats(nc, dve, s, "n", tiles(0), stats, mv, 0)
                        norm_vector_apply(nc, dve, s, "n", tiles(0), mv, rstd, h0, 0)
                    for k in range(4):
                        if front:
                            stack(b, k, par)
                            dve.wait_ge(s[("qs", "qs", "ks", "ks")[k]], 2 * b + k % 2 + 1)
                            dve.sem_inc(s["ring_free"], 1)
                        if front and k == 1:
                            values(b, par)
                        if tail and k == 3:
                            output(b - 2, 0)
                    if nxt:
                        norm_vector_stats(nc, dve, s, "n", tiles(b + 1), stats, mv, b + 1)
                    if tail:
                        output(b - 2, 1)
                    for k, (g, t, ip) in enumerate(STEPS):
                        if front:
                            dve.wait_ge(s["s_ps"], 16 * b + k + 1)
                            nc.vector.tensor_reduce(mx[:, t, g, 2 * ip:2 * ip + 2], ring[k % 2][:, :, :], AX.X, ALU.max).then_inc(s["ring_free"], 1)
                            if k == 7:
                                negate(b, 0)
                            if k == 15:
                                negate(b, 1)
                        if tail and k == 1:
                            dve.wait_ge(s["xo"], b - 1)
                            x2 = T["x"][:, TB * (b - 2):TB * (b - 1), :] if isinstance(b, int) else T["x"][:, bass.ds(TB * b - 2 * TB, TB), :]
                            x2 = x2.rearrange("p a d -> p (a d)")
                            nc.vector.tensor_tensor(x2, x2, mb[:, 0:S], ALU.add).then_inc(s["x1"], 1)
                        if nxt and k == 3:
                            norm_vector_apply(nc, dve, s, "n", tiles(b + 1), mv, rstd, h0, b + 1)

                def values(b, par):
                    dve.wait_ge(s["v_ps"], b + 1)
                    need(dve, s["pv"], HG * (b - 1))
                    for t in range(TB):
                        nc.vector.tensor_copy(vaug[par][:, t, :, 0:DK], ma[:, S + t * P:S + (t + 1) * P].rearrange("p (h k) -> p h k", k=DK)).then_inc(s["v"], 1)

                windows(dve, window)

            @block.scalar
            def _(act):
                def modulated(b):
                    at = (lambda c: T["mod"][:, L0A, c, b:b + 1]) if isinstance(b, int) else (lambda c: T["mod"][:, L0A, c, bass.ds(b, 1)])
                    act.wait_ge(s["ht_ps"], b + 1)
                    need(act, s["qk_ps"], 4 * b)
                    nc.scalar.activation(ht[:, :], ma[:, 0:S], ACT.Identity, scale=at(1), bias=at(0)).then_inc(s["ht"], 1)
                    act.wait_ge(s["ht"], b + 1)
                    nc.scalar.activation(ht_hi[:, :], ht[:, :], ACT.Copy).then_inc(s["ht_hi"], 1)

                def rounded(b, k):
                    act.wait_ge(s["qk_ps"], 4 * b + k + 1)
                    j = k // 2
                    bias = T["rows"][:, 4:5] if j else 0.0
                    nc.scalar.activation(hs[:, k % 2, :, :].bitcast(F32R), ring[k % 2][:, :, :], ACT.Identity, bias=bias,
                                         scale=T["rows"][:, 2 * j + 1:2 * j + 2]).then_inc(s["qk_hs"], 1)

                def maxima(b, half):
                    act.wait_ge(s["mt_ps"], 2 * b + half + 1)
                    need(act, s[f"mblk{half}"], 16 * HB * b)
                    nc.scalar.activation(mt[half][:, :, :].bitcast(F32R), ma[0:2 * HB, :].rearrange("p (g n) -> p g n", g=2), ACT.Copy).then_inc(s["mt"], 1)

                def exponentials(b, k):
                    g, nt, ip = STEPS[k]
                    act.wait_ge(s["st_ps"], 16 * b + k + 1)
                    if k % 4 == 0:
                        need(act, s["pv"], HG * b + g - 1)
                    nc.scalar.activation(pt[:, g % 2, nt, 2 * ip:2 * ip + 2, :], st[k % 2][:, :, :], ACT.Exp,
                                         scale=ATTN_SCALE).then_inc(s["pt"], 1)

                def products(b, half):
                    act.wait_ge(s["pv"], HG * b + 2 * half + 2)
                    if half == 0:
                        need(act, s["ut_ps"], TB * b)
                    nc.scalar.activation(us[:, 2 * half:2 * half + 2, :], u[:, 2 * half:2 * half + 2, :], ACT.Copy).then_inc(s["us"], 1)

                def window(b, par, inner=False):
                    front, back, tail, nxt = parts(b, inner)
                    if isinstance(b, int) and b == 0:
                        modulated(0)
                    if front:
                        rounded(b, 0)
                    if tail:
                        products(b - 2, 1)
                    for k in range(16):
                        if front and 1 <= k <= 3:
                            rounded(b, k)
                        if back and k == 4:
                            maxima(b - 1, 1)
                        if back:
                            exponentials(b - 1, k)
                        if tail and k == 7:
                            act.wait_ge(s["ot_ps"], b - 1)
                            need(act, s["xo"], b - 2)
                            nc.scalar.activation(ots[:, :], mb[:, 0:S], ACT.Copy).then_inc(s["ots"], 1)
                        if front and k == 12:
                            maxima(b, 0)
                        if back and k == 13:
                            products(b - 1, 0)
                        if nxt and k == 13:
                            modulated(b + 1)

                windows(act, window)

            @block.tensor
            def _(pe):
                def transposed(b):
                    pe.wait_ge(s["n_h0"], TB * (b + 1))
                    need(pe, s["mt"], 2 * b - 1)
                    for t in range(TB):
                        last = nc.tensor.transpose(ma[:, t * P:(t + 1) * P], h0[:, t, :], T["ident"][:, :])
                    last.then_inc(s["ht_ps"], 1)

                def values(b):
                    pe.wait_ge(s["ht"], b + 1)
                    for t in range(TB):
                        last = nc.tensor.matmul(ma[:, S + t * P:S + (t + 1) * P], ht[:, t * P:(t + 1) * P],
                                                T["wv"][:, :, :].rearrange("p h k -> p (h k)"), start=True, stop=True)
                    last.then_inc(s["v_ps"], 1)

                def project(b, k):
                    if k == 0:
                        pe.wait_ge(s["ht_lo"], b + 1)
                    need(pe, s["ring_free"], FILLS * b + k - 1)
                    j = k // 2
                    for a in range(2):
                        g = 2 * (k % 2) + a
                        dst = ring[k % 2][:, a, :]
                        nc.tensor.matmul(dst, T["wqk_hi"][:, j, g, :], ht_hi[:, :], start=True, stop=False)
                        nc.tensor.matmul(dst, T["wqk_hi"][:, j, g, :], ht_lo[:, :], start=False, stop=False)
                        last = nc.tensor.matmul(dst, T["wqk_lo"][:, j, g, :], ht_hi[:, :], start=False, stop=True)
                    last.then_inc(s["qk_ps"], 1)

                def scores(b, k, par):
                    g, qt, ip = STEPS[k]
                    if k == 0:
                        pe.wait_ge(s["ks"], 2 * b + 2)
                        pe.wait_ge(s["qblk"], 16 * HB * (b + 1))
                    pe.wait_ge(s["ring_free"], FILLS * b + 3 + k)
                    for a in range(2):
                        last = nc.tensor.matmul(ring[k % 2][:, a, :], qblk[par][:, g, 2 * ip + a, qt * P:(qt + 1) * P],
                                                ks[par][:, g, :], start=True, stop=True)
                    last.then_inc(s["s_ps"], 1)

                def maxima(b, half, nxt):
                    pe.wait_ge(s["nm"], 2 * b + half + 1)
                    if half == 0:
                        need(pe, s["mt"], 2 * b)
                    elif nxt:
                        pe.wait_ge(s["v"], TB * (b + 2))
                    for g in range(2):
                        for t in range(TB):
                            last = nc.tensor.transpose(ma[0:2 * HB, g * S + t * P:g * S + (t + 1) * P],
                                                       nm[:, t, 2 * half + g, :, :].rearrange("p i l -> p (i l)"), T["ident"][:, :])
                    last.then_inc(s["mt_ps"], 1)

                def shifted(b, k, par):
                    g, nt, ip = STEPS[k]
                    if k % 8 == 0:
                        pe.wait_ge(s[f"mblk{k // 8}"], 16 * HB * (b + 1))
                    need(pe, s["pt"], 16 * b + k - 1)
                    nc.tensor.matmul(st[k % 2][:, :, :].rearrange("p a n -> p (a n)"), ks[par][:, g, nt * P:(nt + 1) * P],
                                     qblk[par][:, g, 2 * ip:2 * ip + 2, :].rearrange("p a n -> p (a n)"),
                                     start=True, stop=True).then_inc(s["st_ps"], 1)

                def products(b, g, par):
                    pe.wait_ge(s["pt"], 16 * b + 4 * (g + 1))
                    if g == 0:
                        need(pe, s["us"], 2 * b)
                    for nt in range(TB):
                        for i in range(HB):
                            last = nc.tensor.matmul(u[i * STACK:(i + 1) * STACK, g, :], vaug[par][:, nt, HB * g + i, :],
                                                    pt[:, g % 2, nt, i, :], start=(nt == 0), stop=(nt == TB - 1),
                                                    skip_group_check=True)
                    last.then_inc(s["pv"], 1)

                def heads(b, t):
                    if t == 0:
                        pe.wait_ge(s["us"], 2 * (b + 1))
                        need(pe, s["x1"], b)
                    else:
                        pe.wait_ge(s["o"], TB * b + t)
                    for g in range(HG):
                        last = nc.tensor.transpose(mb[:, g * P:(g + 1) * P], us[:, g, t * P:(t + 1) * P], T["ident"][:, :])
                    last.then_inc(s["ut_ps"], 1)

                def outputs_transposed(b):
                    pe.wait_ge(s["o"], TB * (b + 1))
                    for t in range(TB):
                        last = nc.tensor.transpose(mb[:, t * P:(t + 1) * P], o[:, t, :, :].rearrange("p h k -> p (h k)"), T["ident"][:, :])
                    last.then_inc(s["ot_ps"], 1)

                def project_out(b):
                    pe.wait_ge(s["ots"], b + 1)
                    w = T["wo_b"][:, b, :] if isinstance(b, int) else T["wo_b"][:, bass.ds(b, 1), :].rearrange("p a e -> p (a e)")
                    for t in range(TB):
                        last = nc.tensor.matmul(mb[:, t * P:(t + 1) * P], ots[:, t * P:(t + 1) * P], w, start=True, stop=True)
                    last.then_inc(s["xo"], 1)

                def window(b, par, inner=False):
                    front, back, tail, nxt = parts(b, inner)
                    if isinstance(b, int) and b == 0:
                        transposed(0)
                        values(0)
                    if front:
                        project(b, 0)
                    if tail:
                        products(b - 2, HG - 1, par)
                    for k in range(8):
                        if front and 1 <= k <= 3:
                            project(b, k)
                        if back:
                            shifted(b - 1, k, 1 - par)
                        if back and k == 3:
                            maxima(b - 1, 1, front)
                        if tail and k == 3:
                            heads(b - 2, 0)
                        if back and k == 5:
                            products(b - 1, 0, 1 - par)
                        if tail and k == 5:
                            heads(b - 2, 1)
                        if tail and k == 7:
                            outputs_transposed(b - 2)
                    for k in range(16):
                        if front:
                            scores(b, k, par)
                        if tail and k == 1:
                            project_out(b - 2)
                        if back and k % 2 == 1:
                            shifted(b - 1, 8 + k // 2, 1 - par)
                        if back and k == 3:
                            products(b - 1, 1, 1 - par)
                        if front and k == 9:
                            maxima(b, 0, nxt)
                        if back and k == 11:
                            products(b - 1, 2, 1 - par)
                        if nxt and k == 11:
                            transposed(b + 1)
                        if nxt and k == 13:
                            values(b + 1)

                pe.wait_ge(s["zero"], 4)
                windows(pe, window)


def experts(nc, T, sems):
    with ExitStack() as own:
        def tmp(name, shape, dt=F32):
            return own.enter_context(nc.sbuf_tensor("e_" + name, shape, dt))

        h2_hi = tmp("h2_hi", [P, B * S], F32R)
        h2_lo = tmp("h2_lo", [P, B * S], F32R)
        ct_r = tmp("ct_r", [2 * E, B * S], F32R)
        score = tmp("score", [P, TILES, E])
        expert_inputs(nc, T, sems, h2_hi, h2_lo, score)
        routing(nc, T, sems, score, ct_r)
        expert_products(nc, T, sems, h2_hi, h2_lo, ct_r)


def expert_inputs(nc, T, sems, h2_hi, h2_lo, score):
    with ExitStack() as own:
        def tmp(name, shape, dt=F32):
            return own.enter_context(nc.sbuf_tensor("i_" + name, shape, dt))

        stats = tmp("stats", [P, TB, 6])
        mv = tmp("mv", [P, TB, 2])
        veps = tmp("veps", [P, 8])
        rstd = tmp("rstd", [P, 8])
        h0 = tmp("h0", [P, TB, D])
        ht = tmp("ht", [P, S])
        hp = own.enter_context(nc.psum_tensor("i_hp", [P, 512], F32))
        lg = own.enter_context(nc.psum_tensor("i_lg", [P, 512], F32))
        s = sems("i", ["n_" + n for n in NORM_SEMS] + ["ht_ps", "ht", "hi", "lo", "lg", "score"], own)
        with nc.Block() as block:
            @block.gpsimd
            def _(pool):
                with pool.Fori(0, B) as b:
                    norm_pool_rstd(nc, pool, s, "n", mv, veps, rstd, T["eps"], T["neg_half"], b)

            @block.vector
            def _(dve):
                with dve.Fori(0, B) as b:
                    xt = [T["x"][:, bass.ds(TB * b + t, 1), :].rearrange("p a d -> p (a d)") for t in range(TB)]
                    norm_vector_stats(nc, dve, s, "n", xt, stats, mv, b)
                    dve.wait_ge(s["ht_ps"], b)
                    norm_vector_apply(nc, dve, s, "n", xt, mv, rstd, h0, b)
                    dve.wait_ge(s["hi"], b + 1)
                    nc.vector.tensor_tensor(h2_lo[:, bass.ds(S * b, S)], ht[:, :], h2_hi[:, bass.ds(S * b, S)].bitcast(F32),
                                            ALU.subtract).then_inc(s["lo"], 1)

            @block.scalar
            def _(act):
                with act.Fori(0, B) as b:
                    act.wait_ge(s["ht_ps"], b + 1)
                    act.wait_ge(s["lo"], b)
                    nc.scalar.activation(ht[:, :], hp[:, 0:S], ACT.Identity, scale=T["mod"][:, L0F, 1, bass.ds(b, 1)],
                                         bias=T["mod"][:, L0F, 0, bass.ds(b, 1)]).then_inc(s["ht"], 1)
                    act.wait_ge(s["ht"], b + 1)
                    nc.scalar.activation(h2_hi[:, bass.ds(S * b, S)], ht[:, :], ACT.Copy).then_inc(s["hi"], 1)
                    act.wait_ge(s["lg"], b + 1)
                    nc.scalar.activation(score[:, bass.ds(TB * b, TB), :].rearrange("p a e -> p (a e)"), lg[:, 0:TB * E],
                                         ACT.Sigmoid).then_inc(s["score"], 1)

            @block.tensor
            def _(pe):
                with pe.Fori(0, B) as b:
                    pe.wait_ge(s["n_h0"], TB * (b + 1))
                    pe.wait_ge(s["ht"], b)
                    for t in range(TB):
                        last = nc.tensor.transpose(hp[:, t * P:(t + 1) * P], h0[:, t, :], T["ident"][:, :])
                    last.then_inc(s["ht_ps"], 1)
                    pe.wait_ge(s["ht"], b + 1)
                    pe.wait_ge(s["score"], b)
                    for t in range(TB):
                        last = nc.tensor.matmul(lg[:, t * E:(t + 1) * E], ht[:, t * P:(t + 1) * P], T["gate_t"][:, :],
                                                start=True, stop=True)
                    last.then_inc(s["lg"], 1)


def routing(nc, T, sems, score, ct_r):
    with ExitStack() as own:
        def tmp(name, shape, dt=F32):
            return own.enter_context(nc.sbuf_tensor("r_" + name, shape, dt))

        gsum = tmp("gsum", [P, TILES, GROUPS + TOPG])
        best = tmp("best", [P, TILES, GROUPS])
        seek = tmp("seek", [P, TILES, GROUPS])
        left = tmp("left", [P, TILES, GROUPS + TOPG])
        gmask = tmp("gmask", [P, TILES, GROUPS])
        masked = tmp("masked", [P, TILES, E])
        top = tmp("top", [P, TILES, TOPK])
        rest = tmp("rest", [P, TILES, E])
        w = tmp("w", [P, TILES, E])
        total = tmp("total", [P, TILES])
        inv = tmp("inv", [P, TILES])
        cw = tmp("cw", [P, TILES, E])
        c2 = tmp("c2", [P, TILES, 2, E])
        ps = [own.enter_context(nc.psum_tensor(f"r_ps{i}", [P, 512], F32)) for i in range(4)]
        s = sems("r", ["fill", "gsum", "best", "seek", "left", "gmask", "masked", "top", "rest", "w", "total", "tmax", "inv",
                       "cw", "c_hi", "c_lo", "ps", "ct"], own)
        with nc.Block() as block:
            @block.vector
            def _(dve):
                nc.vector.memset(gsum[:, :, GROUPS:], -5.0).then_inc(s["fill"], 1)
                nc.vector.memset(seek[:, :, TOPG:], -5.0).then_inc(s["fill"], 1)
                nc.vector.tensor_reduce(gsum[:, :, 0:GROUPS], score[:, :, :].rearrange("p t (g k) -> p t g k", k=EPG),
                                        AX.X, ALU.add).then_inc(s["gsum"], 1)
                dve.wait_ge(s["gsum"], 1)
                for t in range(TILES):
                    nc.vector.max(best[:, t, :], gsum[:, t, 0:GROUPS]).then_inc(s["best"], 1)
                dve.wait_ge(s["best"], TILES)
                nc.vector.tensor_copy(seek[:, :, 0:TOPG], best[:, :, 0:TOPG]).then_inc(s["seek"], 1)
                dve.wait_ge(s["seek"], 1)
                dve.wait_ge(s["fill"], 2)
                for t in range(TILES):
                    nc.vector.match_replace(left[:, t, :], seek[:, t, :], gsum[:, t, :], -1.0).then_inc(s["left"], 1)
                dve.wait_ge(s["left"], TILES)
                nc.vector.tensor_scalar(gmask[:, :, :], left[:, :, 0:GROUPS], 0.0, None, ALU.is_lt).then_inc(s["gmask"], 1)
                dve.wait_ge(s["gmask"], 1)
                nc.vector.tensor_tensor(masked[:, :, :].rearrange("p t (g k) -> p (t g) k", k=EPG),
                                        score[:, :, :].rearrange("p t (g k) -> p (t g) k", k=EPG),
                                        gmask[:, :, :].rearrange("p t g -> p (t g)").unsqueeze(2).to_broadcast([P, TILES * GROUPS, EPG]),
                                        ALU.mult).then_inc(s["masked"], 1)
                dve.wait_ge(s["masked"], 1)
                for t in range(TILES):
                    nc.vector.max(top[:, t, :], masked[:, t, :]).then_inc(s["top"], 1)
                dve.wait_ge(s["top"], TILES)
                for t in range(TILES):
                    nc.vector.match_replace(rest[:, t, :], top[:, t, :], masked[:, t, :], -1.0).then_inc(s["rest"], 1)
                dve.wait_ge(s["rest"], TILES)
                nc.vector.scalar_tensor_tensor(w[:, :, :].rearrange("p t e -> p (t e)"), rest[:, :, :].rearrange("p t e -> p (t e)"), 0.0,
                                               masked[:, :, :].rearrange("p t e -> p (t e)"), ALU.is_lt, ALU.mult).then_inc(s["w"], 1)
                dve.wait_ge(s["w"], 1)
                nc.vector.tensor_reduce(total[:, :], w[:, :, :], AX.X, ALU.add).then_inc(s["total"], 1)
                dve.wait_ge(s["total"], 1)
                nc.vector.tensor_scalar(total[:, :], total[:, :], 1e-12, None, ALU.max).then_inc(s["tmax"], 1)
                dve.wait_ge(s["tmax"], 1)
                nc.vector.reciprocal(inv[:, :], total[:, :]).then_inc(s["inv"], 1)
                dve.wait_ge(s["inv"], 1)
                nc.vector.tensor_tensor(cw[:, :, :], w[:, :, :], inv[:, :].unsqueeze(2).to_broadcast([P, TILES, E]),
                                        ALU.mult).then_inc(s["cw"], 1)
                dve.wait_ge(s["cw"], 1)
                nc.vector.tensor_copy(c2[:, :, 0, :].bitcast(F32R), cw[:, :, :]).then_inc(s["c_hi"], 1)
                dve.wait_ge(s["c_hi"], 1)
                nc.vector.tensor_tensor(c2[:, :, 1, :].bitcast(F32R), cw[:, :, :], c2[:, :, 0, :], ALU.subtract).then_inc(s["c_lo"], 1)

            @block.tensor
            def _(pe):
                pe.wait_ge(s["c_lo"], 1)
                for t in range(TILES):
                    last = nc.tensor.transpose(ps[t // 4][0:2 * E, t % 4 * P:(t % 4 + 1) * P],
                                               c2[:, t, :, :].rearrange("p l e -> p (l e)"), T["ident"][:, :])
                    if t % 4 == 3:
                        last.then_inc(s["ps"], 1)

            @block.scalar
            def _(act):
                for r in range(4):
                    act.wait_ge(s["ps"], r + 1)
                    nc.scalar.activation(ct_r[:, r * 512:(r + 1) * 512], ps[r][0:2 * E, :], ACT.Copy).then_inc(s["ct"], 1)


def expert_products(nc, T, sems, h2_hi, h2_lo, ct_r):
    with ExitStack() as own:
        def tmp(name, shape, dt=F32):
            return own.enter_context(nc.sbuf_tensor("x_" + name, shape, dt))

        NP = EP + 1
        sg = tmp("sg", [P, 2, N2])
        su = tmp("su", [P, 2, N2])
        act_w = tmp("act_w", [P, 2, N2])
        yts = tmp("yts", [P, N2])
        diag = tmp("diag", [P, SB, P])
        g_ps = [own.enter_context(nc.psum_tensor(f"x_g{i}", [P, N2], F32)) for i in range(2)]
        u_ps = [own.enter_context(nc.psum_tensor(f"x_u{i}", [P, N2], F32)) for i in range(2)]
        w_ps = [own.enter_context(nc.psum_tensor(f"x_w{i}", [P, N2], F32)) for i in range(2)]
        y_ps = own.enter_context(nc.psum_tensor("x_y", [P, N2], F32))
        o_ps = own.enter_context(nc.psum_tensor("x_o", [P, N2], F32))
        s = sems("x", ["g", "u", "silu", "su", "act", "down", "y", "yts", "diag", "o", "res"], own)
        last_of_slot = lambda p: 1 if p == 0 else 2

        with nc.Block() as block:
            @block.tensor
            def _(pe):
                with pe.Fori(0, B // SB) as q:
                    f0 = NP * q
                    cols = bass.ds(N2 * q, N2)

                    def project(p):
                        m = P if p < EP else I
                        w_hi = [T["gu_hi"][:, j, p, :] if p < EP else T["sh_hi"][:, j, :] for j in range(2)]
                        w_lo = [T["gu_lo"][:, j, p, :] if p < EP else T["sh_lo"][:, j, :] for j in range(2)]
                        if p < 2:
                            pe.wait_ge(s["act"], f0)
                        for j, dst in enumerate((g_ps[p % 2], u_ps[p % 2])):
                            nc.tensor.matmul(dst[0:m, :], w_hi[j], h2_hi[:, cols], start=True, stop=False)
                            nc.tensor.matmul(dst[0:m, :], w_hi[j], h2_lo[:, cols], start=False, stop=False)
                            nc.tensor.matmul(dst[0:m, :], w_lo[j], h2_hi[:, cols], start=False, stop=True).then_inc(s[("g", "u")[j]], 1)
                        if p < EP:
                            nc.tensor.matmul(w_ps[p % 2][:, :], T["sel"][:, p, :], ct_r[:, cols], start=True, stop=True).then_inc(s["u"], 1)

                    project(0)
                    for p in range(NP):
                        if p + 1 < NP:
                            project(p + 1)
                        pe.wait_ge(s["act"], f0 + p + 1)
                        if p == 0:
                            pe.wait_ge(s["yts"], q)
                        if p < EP:
                            nc.tensor.matmul(y_ps[:, :], T["down"][:, p, :], act_w[:, p % 2, :], start=(p == 0),
                                             stop=False).then_inc(s["down"], 1)
                        else:
                            nc.tensor.matmul(y_ps[:, :], T["sh_down"][:, :], act_w[0:I, p % 2, :], start=False,
                                             stop=True).then_inc(s["down"], 1)
                    pe.wait_ge(s["yts"], q + 1)
                    pe.wait_ge(s["diag"], SB * (q + 1))
                    pe.wait_ge(s["res"], q)
                    for t in range(TB * SB):
                        last = nc.tensor.matmul(o_ps[:, t * P:(t + 1) * P], yts[:, t * P:(t + 1) * P], diag[:, t // TB, :],
                                                start=True, stop=True)
                    last.then_inc(s["o"], 1)

            @block.scalar
            def _(act):
                with act.Fori(0, B // SB) as q:
                    f0 = NP * q
                    for p in range(NP):
                        m = P if p < EP else I
                        act.wait_ge(s["g"], f0 + p + 1)
                        if p >= 2:
                            act.wait_ge(s["su"], f0 + p - 1)
                        else:
                            act.wait_ge(s["su"], f0)
                        nc.scalar.activation(sg[0:m, p % 2, :], g_ps[p % 2][0:m, :], ACT.Silu).then_inc(s["silu"], 1)
                    act.wait_ge(s["down"], NP * (q + 1))
                    act.wait_ge(s["o"], q)
                    nc.scalar.activation(yts[:, :], y_ps[:, :], ACT.Copy).then_inc(s["yts"], 1)

            @block.vector
            def _(dve):
                with dve.Fori(0, B // SB) as q:
                    f0 = NP * q
                    dve.wait_ge(s["o"], q)
                    for k in range(SB):
                        nc.vector.tensor_scalar(diag[:, k, :], T["ident"][:, :], T["mod"][:, L0F, 2, bass.ds(SB * q + k, 1)], None,
                                                ALU.mult).then_inc(s["diag"], 1)
                    for p in range(NP):
                        dve.wait_ge(s["silu"], f0 + p + 1)
                        dve.wait_ge(s["u"], (2 * EP + 1) * q + (2 * p + 2 if p < EP else 2 * EP + 1))
                        if p < EP:
                            nc.vector.tensor_tensor(su[:, p % 2, :], sg[:, p % 2, :], u_ps[p % 2][:, :], ALU.mult).then_inc(s["su"], 1)
                            dve.wait_ge(s["su"], f0 + p + 1)
                            if p >= 2:
                                dve.wait_ge(s["down"], f0 + p - 1)
                            else:
                                dve.wait_ge(s["down"], f0)
                            nc.vector.tensor_tensor(act_w[:, p % 2, :], su[:, p % 2, :], w_ps[p % 2][:, :], ALU.mult).then_inc(s["act"], 1)
                        else:
                            dve.wait_ge(s["down"], f0 + p - 1)
                            nc.vector.tensor_tensor(act_w[0:I, p % 2, :], sg[0:I, p % 2, :], u_ps[p % 2][0:I, :], ALU.mult).then_inc(s["act"], 1)
                            dve.wait_ge(s["act"], f0 + p + 1)
                            dve.sem_inc(s["su"], 1)
                    dve.wait_ge(s["o"], q + 1)
                    xq = T["x"][:, bass.ds(TB * SB * q, TB * SB), :].rearrange("p a d -> p (a d)")
                    nc.vector.tensor_tensor(xq, xq, o_ps[:, :], ALU.add).then_inc(s["res"], 1)


def linear_attention(nc, T, sems):
    with ExitStack() as own:
        def tmp(name, shape, dt=F32):
            return own.enter_context(nc.sbuf_tensor("l_" + name, shape, dt))

        NT = TB * SB
        stats = tmp("stats", [P, NT, 6])
        mv = tmp("mv", [P, NT, 2])
        veps = tmp("veps", [P, 8])
        rstd = tmp("rstd", [P, 8])
        h0 = tmp("h0", [P, NT, D])
        ht = tmp("ht", [P, N2])
        qk_stats = tmp("qk_stats", [P, 2 * NT, 6])
        qk_mv = tmp("qk_mv", [P, NT, 2, 2])
        den = tmp("den", [P, NT, 2])
        r1 = tmp("r1", [P, NT, 2])
        cen = tmp("cen", [P, 2 * NT, D])
        sq = tmp("sq", [P, NT, 2, D])
        q4 = tmp("q4", [P, NT, D])
        q4s = tmp("q4s", [P, NT])
        r1q = tmp("r1q", [P, NT])
        n2 = tmp("n2", [P, NT])
        nq = tmp("nq", [P, NT])
        rq = tmp("rq", [P, NT])
        q2n = tmp("q2n", [P, NT, D])
        k2 = tmp("k2", [P, NT, D])
        k4 = tmp("k4", [P, NT, D])
        v = tmp("v", [P, NT, D])
        q2t = tmp("q2t", [P, N2])
        kn = tmp("kn", [P, SB])
        knr = tmp("knr", [P, SB])
        rk = tmp("rk", [P, SB])
        kvs = tmp("kvs", [P, SB, D])
        zts = tmp("zts", [P, N2])
        yts = tmp("yts", [P, N2])
        diag = tmp("diag", [P, SB, P])
        ht_ps = own.enter_context(nc.psum_tensor("l_ht_ps", [P, 512], F32))
        qk_ps = own.enter_context(nc.psum_tensor("l_qk", [P, NT, 2 * D], F32))
        v_ps = own.enter_context(nc.psum_tensor("l_v_ps", [P, NT, D], F32))
        kv_ps = own.enter_context(nc.psum_tensor("l_kv", [P, 512], F32))
        qt_ps = own.enter_context(nc.psum_tensor("l_qt", [P, 512], F32))
        z_ps = own.enter_context(nc.psum_tensor("l_z", [P, 512], F32))
        y_ps = own.enter_context(nc.psum_tensor("l_y", [P, 512], F32))
        s = sems("l", ["n_" + n for n in NORM_SEMS] +
                 ["ht_ps", "ht", "qk", "v_ps", "v", "qk_stats", "qk_mv", "den", "r1", "cen", "sq", "q4", "q4s", "r1q", "n2", "nq",
                  "nqm", "rq", "rq2", "q2n", "k2", "k4", "kv", "kn", "knr", "knm", "rk", "kvs", "qt", "q2t", "z", "zts", "y", "yts",
                  "diag", "o", "res"], own)
        with nc.Block() as block:
            @block.gpsimd
            def _(pool):
                with pool.Fori(0, B // SB) as q:
                    norm_pool_rstd(nc, pool, s, "n", mv, veps, rstd, T["eps"], T["neg_half"], q)
                    pool.wait_ge(s["n2"], q + 1)
                    nc.gpsimd.tensor_tensor(nq[:, :], n2[:, :], T["half"][:, 0:NT], ALU.pow).then_inc(s["nq"], 1)
                    pool.wait_ge(s["kn"], q + 1)
                    nc.gpsimd.tensor_tensor(knr[:, :], kn[:, :], T["half"][:, 0:SB], ALU.pow).then_inc(s["knr"], 1)

            @block.vector
            def _(dve):
                with dve.Fori(0, B // SB) as q:
                    xt = [T["x"][:, bass.ds(NT * q + t, 1), :].rearrange("p a d -> p (a d)") for t in range(NT)]
                    norm_vector_stats(nc, dve, s, "n", xt, stats, mv, q)
                    norm_vector_apply(nc, dve, s, "n", xt, mv, rstd, h0, q)
                    for k in range(SB):
                        nc.vector.tensor_scalar(diag[:, k, :], T["ident"][:, :], T["mod"][:, L1A, 2, bass.ds(SB * q + k, 1)], None,
                                                ALU.mult).then_inc(s["diag"], 1)
                    dve.wait_ge(s["qk"], q + 1)
                    for t in range(NT):
                        for j in range(2):
                            nc.vector.bn_stats(qk_stats[:, 2 * t + j, :], qk_ps[:, t, j * D:(j + 1) * D]).then_inc(s["qk_stats"], 1)
                    nc.vector.drain()
                    for t in range(NT):
                        for j in range(2):
                            nc.vector.bn_aggr(qk_mv[:, t, j, :], qk_stats[:, 2 * t + j, :]).then_inc(s["qk_mv"], 1)
                    dve.wait_ge(s["qk_mv"], 2 * NT * (q + 1))
                    nc.vector.tensor_tensor(cen[:, :, :], qk_ps[:, :, :].rearrange("p t (j d) -> p (t j) d", j=2),
                                            qk_mv[:, :, :, 0].rearrange("p t j -> p (t j)").unsqueeze(2).to_broadcast([P, 2 * NT, D]),
                                            ALU.subtract).then_inc(s["cen"], 1)
                    nc.vector.tensor_scalar(den[:, :, :], qk_mv[:, :, :, 1], float(D), 1e-7, ALU.mult, ALU.add).then_inc(s["den"], 1)
                    dve.wait_ge(s["den"], q + 1)
                    nc.vector.reciprocal(r1[:, :, :], den[:, :, :]).then_inc(s["r1"], 1)
                    dve.wait_ge(s["r1"], q + 1)
                    nc.vector.tensor_tensor(r1q[:, :], r1[:, :, 0], r1[:, :, 0], ALU.mult).then_inc(s["r1q"], 1)
                    dve.wait_ge(s["sq"], q + 1)
                    nc.vector.tensor_tensor(k2[:, :, :], sq[:, :, 1, :], r1[:, :, 1].unsqueeze(2).to_broadcast([P, NT, D]),
                                            ALU.mult).then_inc(s["k2"], 1)
                    nc.vector.tensor_tensor(q4[:, :, :], sq[:, :, 0, :], sq[:, :, 0, :], ALU.mult).then_inc(s["q4"], 1)
                    dve.wait_ge(s["q4"], q + 1)
                    nc.vector.tensor_reduce(q4s[:, :], q4[:, :, :], AX.X, ALU.add).then_inc(s["q4s"], 1)
                    dve.wait_ge(s["q4s"], q + 1)
                    dve.wait_ge(s["r1q"], q + 1)
                    nc.vector.tensor_tensor(n2[:, :], q4s[:, :], r1q[:, :], ALU.mult).then_inc(s["n2"], 1)
                    dve.wait_ge(s["nq"], q + 1)
                    nc.vector.tensor_scalar(nq[:, :], nq[:, :], 1e-12, None, ALU.max).then_inc(s["nqm"], 1)
                    dve.wait_ge(s["nqm"], q + 1)
                    nc.vector.reciprocal(rq[:, :], nq[:, :]).then_inc(s["rq"], 1)
                    dve.wait_ge(s["rq"], q + 1)
                    nc.vector.tensor_tensor(rq[:, :], rq[:, :], r1[:, :, 0], ALU.mult).then_inc(s["rq2"], 1)
                    dve.wait_ge(s["rq2"], q + 1)
                    nc.vector.tensor_tensor(q2n[:, :, :], sq[:, :, 0, :], rq[:, :].unsqueeze(2).to_broadcast([P, NT, D]),
                                            ALU.mult).then_inc(s["q2n"], 1)
                    dve.wait_ge(s["kv"], q + 1)
                    nc.vector.tensor_copy(kn[:, :], kv_ps[:, SB * D:SB * D + SB]).then_inc(s["kn"], 1)
                    dve.wait_ge(s["knr"], q + 1)
                    nc.vector.tensor_scalar(knr[:, :], knr[:, :], 1e-12, float(S) ** 0.5, ALU.max, ALU.mult).then_inc(s["knm"], 1)
                    dve.wait_ge(s["knm"], q + 1)
                    nc.vector.reciprocal(rk[:, :], knr[:, :]).then_inc(s["rk"], 1)
                    dve.wait_ge(s["rk"], q + 1)
                    for k in range(SB):
                        nc.vector.tensor_scalar(kvs[:, k, :], kv_ps[:, k * D:(k + 1) * D], rk[:, k:k + 1], None,
                                                ALU.mult).then_inc(s["kvs"], 1)
                    dve.wait_ge(s["o"], q + 1)
                    xq = T["x"][:, bass.ds(NT * q, NT), :].rearrange("p a d -> p (a d)")
                    nc.vector.tensor_tensor(xq, xq, ht_ps[:, :], ALU.add).then_inc(s["res"], 1)

            @block.scalar
            def _(act):
                with act.Fori(0, B // SB) as q:
                    act.wait_ge(s["ht_ps"], q + 1)
                    for k in range(SB):
                        nc.scalar.activation(ht[:, k * S:(k + 1) * S], ht_ps[:, k * S:(k + 1) * S], ACT.Identity,
                                             scale=T["mod"][:, L1A, 1, bass.ds(SB * q + k, 1)],
                                             bias=T["mod"][:, L1A, 0, bass.ds(SB * q + k, 1)]).then_inc(s["ht"], 1)
                    act.wait_ge(s["v_ps"], q + 1)
                    nc.scalar.activation(v[:, :, :], v_ps[:, :, :], ACT.Copy).then_inc(s["v"], 1)
                    act.wait_ge(s["cen"], q + 1)
                    nc.scalar.activation(sq[:, :, :, :].rearrange("p t j d -> p (t j) d"), cen[:, :, :], ACT.Square).then_inc(s["sq"], 1)
                    act.wait_ge(s["k2"], q + 1)
                    nc.scalar.activation(k4[:, :, :], k2[:, :, :], ACT.Square).then_inc(s["k4"], 1)
                    act.wait_ge(s["qt"], q + 1)
                    nc.scalar.activation(q2t[:, :], qt_ps[:, :], ACT.Copy).then_inc(s["q2t"], 1)
                    act.wait_ge(s["z"], q + 1)
                    nc.scalar.activation(zts[:, :], z_ps[:, :], ACT.Identity, bias=T["bv"][:, 0:1]).then_inc(s["zts"], 1)
                    act.wait_ge(s["y"], q + 1)
                    nc.scalar.activation(yts[:, :], y_ps[:, :], ACT.Identity, bias=T["bln"][:, 0:1]).then_inc(s["yts"], 1)

            @block.tensor
            def _(pe):
                with pe.Fori(0, B // SB) as q:
                    pe.wait_ge(s["n_h0"], NT * (q + 1))
                    for t in range(NT):
                        last = nc.tensor.transpose(ht_ps[:, t * P:(t + 1) * P], h0[:, t, :], T["ident"][:, :])
                    last.then_inc(s["ht_ps"], 1)
                    pe.wait_ge(s["ht"], SB * (q + 1))
                    for t in range(NT):
                        nc.tensor.matmul(qk_ps[:, t, :], ht[:, t * P:(t + 1) * P], T["wqkv"][:, 0:2 * D], start=True, stop=False)
                        last = nc.tensor.matmul(qk_ps[:, t, :], T["ones"][0:1, :], T["bqkv"][:, 0:2 * D], start=False, stop=True)
                    last.then_inc(s["qk"], 1)
                    for t in range(NT):
                        nc.tensor.matmul(v_ps[:, t, :], ht[:, t * P:(t + 1) * P], T["wqkv"][:, 2 * D:3 * D], start=True, stop=False)
                        last = nc.tensor.matmul(v_ps[:, t, :], T["ones"][0:1, :], T["bqkv"][:, 2 * D:3 * D], start=False, stop=True)
                    last.then_inc(s["v_ps"], 1)
                    pe.wait_ge(s["v"], q + 1)
                    pe.wait_ge(s["k4"], q + 1)
                    for k in range(SB):
                        for t in range(TB):
                            nc.tensor.matmul(kv_ps[:, k * D:(k + 1) * D], k2[:, TB * k + t, :], v[:, TB * k + t, :],
                                             start=(t == 0), stop=(t == TB - 1))
                    for k in range(SB):
                        for t in range(TB):
                            last = nc.tensor.matmul(kv_ps[:, SB * D + k:SB * D + k + 1], k4[:, TB * k + t, :], T["ones"][:, 0:1],
                                                    start=(t == 0), stop=(t == TB - 1))
                    last.then_inc(s["kv"], 1)
                    pe.wait_ge(s["q2n"], q + 1)
                    for t in range(NT):
                        last = nc.tensor.transpose(qt_ps[:, t * P:(t + 1) * P], q2n[:, t, :], T["ident"][:, :])
                    last.then_inc(s["qt"], 1)
                    pe.wait_ge(s["kvs"], SB * (q + 1))
                    pe.wait_ge(s["q2t"], q + 1)
                    for k in range(SB):
                        z = z_ps[:, k * S:(k + 1) * S]
                        nc.tensor.matmul(z, T["wqkv"][:, 2 * D:3 * D], ht[:, k * S:(k + 1) * S], start=True, stop=False)
                        last = nc.tensor.matmul(z, kvs[:, k, :], q2t[:, k * S:(k + 1) * S], start=False, stop=True)
                    last.then_inc(s["z"], 1)
                    pe.wait_ge(s["zts"], q + 1)
                    nc.tensor.matmul(y_ps[:, :], T["wln"][:, :], zts[:, :], start=True, stop=True).then_inc(s["y"], 1)
                    pe.wait_ge(s["yts"], q + 1)
                    pe.wait_ge(s["diag"], SB * (q + 1))
                    for t in range(NT):
                        last = nc.tensor.matmul(ht_ps[:, t * P:(t + 1) * P], yts[:, t * P:(t + 1) * P], diag[:, t // TB, :],
                                                start=True, stop=True)
                    last.then_inc(s["o"], 1)


def slots(nc, T, sems):
    with ExitStack() as own:
        def tmp(name, shape, dt=F32):
            return own.enter_context(nc.sbuf_tensor("s_" + name, shape, dt))

        stats = tmp("stats", [P, TB, 6])
        mv = tmp("mv", [P, TB, 2])
        veps = tmp("veps", [P, 8])
        rstd = tmp("rstd", [P, 8])
        h0 = tmp("h0", [P, TB, D])
        ht = tmp("ht", [P, S])
        hsq = tmp("hsq", [P, S])
        gdiag = tmp("gdiag", [P, P])
        ssum = tmp("ssum", [P, TB])
        norm = tmp("norm", [P, TB])
        rnorm = tmp("rnorm", [P, TB])
        xn = tmp("xn", [P, TB, D + 1])
        xnt_hi = tmp("xnt_hi", [P, S], F32R)
        xnt_lo = tmp("xnt_lo", [P, S], F32R)
        m_slot = tmp("m_slot", [P, SC])
        m_tok = tmp("m_tok", [P, TB])
        d_slot = tmp("d_slot", [P, SC, P], F32R)
        d_tok = tmp("d_tok", [P, TB, P], F32R)
        disp = tmp("disp", [P, TB, SLOTS])
        comb = [tmp(f"comb{i}", [P, SC, S]) for i in range(2)]
        rz = tmp("rz", [P, SC])
        sl = tmp("sl", [P, SC, D])
        slt_hi = tmp("slt_hi", [P, SLOTS], F32R)
        slt_lo = tmp("slt_lo", [P, SLOTS], F32R)
        hid = tmp("hid", [P, HC, SLOTS])
        proc = tmp("proc", [P, SC, D + 1])
        ru = tmp("ru", [P, TB])
        yo = tmp("yo", [P, TB, D])
        pa = own.enter_context(nc.psum_tensor("s_a", [P, TB, SLOTS], F32))
        pb = own.enter_context(nc.psum_tensor("s_b", [P, SC, S], F32))
        ma = own.enter_context(nc.psum_tensor("s_ma", [P, 512], F32))
        pc = own.enter_context(nc.psum_tensor("s_c", [P, 2, 512], F32))
        mb = own.enter_context(nc.psum_tensor("s_mb", [P, 512], F32))
        s = sems("s", ["n_" + n for n in NORM_SEMS] +
                 ["one", "gdiag", "ht_ps", "ht", "hsq", "ss", "ssum", "norm", "nm", "rn", "xt_ps", "xn", "xnt_ps", "xnt_hi", "xnt_lo",
                  "la", "lb", "m_tok", "m_slot", "d", "fa", "fb", "disp", "comb", "sl_ps", "rz", "sl", "slt_ps", "slt_hi", "slt_lo",
                  "h_ps", "hid", "pr_ps", "proc", "u_ps", "ru", "yo", "res"], own)
        slot_out = lambda c, n: pc[:, c // 2, c % 2 * (D + 1):c % 2 * (D + 1) + n]

        def windows(eng, window):
            for b in (0, 1):
                window(b, b % 2)
            with eng.Fori(0, (B - 4) // 2) as turn:
                window(2 * turn + 2, 0, True)
                window(2 * turn + 3, 1, True)
            for b in range(B - 2, B + 1):
                window(b, b % 2)

        def parts(b, inner):
            return (True, True, True) if inner else (b < B, 1 <= b, b + 1 < B)

        with nc.Block() as block:
            @block.gpsimd
            def _(pool):
                nc.gpsimd.memset(xn[:, :, D:D + 1], 1.0).then_inc(s["one"], 1)
                nc.gpsimd.memset(proc[:, :, D:D + 1], 1.0).then_inc(s["one"], 1)
                norm_pool_rstd(nc, pool, s, "n", mv, veps, rstd, T["eps"], T["neg_half"], 0)

                def norms(b):
                    pool.wait_ge(s["ssum"], b + 1)
                    nc.gpsimd.tensor_tensor(norm[:, :], ssum[:, :], T["half"][:, 0:TB], ALU.pow).then_inc(s["norm"], 1)

                with pool.Fori(0, B - 1) as b:
                    norms(b)
                    norm_pool_rstd(nc, pool, s, "n", mv, veps, rstd, T["eps"], T["neg_half"], b + 1)
                norms(B - 1)

            @block.vector
            def _(dve):
                def tiles(b):
                    if isinstance(b, int):
                        return [T["x"][:, TB * b + t, :] for t in range(TB)]
                    return [T["x"][:, bass.ds(TB * b + t, 1), :].rearrange("p a d -> p (a d)") for t in range(TB)]

                def window(b, par, inner=False):
                    front, back, nxt = parts(b, inner)
                    if back:
                        dve.wait_ge(s["sl_ps"], b)
                        for k in range(SC):
                            nc.vector.reciprocal(rz[:, k:k + 1], slot_out(k, D + 1)[:, D:D + 1]).then_inc(s["rz"], 1)
                        dve.wait_ge(s["rz"], SC * b)
                        for k in range(SC):
                            nc.vector.tensor_scalar(sl[:, k, :], slot_out(k, D), rz[:, k:k + 1], None, ALU.mult).then_inc(s["sl"], 1)
                    if front:
                        dve.wait_ge(s["ss"], b + 1)
                        nc.vector.tensor_copy(ssum[:, :], ma[:, 256:256 + TB]).then_inc(s["ssum"], 1)
                        dve.wait_ge(s["norm"], b + 1)
                        nc.vector.tensor_scalar(norm[:, :], norm[:, :], 1e-12, None, ALU.max).then_inc(s["nm"], 1)
                        dve.wait_ge(s["nm"], b + 1)
                        nc.vector.reciprocal(rnorm[:, :], norm[:, :]).then_inc(s["rn"], 1)
                        dve.wait_ge(s["rn"], b + 1)
                        dve.wait_ge(s["xt_ps"], b + 1)
                        need(dve, s["sl_ps"], b)
                        nc.vector.tensor_tensor(xn[:, :, 0:D], ma[:, 0:S].rearrange("p (t d) -> p t d", t=TB),
                                                rnorm[:, :].unsqueeze(2).to_broadcast([P, TB, D]), ALU.mult).then_inc(s["xn"], 1)
                    if back:
                        dve.wait_ge(s["slt_hi"], b)
                        nc.vector.tensor_tensor(slt_lo[:, :], mb[:, :], slt_hi[:, :].bitcast(F32), ALU.subtract).then_inc(s["slt_lo"], 1)
                    if front:
                        dve.wait_ge(s["xnt_hi"], b + 1)
                        nc.vector.tensor_tensor(xnt_lo[:, :], ma[:, S:2 * S], xnt_hi[:, :].bitcast(F32), ALU.subtract).then_inc(s["xnt_lo"], 1)
                    if nxt:
                        norm_vector_stats(nc, dve, s, "n", tiles(b + 1), stats, mv, b + 1)
                    if front:
                        dve.wait_ge(s["la"], b + 1)
                        nc.vector.tensor_reduce(m_tok[:, :], pa[:, :, :], AX.X, ALU.max).then_inc(s["m_tok"], 1)
                        dve.wait_ge(s["lb"], b + 1)
                        nc.vector.tensor_reduce(m_slot[:, :], pb[:, :, :], AX.X, ALU.max).then_inc(s["m_slot"], 1)
                        dve.wait_ge(s["m_slot"], b + 1)
                        for k in range(SC):
                            nc.vector.tensor_scalar(d_slot[:, k, :], T["ident"][:, :], m_slot[:, k:k + 1], -1.0,
                                                    ALU.mult, ALU.mult).then_inc(s["d"], 1)
                        for t in range(TB):
                            nc.vector.tensor_scalar(d_tok[:, t, :], T["ident"][:, :], m_tok[:, t:t + 1], -1.0,
                                                    ALU.mult, ALU.mult).then_inc(s["d"], 1)
                    if nxt:
                        norm_vector_apply(nc, dve, s, "n", tiles(b + 1), mv, rstd, h0, b + 1)
                    if back:
                        dve.wait_ge(s["pr_ps"], b)
                        nc.vector.tensor_copy(proc[:, :, 0:D], mb[:, :].rearrange("p (c d) -> p c d", c=SC)).then_inc(s["proc"], 1)
                        dve.wait_ge(s["u_ps"], b)
                        uo = mb[:, 0:TB * (D + 1)].rearrange("p (t d) -> p t d", t=TB)
                        nc.vector.reciprocal(ru[:, :], uo[:, :, D]).then_inc(s["ru"], 1)
                        dve.wait_ge(s["ru"], b)
                        gate = T["gb"][:, b - 1, :] if isinstance(b, int) else T["gb"][:, bass.ds(b - 1, 1), :].rearrange("p a d -> p (a d)")
                        for t in range(TB):
                            nc.vector.scalar_tensor_tensor(yo[:, t, :], uo[:, t, 0:D], ru[:, t:t + 1], gate,
                                                           ALU.mult, ALU.mult).then_inc(s["yo"], 1)
                        dve.wait_ge(s["yo"], TB * b)
                        xb = T["x"][:, TB * (b - 1):TB * b, :] if isinstance(b, int) else T["x"][:, bass.ds(TB * b - TB, TB), :]
                        nc.vector.tensor_tensor(xb, xb, yo[:, :, :], ALU.add).then_inc(s["res"], 1)

                nc.vector.tensor_scalar(gdiag[:, :], T["ident"][:, :], T["gx"][:, 0:1], float(D) ** 0.5,
                                        ALU.mult, ALU.mult).then_inc(s["gdiag"], 1)
                norm_vector_stats(nc, dve, s, "n", tiles(0), stats, mv, 0)
                norm_vector_apply(nc, dve, s, "n", tiles(0), mv, rstd, h0, 0)
                windows(dve, window)

            @block.scalar
            def _(act):
                def window(b, par, inner=False):
                    front, back, nxt = parts(b, inner)
                    if front:
                        at = (lambda c: T["mod"][:, L1F, c, b:b + 1]) if isinstance(b, int) else (lambda c: T["mod"][:, L1F, c, bass.ds(b, 1)])
                        act.wait_ge(s["ht_ps"], b + 1)
                        nc.scalar.activation(ht[:, :], ma[:, 0:S], ACT.Identity, scale=at(1), bias=at(0)).then_inc(s["ht"], 1)
                        act.wait_ge(s["ht"], b + 1)
                        nc.scalar.activation(hsq[:, :], ht[:, :], ACT.Square).then_inc(s["hsq"], 1)
                    if back:
                        act.wait_ge(s["slt_ps"], b)
                        nc.scalar.activation(slt_hi[:, :], mb[:, :], ACT.Copy).then_inc(s["slt_hi"], 1)
                    if front:
                        act.wait_ge(s["xnt_ps"], b + 1)
                        nc.scalar.activation(xnt_hi[:, :], ma[:, S:2 * S], ACT.Copy).then_inc(s["xnt_hi"], 1)
                    if back:
                        for j in range(HC):
                            act.wait_ge(s["h_ps"], HC * (b - 1) + j + 1)
                            nc.scalar.activation(hid[:, j, :], pc[:, j % 2, :], ACT.Gelu).then_inc(s["hid"], 1)
                    if front:
                        act.wait_ge(s["fa"], b + 1)
                        nc.scalar.activation(disp[:, :, :], pa[:, :, :], ACT.Exp).then_inc(s["disp"], 1)
                        act.wait_ge(s["fb"], b + 1)
                        nc.scalar.activation(comb[par][:, :, :], pb[:, :, :], ACT.Exp).then_inc(s["comb"], 1)

                windows(act, window)

            @block.tensor
            def _(pe):
                def exact(dst, w, x, skip=False):
                    nc.tensor.matmul(dst, w[0], x[0], start=True, stop=False, skip_group_check=skip)
                    nc.tensor.matmul(dst, w[0], x[1], start=False, stop=False, skip_group_check=skip)
                    return nc.tensor.matmul(dst, w[1], x[0], start=False, stop=not skip, skip_group_check=skip)

                def window(b, par, inner=False):
                    front, back, nxt = parts(b, inner)
                    if front:
                        pe.wait_ge(s["n_h0"], TB * (b + 1))
                        need(pe, s["xnt_lo"], b)
                        for t in range(TB):
                            last = nc.tensor.transpose(ma[:, t * P:(t + 1) * P], h0[:, t, :], T["ident"][:, :])
                        last.then_inc(s["ht_ps"], 1)
                    if back:
                        pe.wait_ge(s["disp"], b)
                        need(pe, s["hid"], HC * (b - 1))
                        for k in range(SC):
                            for t in range(TB):
                                last = nc.tensor.matmul(slot_out(k, D + 1), disp[:, t, k * P:(k + 1) * P], xn[:, t, :],
                                                        start=(t == 0), stop=(t == TB - 1), skip_group_check=True)
                        last.then_inc(s["sl_ps"], 1)
                    if front:
                        pe.wait_ge(s["hsq"], b + 1)
                        for t in range(TB):
                            last = nc.tensor.matmul(ma[:, 256 + t:257 + t], hsq[:, t * P:(t + 1) * P], T["ones"][:, 0:1], start=True, stop=True)
                        last.then_inc(s["ss"], 1)
                        pe.wait_ge(s["ssum"], b + 1)
                        for t in range(TB):
                            last = nc.tensor.matmul(ma[:, t * P:(t + 1) * P], ht[:, t * P:(t + 1) * P], gdiag[:, :],
                                                    start=True, stop=True)
                        last.then_inc(s["xt_ps"], 1)
                    if back:
                        pe.wait_ge(s["sl"], SC * b)
                        need(pe, s["res"], b - 1)
                        for k in range(SC):
                            last = nc.tensor.transpose(mb[:, k * P:(k + 1) * P], sl[:, k, :], T["ident"][:, :])
                        last.then_inc(s["slt_ps"], 1)
                    if front:
                        pe.wait_ge(s["xn"], b + 1)
                        for t in range(TB):
                            last = nc.tensor.transpose(ma[:, S + t * P:S + (t + 1) * P], xn[:, t, 0:D], T["ident"][:, :])
                        last.then_inc(s["xnt_ps"], 1)

                    def hidden(j):
                        if j == 0:
                            pe.wait_ge(s["slt_lo"], b)
                        if j >= 2:
                            pe.wait_ge(s["hid"], HC * (b - 1) + j - 1)
                        cols = slice(j * P, (j + 1) * P)
                        exact(pc[:, j % 2, :], (T["w1_hi"][:, cols], T["w1_lo"][:, cols]), (slt_hi[:, :], slt_lo[:, :])).then_inc(s["h_ps"], 1)

                    if back:
                        hidden(0)
                        hidden(1)
                    if front:
                        pe.wait_ge(s["xnt_lo"], b + 1)
                        need(pe, s["disp"], b)
                        for t in range(TB):
                            cols = slice(t * P, (t + 1) * P)
                            last = exact(pa[:, t, :], (xnt_hi[:, cols], xnt_lo[:, cols]), (T["se_hi"][:, :], T["se_lo"][:, :]), True)
                        last.then_inc(s["la"], 1)
                    if back:
                        hidden(2)
                    if front:
                        need(pe, s["comb"], b)
                        for k in range(SC):
                            w = T["se_hi"][:, k * P:(k + 1) * P], T["se_lo"][:, k * P:(k + 1) * P]
                            nc.tensor.matmul(pb[:, k, :], w[0], xnt_hi[:, :], start=(k % 2 == 0), stop=False, skip_group_check=True)
                            nc.tensor.matmul(pb[:, k, :], w[0], xnt_lo[:, :], start=False, stop=False, skip_group_check=True)
                            last = nc.tensor.matmul(pb[:, k, :], w[1], xnt_hi[:, :], start=False, stop=False, skip_group_check=True)
                        last.then_inc(s["lb"], 1)
                    if back:
                        hidden(3)
                        pe.wait_ge(s["slt_lo"], b)
                        pe.wait_ge(s["hid"], HC * b)
                        for k in range(SC):
                            for j in range(HC):
                                last = nc.tensor.matmul(mb[:, k * P:(k + 1) * P], hid[:, j, k * P:(k + 1) * P], T["w2"][:, j, :],
                                                        start=(j == 0), stop=(j == HC - 1))
                        last.then_inc(s["pr_ps"], 1)
                    if front:
                        pe.wait_ge(s["d"], (SC + TB) * (b + 1))
                        for t in range(TB):
                            last = nc.tensor.matmul(pa[:, t, :], T["ones_r"][:, :], d_slot[:, :, :].rearrange("p c n -> p (c n)"),
                                                    start=False, stop=True, skip_group_check=True)
                        last.then_inc(s["fa"], 1)
                        for k in range(SC):
                            last = nc.tensor.matmul(pb[:, k, :], T["ones_r"][:, :], d_tok[:, :, :].rearrange("p t n -> p (t n)"),
                                                    start=False, stop=True, skip_group_check=True)
                        last.then_inc(s["fb"], 1)
                    if back:
                        pe.wait_ge(s["comb"], b)
                        pe.wait_ge(s["proc"], b)
                        for t in range(TB):
                            for k in range(SC):
                                last = nc.tensor.matmul(mb[:, t * (D + 1):(t + 1) * (D + 1)], comb[1 - par][:, k, t * P:(t + 1) * P],
                                                        proc[:, k, :], start=(k == 0), stop=(k == SC - 1))
                        last.then_inc(s["u_ps"], 1)

                pe.wait_ge(s["one"], 2)
                pe.wait_ge(s["gdiag"], 1)
                windows(pe, window)


_INS = ['L0_attn_q', 'L0_attn_W_query', 'L0_attn_W_key', 'L0_attn_W_val', 'L0_attn_W_out', 'L0_ffn_gate_w',
        'L0_ffn_expert_gate', 'L0_ffn_expert_up', 'L0_ffn_expert_down', 'L0_ffn_shared_gate_w', 'L0_ffn_shared_up_w',
        'L0_ffn_shared_down_w', 'L0_c', 'L0_wmod', 'L1_attn_Wqkv', 'L1_attn_bqkv', 'L1_attn_Wln', 'L1_attn_bln',
        'L1_ffn_gamma_x', 'L1_ffn_gamma_slot', 'L1_ffn_slot_embeds', 'L1_ffn_w1', 'L1_ffn_w2', 'L1_c', 'L1_wmod']


def kernel(**inputs):
    import numpy as _np
    import concourse.bacc as _bacc
    from concourse import mybir as _mybir
    from concourse.bass_utils import run_bass_kernel_spmd as _run

    nc = _bacc.Bacc("TRN2", target_bir_lowering=False, num_devices=1)
    arrays, aps = {}, {}
    for name in _INS:
        a = _np.ascontiguousarray(inputs[name])
        arrays[f"in_{name}_dram"] = a
        aps[name] = nc.dram_tensor(f"in_{name}_dram", a.shape, _mybir.dt.from_np(a.dtype), kind="ExternalInput").ap()
    rows = row_constants()
    arrays["rows_dram"] = rows
    aps["rows"] = nc.dram_tensor("rows_dram", rows.shape, _mybir.dt.from_np(rows.dtype), kind="ExternalInput").ap()
    out = nc.dram_tensor("out_dram", (B, S, D), F32, kind="ExternalOutput").ap()
    network(nc, aps, out)
    r = _run(nc, [arrays], core_ids=[0])
    return r.results[0]["out_dram"]
```

```python
from contextlib import ExitStack

import numpy as np
import concourse.bass as bass
from concourse import mybir

F32 = mybir.dt.float32
F32R = mybir.dt.float32r
ALU = mybir.AluOpType
ACT = mybir.ActivationFunctionType
AX = mybir.AxisListType

P = 128
B, S, D = 8, 256, 128
TB = S // P
TILES = B * TB
H, DK = 16, 8
HB = 4
HG = H // HB
STACK = P // HB
M_ROW = 3 * DK
E, I = 32, 64
EP = E // 2
TOPK, GROUPS, TOPG = 8, 8, 4
EPG = E // GROUPS
SB = 2
N2 = SB * S
SLOTS = 512
SC = SLOTS // P
HID = 512
HC = HID // P
LN_EPS = 1e-5
ATTN_SCALE = float(1.0 / np.sqrt(DK))

L0A, L0F, L1A, L1F = range(4)


def row_constants():
    part = np.arange(P) % STACK // DK
    row = np.arange(P) % STACK
    q_low = (part == 1).astype(np.float32)
    k_low = (part == 2).astype(np.float32)
    ones = ((row == M_ROW) | (row == M_ROW + 1)).astype(np.float32)
    return np.ascontiguousarray(np.stack([q_low, 1 - 2 * q_low, k_low, 1 - 2 * k_low, ones], axis=1))


def norm_vector_stats(nc, dve, s, name, x_tiles, N, n):
    for t, x in enumerate(x_tiles):
        nc.vector.bn_stats(N["stats"][:, t, :], x).then_inc(s[name + "_stats"], 1)
    nc.vector.drain()
    for t in range(len(x_tiles)):
        nc.vector.bn_aggr(N["mv"][:, t, :], N["stats"][:, t, :]).then_inc(s[name + "_mv"], 1)


def norm_pool_rstd(nc, pool, s, name, k, T, N, n):
    pool.wait_ge(s[name + "_mv"], k * n)
    nc.gpsimd.tensor_tensor(N["veps"][:, 0:k], N["mv"][:, 0:k, 1], T["eps"][:, 0:k], ALU.add).then_inc(s[name + "_veps"], 1)
    pool.wait_ge(s[name + "_veps"], n)
    nc.gpsimd.tensor_tensor(N["rstd"][:, 0:k], N["veps"][:, 0:k], T["neg_half"][:, 0:k], ALU.pow).then_inc(s[name + "_rstd"], 1)


def norm_vector_apply(nc, dve, s, name, x_tiles, N, n):
    dve.wait_ge(s[name + "_rstd"], n)
    for t, x in enumerate(x_tiles):
        nc.vector.tensor_scalar(N["h0"][:, t, :], x, N["mv"][:, t, 0:1], N["rstd"][:, t:t + 1],
                                ALU.subtract, ALU.mult).then_inc(s[name + "_h0"], 1)


NORM_SEMS = ["stats", "mv", "veps", "rstd", "h0"]


def network(nc, A, out):
    with ExitStack() as ctx:
        def sb(name, shape, dt=F32):
            return ctx.enter_context(nc.sbuf_tensor(name, shape, dt))

        def sems(prefix, names, own=ctx):
            made = {n: nc.alloc_semaphore(f"{prefix}_{n}") for n in names}
            own.callback(nc.all_engine_barrier)
            own.callback(nc.clear_and_free_semaphores, list(made.values()))
            return made

        T = {}
        T["x"] = sb("x", [P, TILES, D])
        T["ident"] = sb("ident", [P, P])
        T["ones"] = sb("ones", [P, P])
        T["ones_r"] = sb("ones_r", [P, P], F32R)
        T["mod"] = sb("mod", [P, 4, 3, B])
        T["neg_half"] = sb("neg_half", [P, 8])
        T["half"] = sb("half", [P, 8])
        T["eps"] = sb("eps", [P, 8])
        T["rows"] = sb("rows", [P, 5])
        T["wo"] = sb("wo", [P, D])
        T["gates"] = sb("gates", [P, 4, B])
        T["g_rows"] = sb("g_rows", [4 * B, D])
        T["wv"] = sb("wv", [P, H, DK])
        T["diag"] = sb("diag", [P, B, P])
        T["wo_b"] = sb("wo_b", [P, B, D])
        T["wqk_hi"] = sb("wqk_hi", [P, 2, HG, P], F32R)
        T["wqk_lo"] = sb("wqk_lo", [P, 2, HG, P], F32R)
        T["gate_t"] = sb("gate_t", [P, E])
        T["gu_hi"] = sb("gu_hi", [P, 2, EP, P], F32R)
        T["gu_lo"] = sb("gu_lo", [P, 2, EP, P], F32R)
        T["down"] = sb("down", [P, EP, P])
        T["sh_hi"] = sb("sh_hi", [P, 2, I], F32R)
        T["sh_lo"] = sb("sh_lo", [P, 2, I], F32R)
        T["sh_down"] = sb("sh_down", [I, P])
        T["sel"] = sb("sel", [2 * E, EP, P], F32R)
        T["wqkv"] = sb("wqkv", [P, 3 * D])
        T["bqkv_hi"] = sb("bqkv_hi", [1, 3 * D], F32R)
        T["bqkv_lo"] = sb("bqkv_lo", [1, 3 * D], F32R)
        T["bv"] = sb("bv", [P, 1])
        T["wln_b"] = sb("wln_b", [P, B, D])
        T["bln_hi"] = sb("bln_hi", [1, B, D], F32R)
        T["bln_lo"] = sb("bln_lo", [1, B, D], F32R)
        T["gx"] = sb("gx", [P, 1])
        T["gs"] = sb("gs", [P, 1])
        T["w1_hi"] = sb("w1_hi", [P, HID], F32R)
        T["w1_lo"] = sb("w1_lo", [P, HID], F32R)
        T["w2"] = sb("w2", [P, HC, D])
        T["se_hi"] = sb("se_hi", [P, SLOTS], F32R)
        T["se_lo"] = sb("se_lo", [P, SLOTS], F32R)
        T["gb"] = sb("gb", [P, B, D])

        loads = sems("load", ["gate", "up0", "up1", "down", "wo", "weights", "rows", "gates0", "gates1", "gates2"])
        gate_rows = nc.dram_tensor("gate_rows", (4 * B, D), F32, kind="Internal").ap()
        T["norm"] = {"stats": sb("stats", [P, TB * SB, 6]), "mv": sb("mv", [P, TB * SB, 2]), "veps": sb("veps", [P, 8]),
                     "rstd": sb("rstd", [P, 8]), "h0": sb("h0", [P, TB * SB, D])}
        prepare(nc, T, A, loads, sems)
        attention(nc, T, A, loads, gate_rows, sems)
        experts(nc, T, sems)
        linear_attention(nc, T, sems)
        slots(nc, T, out, sems)


def raw_weights(T, last=None):
    return [T["wln_b"][:, :, :], T["diag"][:, :, :], T["gb"][:, :, :], last]


def prepare(nc, T, A, loads, sems):
    with ExitStack() as own:
        def tmp(name, shape, dt=F32):
            return own.enter_context(nc.sbuf_tensor("p_" + name, shape, dt))

        c = tmp("c", [B, 2, P])
        cs = tmp("cs", [B, 2, P])
        ct = tmp("ct", [P, 2, B])
        wmod = tmp("wmod", [P, 2, 6 * D])
        wq = tmp("wq", [P, H, DK])
        wk = tmp("wk", [P, H, DK])
        wqs = tmp("wqs", [P, HG, HB, 4, DK])
        wks = tmp("wks", [P, HG, HB, 4, DK])
        sgn = tmp("sgn", [P, 4, B])
        raw = tmp("raw", [P, 4, B])
        size = tmp("size", [P, 4, B])
        mag = tmp("mag", [P, 4, B])
        gates = T["gates"]
        sel0 = tmp("sel0", [2 * E, EP, 2, I])
        ps = [own.enter_context(nc.psum_tensor(f"p_ps{i}", [P, 512], F32)) for i in range(3)]
        s = sems("p", ["x", "small", "wqkv", "const", "id0", "cs", "ct_ps", "ct", "mod_ps", "mod", "sgn", "raw", "size", "mag", "gates",
                       "stk0", "stk", "stkhi", "stklo", "sel0", "selm", "sel", "g_ps", "g_rows"] +
                 ["f_" + n for n in NORM_SEMS], own)

        with nc.Block() as block:
            @block.sync
            def _(sp):
                sp.dma_start(c[:, 0, :], A["L0_c"]).then_inc(s["small"], 16)
                sp.dma_start(c[:, 1, :], A["L1_c"]).then_inc(s["small"], 16)
                sp.dma_start(wmod[:, 0, :], A["L0_wmod"]).then_inc(s["small"], 16)
                sp.dma_start(wmod[:, 1, :], A["L1_wmod"]).then_inc(s["small"], 16)
                sp.dma_start(T["x"][:, :, :], A["L0_attn_q"].rearrange("b (t p) d -> p (b t) d", p=P)).then_inc(s["x"], 16)
                for k, (half, name) in enumerate((("gate", "gate"), ("gate", "gate"), ("up", "up0"))):
                    src = A["L0_ffn_expert_" + half].rearrange("(p e) i d -> (e i) p d", e=2)
                    sp.dma_start(raw_weights(T)[k], src[:, EP // 2 * (k % 2):EP // 2 * (k % 2 + 1), :]).then_inc(loads[name], 16)
                sp.dma_start(T["down"][:, :, :].rearrange("d p (e i) -> d (p e) i", e=2),
                             A["L0_ffn_expert_down"].rearrange("e d i -> d e i")).then_inc(loads["down"], 16)
                sp.dma_start(T["wo"][:, :], A["L0_attn_W_out"].rearrange("h k e -> (h k) e")).then_inc(loads["wo"], 16)
                sp.wait_ge(s["x"], 16)

            @block.gpsimd
            def _(pool):
                nc.gpsimd.memset(T["ident"][:, :], 0.0).then_inc(s["id0"], 1)
                nc.gpsimd.memset(T["ones"][:, :], 1.0).then_inc(s["const"], 1)
                nc.gpsimd.memset(T["neg_half"][:, :], -0.5).then_inc(s["const"], 1)
                nc.gpsimd.memset(T["half"][:, :], 0.5).then_inc(s["const"], 1)
                nc.gpsimd.memset(T["eps"][:, :], LN_EPS).then_inc(s["const"], 1)
                pool.wait_ge(s["id0"], 1)
                nc.gpsimd.affine_select(out=T["ident"][:, :], in_=T["ident"][:, :], compare_op=ALU.not_equal, fill=1.0,
                                        base=0, pattern=[[-1, P]], channel_multiplier=1).then_inc(s["const"], 1)
                nc.gpsimd.memset(wqs[:, :, :, :, :], 0.0).then_inc(s["stk0"], 1)
                nc.gpsimd.memset(wks[:, :, :, :, :], 0.0).then_inc(s["stk0"], 1)
                nc.gpsimd.memset(sel0[:, :, :, :], 0.0).then_inc(s["sel0"], 1)
                pool.wait_ge(s["sel0"], 1)
                nc.gpsimd.affine_select(out=sel0[:, :, :, :], in_=sel0[:, :, :, :], compare_op=ALU.not_equal, fill=1.0,
                                        base=0, pattern=[[-2, EP], [-1, 2], [0, I]], channel_multiplier=1).then_inc(s["sel0"], 1)
                pool.wait_ge(s["sel0"], 2)
                nc.gpsimd.affine_select(out=sel0[:, :, :, :], in_=sel0[:, :, :, :], compare_op=ALU.not_equal, fill=1.0,
                                        base=-E, pattern=[[-2, EP], [-1, 2], [0, I]], channel_multiplier=1).then_inc(s["selm"], 1)
                norm_pool_rstd(nc, pool, s, "f", TB, T, T["norm"], 1)

            @block.scalar
            def _(act):
                act.dma_start(wq[:, :, :], A["L0_attn_W_query"].rearrange("h d k -> d h k")).then_inc(s["wqkv"], 16)
                act.dma_start(wk[:, :, :], A["L0_attn_W_key"].rearrange("h d k -> d h k")).then_inc(s["wqkv"], 16)
                act.dma_start(T["wv"][:, :, :], A["L0_attn_W_val"].rearrange("h d k -> d h k")).then_inc(s["wqkv"], 16)
                act.dma_start(T["rows"][:, :], A["rows"]).then_inc(s["wqkv"], 16)
                act.wait_ge(s["small"], 64)
                nc.scalar.activation(cs[:, :, :], c[:, :, :], ACT.Silu).then_inc(s["cs"], 1)
                act.wait_ge(s["stk"], 6)
                for j, st in enumerate((wqs, wks)):
                    nc.scalar.activation(T["wqk_hi"][:, j, :, :], st.rearrange("p g i c k -> p g (i c k)"), ACT.Copy).then_inc(s["stkhi"], 1)

            @block.vector
            def _(dve):
                dve.wait_ge(s["wqkv"], 4 * 16)
                dve.wait_ge(s["stk0"], 2)
                for w, st in ((wq, wqs), (wk, wks)):
                    for k in range(3):
                        nc.vector.tensor_copy(st[:, :, :, k, :], w[:, :, :].rearrange("p (g i) k -> p g i k", i=HB)).then_inc(s["stk"], 1)
                dve.wait_ge(s["const"], 5)
                nc.vector.tensor_copy(T["ones_r"][:, :], T["ones"][:, :]).then_inc(s["const"], 1)
                dve.wait_ge(s["ct_ps"], 1)
                nc.vector.tensor_copy(ct[:, :, :], ps[0][:, 0:2 * B]).then_inc(s["ct"], 1)
                dve.wait_ge(s["stkhi"], 2)
                for j, st in enumerate((wqs, wks)):
                    nc.vector.tensor_tensor(T["wqk_lo"][:, j, :, :], st.rearrange("p g i c k -> p g (i c k)"),
                                            T["wqk_hi"][:, j, :, :].bitcast(F32), ALU.subtract).then_inc(s["stklo"], 1)
                dve.wait_ge(s["x"], 16)
                norm_vector_stats(nc, dve, s, "f", [T["x"][:, t, :] for t in range(TB)], T["norm"], 1)
                dve.wait_ge(s["selm"], 1)
                nc.vector.tensor_copy(T["sel"][:, :, :], sel0[:, :, :, :].rearrange("p a j i -> p a (j i)")).then_inc(s["sel"], 1)
                dve.wait_ge(s["mod_ps"], 1)
                mod_ps = ps[1][:, 0:12 * B].rearrange("p (a k b) -> p a k b", a=4, k=3)
                nc.vector.tensor_copy(raw[:, :, :], mod_ps[:, :, 2, :]).then_inc(s["raw"], 1)
                nc.vector.tensor_scalar(sgn[:, :, :], mod_ps[:, :, 2, :], 0.0, 2.0, ALU.is_ge, ALU.mult).then_inc(s["sgn"], 1)
                dve.wait_ge(s["raw"], 1)
                nc.vector.scalar_tensor_tensor(size[:, :, :], raw[:, :, :], -1.0, raw[:, :, :], ALU.mult, ALU.max).then_inc(s["size"], 1)
                nc.vector.tensor_copy(T["mod"][:, :, 0, :], mod_ps[:, :, 0, :]).then_inc(s["mod"], 1)
                dve.wait_ge(s["size"], 1)
                nc.vector.tensor_scalar(mag[:, :, :], size[:, :, :], 0.25, None, ALU.max).then_inc(s["mag"], 1)
                nc.vector.tensor_scalar(T["mod"][:, :, 1, :], mod_ps[:, :, 1, :], 1.0, None, ALU.add).then_inc(s["mod"], 1)
                dve.wait_ge(s["mag"], 1)
                dve.wait_ge(s["sgn"], 1)
                nc.vector.scalar_tensor_tensor(gates[:, :, :], sgn[:, :, :], -1.0, mag[:, :, :], ALU.add, ALU.mult).then_inc(s["gates"], 1)
                dve.wait_ge(s["g_ps"], 1)
                nc.vector.tensor_copy(T["g_rows"][:, :], ps[2][0:4 * B, 0:D]).then_inc(s["g_rows"], 1)
                norm_vector_apply(nc, dve, s, "f", [T["x"][:, t, :] for t in range(TB)], T["norm"], 1)

            @block.tensor
            def _(pe):
                pe.wait_ge(s["const"], 5)
                pe.wait_ge(s["cs"], 1)
                for l in range(2):
                    last = nc.tensor.transpose(ps[0][:, l * B:(l + 1) * B], cs[:, l, :], T["ident"][0:B, 0:B])
                last.then_inc(s["ct_ps"], 1)
                pe.wait_ge(s["ct"], 1)
                for l in range(2):
                    for k in range(6):
                        last = nc.tensor.matmul(ps[1][:, (l * 6 + k) * B:(l * 6 + k + 1) * B], wmod[:, l, k * D:(k + 1) * D],
                                                ct[:, l, :], start=True, stop=True)
                last.then_inc(s["mod_ps"], 1)
                pe.wait_ge(s["gates"], 1)
                nc.tensor.transpose(ps[2][0:4 * B, 0:D], gates[:, :, :].rearrange("p a b -> p (a b)"), T["ident"][:, :]).then_inc(s["g_ps"], 1)


def need(eng, sem, n):
    if not isinstance(n, int) or n > 0:
        eng.wait_ge(sem, n)


def at(i, n=1):
    return slice(i, i + n) if isinstance(i, int) else bass.ds(i, n)


def attention(nc, T, A, loads, gate_rows, sems):
    with ExitStack() as own:
        def tmp(name, shape, dt=F32):
            return own.enter_context(nc.sbuf_tensor("a_" + name, shape, dt))

        N, h0 = T["norm"], T["norm"]["h0"]
        ht = tmp("ht", [P, S])
        ht_hi = tmp("ht_hi", [P, S], F32R)
        ht_lo = tmp("ht_lo", [P, S], F32R)
        hs = tmp("hs", [P, 2, 2, S])
        qs = tmp("qs", [P, HG, S], F32R)
        ks = [tmp(f"ks{i}", [P, HG, S], F32R) for i in range(2)]
        qblk = [tmp(f"qblk{i}", [P, HG, HB, S], F32R) for i in range(2)]
        vaug = [tmp(f"vaug{i}", [P, TB, H, STACK]) for i in range(2)]
        mx = tmp("mx", [P, TB, HG, HB])
        nm = tmp("nm", [P, TB, HG, HB, 2])
        mt = [tmp(f"mt{i}", [2 * HB, 2, S]) for i in range(2)]
        pt = tmp("pt", [P, 2, TB, HB, S])
        us = tmp("us", [P, HG, S])
        rec = tmp("rec", [P, TB, H])
        o = tmp("o", [P, TB, H, DK])
        ots = tmp("ots", [P, S])
        shg = tmp("shg", [I, D])
        shu = tmp("shu", [I, D])
        shd = tmp("shd", [D, I])
        gw = tmp("gw", [E, D])
        wln = tmp("wln", [P, D])
        bln = tmp("bln", [1, D])
        bln_g = T["gb"][0:1, :, :]
        bqkv = tmp("bqkv", [1, 3 * D])
        wmean = tmp("wmean", [P, 2, 2])
        bmean = tmp("bmean", [1, 2, 2])
        slot = tmp("slot", [P, SC, D])
        w1 = tmp("w1", [P, HID])
        slot_sq = hs[:, 0, :, :].rearrange("p a n -> p (a n)").rearrange("p (c d) -> p c d", c=SC)
        se_t = slot_sq[:, :, :].rearrange("p c d -> p (c d)")
        ss = tmp("ss", [P, SC])
        sn = tmp("sn", [P, SC])
        snm = tmp("snm", [P, SC])
        sr = tmp("sr", [P, SC])
        ring = [own.enter_context(nc.psum_tensor(f"a_ring{i}", [P, 2, S], F32)) for i in range(2)]
        st = [own.enter_context(nc.psum_tensor(f"a_st{i}", [P, 2, S], F32)) for i in range(2)]
        u = own.enter_context(nc.psum_tensor("a_u", [P, HG, S], F32))
        ma = own.enter_context(nc.psum_tensor("a_ma", [P, 512], F32))
        mb = own.enter_context(nc.psum_tensor("a_mb", [P, 512], F32))
        s = sems("a", [c + "_" + n for c in "nf" for n in NORM_SEMS] +
                 ["ht_ps", "ht", "ht_hi", "ht_lo", "v_ps", "v", "qk_ps", "qk_hs", "qs", "ks", "max",
                  "qblk0", "qblk1", "s_ps", "nm_hi", "nm", "mt_ps", "mt", "mblk0", "mblk1", "st_ps", "pt", "pv", "us", "ut_ps", "rec", "o",
                  "ot_ps", "ots", "xo", "x1", "zero0", "zero1", "vinit", "vone"], own)
        later = sems("w", ["tr", "hi", "lo", "fr", "sh_ps", "sh_hi", "sh", "sh_lo", "sq", "ss", "sn", "snm", "sr", "slot_n", "slot_ps", "se_t",
                           "split", "mean0", "mean", "centred", "bhi", "wo_b", "bln_g", "bln_hi", "wln_b", "diag"], own)
        ROUNDS = [(k, r) for k in range(3) for r in range(EP // 4)]
        raw = raw_weights(T, vaug[(B - 2) % 2][:, :, :, :].rearrange("p t h k -> p (t h k)").rearrange("p (a d) -> p a d", d=D))
        RAW = [(gw, "L0_ffn_gate_w"), (shg, "L0_ffn_shared_gate_w"), (shu, "L0_ffn_shared_up_w"), (shd, "L0_ffn_shared_down_w"),
                 (T["wqkv"], "L1_attn_Wqkv"), (w1, "L1_ffn_w1")]
        STEPS = [(g, t, ip) for g in range(HG) for t in range(TB) for ip in range(2)]
        HALF = len(STEPS) // 2
        CHUNKS = HG * TB
        SHIFTS = [[], [0, 1], [], [2, 3]] + [[k] for k in range(4, 8)] + [[], [8, 9]] + [[k] for k in range(10, 16)]
        def windows(eng, window):
            for b in (0, 1):
                window(b, b % 2)
            with eng.Fori(0, (B - 4) // 2) as turn:
                window(2 * turn + 2, 0, True)
                window(2 * turn + 3, 1, True)
            for b in range(B - 2, B + 2):
                window(b, b % 2)

        def parts(b, inner):
            if inner:
                return True, True, True, True
            return b < B, 1 <= b <= B, 2 <= b, b + 1 < B

        with nc.Block() as block:
            @block.gpsimd
            def _(pool):
                def low(b):
                    pool.wait_ge(s["ht_hi"], b + 1)
                    nc.gpsimd.tensor_tensor(ht_lo[:, :], ht[:, :], ht_hi[:, :].bitcast(F32), ALU.subtract).then_inc(s["ht_lo"], 1)

                for i in range(2):
                    nc.gpsimd.memset(vaug[i][:, :, :, :], 0.0).then_inc(s["vinit"], 1)
                    pool.wait_ge(s["vinit"], i + 1)
                    nc.gpsimd.memset(vaug[i][:, :, :, DK:DK + 1], 1.0).then_inc(s["vone"], 1)
                    if i == 0:
                        low(0)
                norm_pool_rstd(nc, pool, s, "n", TB, T, N, 1)
                nc.gpsimd.memset(qblk[1][:, :, :, :].bitcast(F32), 0.0).then_inc(s["zero1"], 1)
                low(1)
                pool.wait_ge(loads["wo"], 16)
                pool.wait_ge(loads["gates0"], 16)
                nc.gpsimd.tensor_tensor(T["wo_b"][:, :, :], T["wo_b"][:, :, :], T["wo"][:, :].unsqueeze(1).to_broadcast([P, B, D]),
                                        ALU.mult).then_inc(later["wo_b"], 1)
                with pool.Fori(2, B) as b:
                    norm_pool_rstd(nc, pool, s, "n", TB, T, N, b)
                    low(b)
                pool.wait_ge(later["ss"], 1)
                nc.gpsimd.tensor_tensor(sn[:, :], ss[:, :], T["half"][:, 0:SC], ALU.pow).then_inc(later["sn"], 1)
                norm_pool_rstd(nc, pool, s, "f", TB * SB, T, N, 1)
                pool.wait_ge(later["tr"], 4)
                nc.gpsimd.tensor_tensor(T["diag"][:, :, :], T["ident"][:, :].unsqueeze(1).to_broadcast([P, B, P]),
                                        T["gates"][:, L0F, :].unsqueeze(2).to_broadcast([P, B, P]), ALU.mult).then_inc(later["diag"], 1)
                pool.wait_ge(loads["rows"], 3 * 16)
                pool.wait_ge(loads["gates1"], 16)
                pool.wait_ge(later["tr"], 6)
                nc.gpsimd.tensor_tensor(bln_g[:, :, :], T["wln_b"][0:1, :, :], bln[:, :].unsqueeze(1).to_broadcast([1, B, D]),
                                        ALU.mult).then_inc(later["bln_g"], 1)
                pool.wait_ge(later["bln_g"], 1)
                nc.gpsimd.tensor_copy(T["bln_hi"][:, :, :], bln_g[:, :, :]).then_inc(later["bln_hi"], 1)
                pool.wait_ge(later["bln_hi"], 1)
                nc.gpsimd.tensor_tensor(T["bln_lo"][:, :, :], bln_g[:, :, :], T["bln_hi"][:, :, :].bitcast(F32), ALU.subtract).then_inc(later["bln_hi"], 1)
                nc.gpsimd.tensor_tensor(T["wln_b"][:, :, :], T["wln_b"][:, :, :], wln[:, :].unsqueeze(1).to_broadcast([P, B, D]),
                                        ALU.mult).then_inc(later["wln_b"], 1)
            @block.sync
            def _(sp):
                def queries(b, half, par):
                    sp.wait_ge(s["qs"], 2 * b + half + 1)
                    for i in range(HB):
                        r = slice(i * STACK, (i + 1) * STACK)
                        g = slice(2 * half, 2 * half + 2)
                        sp.dma_start(qblk[par][r, g, i, :].bitcast(F32), qs[r, g, :].bitcast(F32)).then_inc(s[f"qblk{half}"], 16)

                def maxima(b, half, par):
                    sp.wait_ge(s["mt"], 2 * b + half + 1)
                    for i in range(HB):
                        r = i * STACK + M_ROW
                        sp.dma_start(qblk[par][r:r + 2, 2 * half:2 * half + 2, i, :].bitcast(F32),
                                     mt[half][2 * i:2 * i + 2, :, :]).then_inc(s[f"mblk{half}"], 16)

                def gates_onto(i, site, dst):
                    rows = gate_rows[B * site:B * (site + 1), :].rearrange("(a b) d -> a b d", a=1)
                    sp.dma_start(dst[:, :, :], rows.to_broadcast([P, B, D])).then_inc(loads[f"gates{i}"], 16)

                def window(b, par, inner=False):
                    front, back, tail, nxt = parts(b, inner)
                    if front:
                        queries(b, 1, par)
                    if back:
                        maxima(b - 1, 1, 1 - par)
                    if isinstance(b, int) and b == B:
                        sp.wait_ge(s["pv"], CHUNKS * (B - 1))
                        sp.dma_start(raw[3], A["L0_ffn_expert_up"].rearrange("(p e) i d -> (e i) p d", e=2)[:, EP // 2:EP, :]
                                     ).then_inc(loads["up1"], 16)
                        sp.wait_ge(later["tr"], 2)
                        gates_onto(1, L1A, T["wln_b"])
                        sp.wait_ge(later["bln_hi"], 2)
                        gates_onto(2, L1F, T["gb"])
                    if isinstance(b, int) and b == 0:
                        sp.wait_ge(s["zero1"], 1)
                    if nxt:
                        queries(b + 1, 0, 1 - par)
                    if front:
                        maxima(b, 0, par)

                sp.dma_start(gate_rows, T["g_rows"][:, :]).then_inc(loads["rows"], 16)
                for dst, name in RAW:
                    sp.dma_start(dst[:, :], A[name]).then_inc(loads["weights"], 16)
                sp.wait_ge(s["zero0"], 1)
                queries(0, 0, 0)
                sp.dma_start(wln[:, :], A["L1_attn_Wln"]).then_inc(loads["rows"], 16)
                sp.dma_start(bln[:, :], A["L1_attn_bln"].rearrange("(a n) -> a n", a=1)).then_inc(loads["rows"], 16)
                sp.wait_ge(loads["rows"], 3 * 16)
                gates_onto(0, L0A, T["wo_b"])
                sp.dma_start(T["w2"][:, :, :], A["L1_ffn_w2"].rearrange("(j p) d -> p j d", p=P)).then_inc(loads["weights"], 16)
                sp.dma_start(slot[:, :, :], A["L1_ffn_slot_embeds"].rearrange("e t d -> (e t) d")
                             .rearrange("(c p) d -> p c d", p=P)).then_inc(loads["weights"], 16)
                windows(sp, window)
                sp.wait_ge(loads["gates2"], 16)

            @block.vector
            def _(dve):
                def tiles(b):
                    return [T["x"][:, at(TB * b + t), :].rearrange("p a d -> p (a d)") for t in range(TB)]

                def stack(b, j, par):
                    half, kind = j // 2, j % 2
                    dve.wait_ge(s["qk_hs"], 4 * b + j + 1)
                    dst, name = ((qs, "qs"), (ks[par], "ks"))[kind]
                    g = 2 * half
                    if kind == 0:
                        need(dve, s[f"qblk{half}"], 16 * HB * b)
                        need(dve, s["st_ps"], 16 * (b - 2) + HALF * (half + 1))
                    nc.vector.scalar_tensor_tensor(dst[:, g:g + 2, :].rearrange("p a n -> p (a n)"),
                                                   ring[j % 2][:, :, :].rearrange("p a n -> p (a n)"), T["rows"][:, 2 * kind:2 * kind + 1],
                                                   hs[:, j % 2, :, :].rearrange("p a n -> p (a n)"), ALU.mult, ALU.add).then_inc(s[name], 1)

                def values(b, par):
                    dve.wait_ge(s["v_ps"], b + 1)
                    if isinstance(b, int) and b < 2:
                        dve.wait_ge(s["vone"], b + 1)
                    need(dve, s["pv"], CHUNKS * (b - 1))
                    for t in range(TB):
                        nc.vector.tensor_copy(vaug[par][:, t, :, 0:DK], ma[:, S + t * P:S + (t + 1) * P].rearrange("p (h k) -> p h k", k=DK)).then_inc(s["v"], 1)

                def output(b, t):
                    dve.wait_ge(s["ut_ps"], TB * b + t + 1)
                    ut = mb[:, :].rearrange("p (h k) -> p h k", k=STACK)
                    nc.vector.reciprocal(rec[:, t, :], ut[:, :, DK]).then_inc(s["rec"], 1)
                    dve.wait_ge(s["rec"], TB * b + t + 1)
                    nc.vector.tensor_tensor(o[:, t, :, :], ut[:, :, 0:DK], rec[:, t, :].unsqueeze(2).to_broadcast([P, H, DK]),
                                            ALU.mult).then_inc(s["o"], 1)

                def negate(b, half):
                    dve.wait_ge(s["max"], 16 * b + HALF * (half + 1))
                    need(dve, s["mt_ps"], 2 * b + half - 1)
                    g = slice(2 * half, 2 * half + 2)
                    m, hi, lo = (a.rearrange("p t g i -> p t (g i)") for a in
                                 (mx[:, :, g, :], nm[:, :, g, :, 0], nm[:, :, g, :, 1]))
                    nc.vector.tensor_scalar(hi.bitcast(F32R), m, -1.0, None, ALU.mult).then_inc(s["nm_hi"], 1)
                    dve.wait_ge(s["nm_hi"], 2 * b + half + 1)
                    nc.vector.scalar_tensor_tensor(lo.bitcast(F32R), m, -1.0, hi, ALU.mult, ALU.subtract).then_inc(s["nm"], 1)

                def residual(b):
                    dve.wait_ge(s["xo"], b + 1)
                    xb = T["x"][:, at(TB * b, TB), :].rearrange("p a d -> p (a d)")
                    nc.vector.tensor_tensor(xb, xb, mb[:, 0:S], ALU.add).then_inc(s["x1"], 1)

                def late(n):
                    if 1 <= n <= 8:
                        k, r = ROUNDS[n - 1]
                        dve.wait_ge(later["hi"], n)
                        nc.vector.tensor_tensor(T["gu_lo"][:, k, 4 * r:4 * r + 4, :].rearrange("p a b -> p (a b)"),
                                                ring[(n - 1) % 2][:, :, :].rearrange("p a n -> p (a n)"),
                                                T["gu_hi"][:, k, 4 * r:4 * r + 4, :].bitcast(F32).rearrange("p a b -> p (a b)"),
                                                ALU.subtract).then_inc(later["lo"], 1)
                    if n == 2:
                        nc.vector.tensor_tensor(slot_sq[:, :, :], slot[:, :, :], slot[:, :, :], ALU.mult).then_inc(later["sq"], 1)
                        dve.wait_ge(later["sq"], 1)
                        nc.vector.tensor_reduce(ss[:, :], slot_sq[:, :, :], AX.X, ALU.add).then_inc(later["ss"], 1)
                    if n == 9:
                        dve.wait_ge(later["sn"], 1)
                        nc.vector.tensor_scalar(snm[:, :], sn[:, :], 1e-12, float(D) ** -0.5, ALU.max, ALU.mult).then_inc(later["snm"], 1)
                        dve.wait_ge(later["snm"], 1)
                        nc.vector.reciprocal(sr[:, :], snm[:, :]).then_inc(later["sr"], 1)
                        dve.wait_ge(later["sr"], 1)
                        nc.vector.tensor_tensor(slot[:, :, :], slot[:, :, :], sr[:, :].unsqueeze(2).to_broadcast([P, SC, D]),
                                                ALU.mult).then_inc(later["slot_n"], 1)
                    if n == 10:
                        nc.vector.tensor_copy(T["w1_hi"][:, :], w1[:, :]).then_inc(later["split"], 1)
                        dve.wait_ge(later["split"], 1)
                        nc.vector.tensor_tensor(T["w1_lo"][:, :], w1[:, :], T["w1_hi"][:, :].bitcast(F32),
                                                ALU.subtract).then_inc(later["split"], 1)
                    if n == 11:
                        for w, m in ((T["wqkv"], wmean), (bqkv, bmean)):
                            nc.vector.tensor_reduce(m[:, 0, :], w[:, 0:2 * D].rearrange("p (j d) -> p j d", j=2), AX.X, ALU.add).then_inc(later["mean0"], 1)
                        dve.wait_ge(later["mean0"], 2)
                        for m in (wmean, bmean):
                            nc.vector.tensor_scalar(m[:, 1, :], m[:, 0, :], 1.0 / D, None, ALU.mult).then_inc(later["mean"], 1)
                        dve.wait_ge(later["mean"], 2)
                        for w, m in ((T["wqkv"], wmean), (bqkv, bmean)):
                            for j in range(2):
                                nc.vector.tensor_scalar(w[:, j * D:(j + 1) * D], w[:, j * D:(j + 1) * D], m[:, 1, j:j + 1], None,
                                                        ALU.subtract).then_inc(later["centred"], 1)
                    if n == 12:
                        dve.wait_ge(later["centred"], 4)
                        nc.vector.tensor_copy(T["bqkv_hi"][:, :], bqkv[:, :]).then_inc(later["bhi"], 1)
                        dve.wait_ge(later["bhi"], 1)
                        nc.vector.tensor_tensor(T["bqkv_lo"][:, :], bqkv[:, :], T["bqkv_hi"][:, :].bitcast(F32), ALU.subtract).then_inc(later["bhi"], 1)
                    if n == 14:
                        dve.wait_ge(later["sh"], 3)
                        nc.vector.tensor_tensor(T["sh_lo"][:, :, :].rearrange("p a b -> p (a b)"),
                                                ring[0][:, :, :].rearrange("p a n -> p (a n)")[:, 0:2 * I],
                                                T["sh_hi"][:, :, :].bitcast(F32).rearrange("p a b -> p (a b)"), ALU.subtract).then_inc(later["sh_lo"], 1)
                    if n == 15:
                        dve.wait_ge(later["slot_ps"], 1)
                        nc.vector.tensor_scalar(se_t[:, :], ring[1][:, :, :].rearrange("p a n -> p (a n)"), T["gs"][:, 0:1], None,
                                                ALU.mult).then_inc(later["se_t"], 1)
                        dve.wait_ge(later["se_t"], 1)
                        nc.vector.tensor_copy(T["se_hi"][:, :], se_t[:, :]).then_inc(later["split"], 1)
                        dve.wait_ge(later["split"], 3)
                        nc.vector.tensor_tensor(T["se_lo"][:, :], se_t[:, :], T["se_hi"][:, :].bitcast(F32), ALU.subtract).then_inc(later["split"], 1)

                def window(b, par, inner=False):
                    front, back, tail, nxt = parts(b, inner)
                    if isinstance(b, int) and b == B:
                        dve.wait_ge(loads["weights"], 12 * 16)
                    for k, (g, qt, ip) in enumerate(STEPS):
                        if isinstance(b, int) and b == B and k in (3, 6):
                            first = [T["x"][:, t, :] for t in range(TB * SB)]
                            if k == 3:
                                dve.wait_ge(s["x1"], SB)
                                norm_vector_stats(nc, dve, s, "f", first, N, 1)
                            else:
                                dve.wait_ge(s["ht_ps"], B)
                                norm_vector_apply(nc, dve, s, "f", first, N, 1)
                        if tail and k == 7:
                            output(b - 2, 0)
                        if front:
                            dve.wait_ge(s["s_ps"], 16 * b + k + 1)
                            nc.vector.tensor_reduce(mx[:, qt, g, 2 * ip:2 * ip + 2], ring[k % 2][:, :, :], AX.X, ALU.max).then_inc(s["max"], 1)
                            if k == 1:
                                if nxt:
                                    norm_vector_stats(nc, dve, s, "n", tiles(b + 1), N, b + 1)
                                stack(b, 2, par)
                                stack(b, 3, par)
                            if k == 4:
                                values(b, par)
                            if k == 9:
                                negate(b, 0)
                            if k == 15:
                                negate(b, 1)
                        if nxt and k == 3:
                            norm_vector_apply(nc, dve, s, "n", tiles(b + 1), N, b + 1)
                        if tail and k == 9:
                            output(b - 2, 1)
                        if nxt and k == 9:
                            stack(b + 1, 0, 1 - par)
                            stack(b + 1, 1, 1 - par)
                        if tail and k == 15:
                            residual(b - 2)
                        if isinstance(b, int) and b >= B:
                            late(16 * (b - B) + k)

                nc.vector.memset(qblk[0][:, :, :, :].bitcast(F32), 0.0).then_inc(s["zero0"], 1)
                stack(0, 0, 0)
                stack(0, 1, 0)
                windows(dve, window)

            @block.scalar
            def _(act):
                def modulated(b):
                    act.wait_ge(s["ht_ps"], b + 1)
                    need(act, s["qk_ps"], 4 * b)
                    nc.scalar.activation(ht[:, :], ma[:, 0:S], ACT.Identity, scale=T["mod"][:, L0A, 1, at(b)],
                                         bias=T["mod"][:, L0A, 0, at(b)]).then_inc(s["ht"], 1)
                    act.wait_ge(s["ht"], b + 1)
                    nc.scalar.activation(ht_hi[:, :], ht[:, :], ACT.Copy).then_inc(s["ht_hi"], 1)

                def rounded(b, j):
                    act.wait_ge(s["qk_ps"], 4 * b + j + 1)
                    kind = j % 2
                    nc.scalar.activation(hs[:, j % 2, :, :].bitcast(F32R), ring[j % 2][:, :, :], ACT.Identity,
                                         bias=T["rows"][:, 4:5] if kind else 0.0,
                                         scale=T["rows"][:, 2 * kind + 1:2 * kind + 2]).then_inc(s["qk_hs"], 1)

                def maxima(b, half):
                    act.wait_ge(s["mt_ps"], 2 * b + half + 1)
                    need(act, s[f"mblk{half}"], 16 * HB * b)
                    nc.scalar.activation(mt[half][:, :, :].bitcast(F32R), ma[0:2 * HB, :].rearrange("p (g n) -> p g n", g=2), ACT.Copy).then_inc(s["mt"], 1)

                def exponentials(b, k):
                    g, nt, ip = STEPS[k]
                    act.wait_ge(s["st_ps"], 16 * b + k + 1)
                    if ip == 0:
                        need(act, s["pv"], CHUNKS * b + k // 2 - 3)
                    nc.scalar.activation(pt[:, g % 2, nt, 2 * ip:2 * ip + 2, :], st[k % 2][:, :, :], ACT.Exp,
                                         scale=ATTN_SCALE).then_inc(s["pt"], 1)

                def products(b, half):
                    act.wait_ge(s["pv"], CHUNKS * b + CHUNKS // 2 * (half + 1))
                    if half == 0:
                        need(act, s["ut_ps"], TB * b)
                    nc.scalar.activation(us[:, 2 * half:2 * half + 2, :], u[:, 2 * half:2 * half + 2, :], ACT.Copy).then_inc(s["us"], 1)

                def late(n):
                    if 1 <= n <= 12:
                        k, r = ROUNDS[n - 1]
                        src = ring[(n - 1) % 2][:, :, :].rearrange("p a n -> p (a n)")
                        act.wait_ge(later["tr"], n)
                        if k < 2:
                            nc.scalar.activation(T["gu_hi"][:, k, 4 * r:4 * r + 4, :].rearrange("p a b -> p (a b)"), src, ACT.Copy).then_inc(later["hi"], 1)
                        else:
                            nc.scalar.activation(T["down"][:, 4 * r:4 * r + 4, :].rearrange("p a b -> p (a b)"), src, ACT.Copy).then_inc(later["fr"], 1)
                    if n == 13:
                        src = ring[0][:, :, :].rearrange("p a n -> p (a n)")
                        act.wait_ge(later["sh_ps"], 1)
                        nc.scalar.activation(T["sh_hi"][:, :, :].rearrange("p a b -> p (a b)"), src[:, 0:2 * I], ACT.Copy).then_inc(later["sh"], 1)
                        nc.scalar.activation(T["sh_down"][:, :], src[0:I, 2 * I:2 * I + P], ACT.Copy).then_inc(later["sh"], 1)
                        nc.scalar.activation(T["gate_t"][:, :], src[:, 2 * I + P:2 * I + P + E], ACT.Copy).then_inc(later["sh"], 1)

                def window(b, par, inner=False):
                    front, back, tail, nxt = parts(b, inner)
                    for k in range(16):
                        if front and k == 2:
                            rounded(b, 2)
                            rounded(b, 3)
                        if back and k == 1:
                            maxima(b - 1, 1)
                        if tail and k == 3:
                            products(b - 2, 1)
                        if nxt and k == 6:
                            modulated(b + 1)
                        if tail and k == 12:
                            act.wait_ge(s["ot_ps"], b - 1)
                            need(act, s["xo"], b - 2)
                            nc.scalar.activation(ots[:, :], mb[:, 0:S], ACT.Copy).then_inc(s["ots"], 1)
                        if front and k == 11:
                            maxima(b, 0)
                        if back and k == 12:
                            products(b - 1, 0)
                        if nxt and k == 10:
                            rounded(b + 1, 0)
                            rounded(b + 1, 1)
                        for n in SHIFTS[k]:
                            if back:
                                exponentials(b - 1, n)
                        if isinstance(b, int) and b >= B:
                            late(16 * (b - B) + k)

                modulated(0)
                for dst, src in ((bqkv, A["L1_attn_bqkv"].rearrange("(a n) -> a n", a=1)),
                                 (T["bv"], A["L1_attn_bqkv"][2 * D:3 * D].rearrange("(n a) -> n a", a=1)),
                                 (T["gx"], A["L1_ffn_gamma_x"].rearrange("(n a) -> n a", a=1)),
                                 (T["gs"], A["L1_ffn_gamma_slot"].rearrange("(n a) -> n a", a=1))):
                    act.dma_start(dst[:, :], src).then_inc(loads["weights"], 16)
                rounded(0, 0)
                rounded(0, 1)
                windows(act, window)

            @block.tensor
            def _(pe):
                def transposed(b):
                    need(pe, s["n_h0"], TB * b)
                    need(pe, s["v"], TB * b)
                    for t in range(TB):
                        last = nc.tensor.transpose(ma[:, t * P:(t + 1) * P], h0[:, t, :], T["ident"][:, :])
                    last.then_inc(s["ht_ps"], 1)

                def values(b):
                    need(pe, s["mt"], 2 * b)
                    for t in range(TB):
                        last = nc.tensor.matmul(ma[:, S + t * P:S + (t + 1) * P], ht[:, t * P:(t + 1) * P],
                                                T["wv"][:, :, :].rearrange("p h k -> p (h k)"), start=True, stop=True)
                    last.then_inc(s["v_ps"], 1)

                def project(b, j):
                    half, kind = j // 2, j % 2
                    if j == 0:
                        pe.wait_ge(s["ht_lo"], b + 1)
                    need(pe, s["max"], 16 * b + j - 1 if j >= 2 else 16 * (b - 1) + 9 + j)
                    for a in range(2):
                        g = 2 * half + a
                        dst = ring[j % 2][:, a, :]
                        nc.tensor.matmul(dst, T["wqk_hi"][:, kind, g, :], ht_hi[:, :], start=True, stop=False)
                        nc.tensor.matmul(dst, T["wqk_hi"][:, kind, g, :], ht_lo[:, :], start=False, stop=False)
                        last = nc.tensor.matmul(dst, T["wqk_lo"][:, kind, g, :], ht_hi[:, :], start=False, stop=True)
                    last.then_inc(s["qk_ps"], 1)

                def scores(b, k, par, nxt):
                    g, qt, ip = STEPS[k]
                    if k % HALF == 0:
                        pe.wait_ge(s["ks"], 2 * b + k // HALF + 1)
                        pe.wait_ge(s[f"qblk{k // HALF}"], 16 * HB * (b + 1))
                    if k in (2, 3):
                        pe.wait_ge(s[("qs", "ks")[k % 2]], 2 * b + 2)
                    elif k in (10, 11) and nxt:
                        pe.wait_ge(s[("qs", "ks")[k % 2]], 2 * b + 3)
                    elif k > 1 or not isinstance(b, int) or b > 0:
                        pe.wait_ge(s["max"], 16 * b + k - 1)
                    elif k == 0:
                        pe.wait_ge(s["qs"], 1)
                    for a in range(2):
                        last = nc.tensor.matmul(ring[k % 2][:, a, :], qblk[par][:, g, 2 * ip + a, qt * P:(qt + 1) * P],
                                                ks[par][:, g, :], start=True, stop=True)
                    last.then_inc(s["s_ps"], 1)

                def maxima(b, half, nxt):
                    pe.wait_ge(s["nm"], 2 * b + half + 1)
                    if half == 1:
                        pe.wait_ge(s["mt"], 2 * b + 1)
                    elif nxt:
                        pe.wait_ge(s["ht"], b + 2)
                    else:
                        pe.wait_ge(s["v"], TB * (b + 1))
                    for g in range(2):
                        for t in range(TB):
                            last = nc.tensor.transpose(ma[0:2 * HB, g * S + t * P:g * S + (t + 1) * P],
                                                       nm[:, t, 2 * half + g, :, :].rearrange("p i l -> p (i l)"), T["ident"][:, :])
                    last.then_inc(s["mt_ps"], 1)

                def shifted(b, k, par):
                    g, nt, ip = STEPS[k]
                    if k % HALF == 0:
                        pe.wait_ge(s[f"mblk{k // HALF}"], 16 * HB * (b + 1))
                    need(pe, s["pt"], 16 * b + k - 1)
                    nc.tensor.matmul(st[k % 2][:, :, :].rearrange("p a n -> p (a n)"), ks[par][:, g, nt * P:(nt + 1) * P],
                                     qblk[par][:, g, 2 * ip:2 * ip + 2, :].rearrange("p a n -> p (a n)"),
                                     start=True, stop=True).then_inc(s["st_ps"], 1)

                def products(b, c, par):
                    g, nt = c // TB, c % TB
                    pe.wait_ge(s["pt"], 16 * b + 2 * (c + 1))
                    if c in (0, CHUNKS // 2):
                        need(pe, s["us"], 2 * b - 1 + (c > 0))
                    for i in range(HB):
                        last = nc.tensor.matmul(u[i * STACK:(i + 1) * STACK, g, :], vaug[par][:, nt, HB * g + i, :],
                                                pt[:, g % 2, nt, i, :], start=(nt == 0), stop=(nt == TB - 1),
                                                skip_group_check=True)
                    last.then_inc(s["pv"], 1)

                def heads(b, t):
                    if t == 0:
                        pe.wait_ge(s["us"], 2 * (b + 1))
                        need(pe, s["x1"], b)
                    else:
                        pe.wait_ge(s["o"], TB * b + t)
                    for g in range(HG):
                        last = nc.tensor.transpose(mb[:, g * P:(g + 1) * P], us[:, g, t * P:(t + 1) * P], T["ident"][:, :])
                    last.then_inc(s["ut_ps"], 1)

                def outputs_transposed(b):
                    pe.wait_ge(s["o"], TB * (b + 1))
                    for t in range(TB):
                        last = nc.tensor.transpose(mb[:, t * P:(t + 1) * P], o[:, t, :, :].rearrange("p h k -> p (h k)"), T["ident"][:, :])
                    last.then_inc(s["ot_ps"], 1)

                def project_out(b):
                    pe.wait_ge(s["ots"], b + 1)
                    w = T["wo_b"][:, at(b), :].rearrange("p a e -> p (a e)")
                    for t in range(TB):
                        last = nc.tensor.matmul(mb[:, t * P:(t + 1) * P], ots[:, t * P:(t + 1) * P], w, start=True, stop=True)
                    last.then_inc(s["xo"], 1)

                def late(n):
                    def bank(i):
                        return ring[i][:, :, :].rearrange("p a n -> p (a n)")

                    if n == 0:
                        pe.wait_ge(s["max"], 16 * B)
                        pe.wait_ge(loads["weights"], 12 * 16)
                    if n < 12:
                        k, r = ROUNDS[n]
                        if n % 2 == 0 and n != 2 and n != 10:
                            pe.wait_ge(*((loads["gate"], 32) if n == 0 else (loads[{4: "up0", 6: "up1", 8: "down"}[n]], 16)))
                        if n >= 2:
                            if n - 2 < 8:
                                pe.wait_ge(later["lo"], n - 1)
                            else:
                                pe.wait_ge(later["fr"], n - 9)
                        for q in range(4):
                            src = T["down"][:, 4 * r + q, :] if k == 2 else raw[n // 2][:, 4 * (n % 2) + q, :]
                            last = nc.tensor.transpose(bank(n % 2)[:, q * P:(q + 1) * P], src, T["ident"][:, :])
                        last.then_inc(later["tr"], 1)
                    if n == 12:
                        pe.wait_ge(later["fr"], 3)
                        nc.tensor.transpose(bank(0)[:, 0:I], shg[:, :], T["ident"][0:I, 0:I])
                        nc.tensor.transpose(bank(0)[:, I:2 * I], shu[:, :], T["ident"][0:I, 0:I])
                        nc.tensor.transpose(bank(0)[0:I, 2 * I:2 * I + P], shd[:, :], T["ident"][:, :])
                        nc.tensor.transpose(bank(0)[:, 2 * I + P:2 * I + P + E], gw[:, :], T["ident"][0:E, 0:E]).then_inc(later["sh_ps"], 1)
                    if n == 13:
                        pe.wait_ge(later["fr"], 4)
                        pe.wait_ge(later["slot_n"], 1)
                        for k in range(SC):
                            last = nc.tensor.transpose(bank(1)[:, k * P:(k + 1) * P], slot[:, k, :], T["ident"][:, :])
                        last.then_inc(later["slot_ps"], 1)

                def window(b, par, inner=False):
                    front, back, tail, nxt = parts(b, inner)
                    for k in range(16):
                        if front:
                            scores(b, k, par, nxt)
                        for n in SHIFTS[k]:
                            if back:
                                shifted(b - 1, n, 1 - par)
                        if front and k == 1:
                            project(b, 2)
                            project(b, 3)
                        if nxt and k == 9:
                            project(b + 1, 0)
                            project(b + 1, 1)
                        if tail and k == 1:
                            products(b - 2, CHUNKS - 1, par)
                        if back and k == 0:
                            maxima(b - 1, 1, front)
                        if front and k == 3:
                            values(b)
                        if back and k >= 3 and k % 2 == 1:
                            products(b - 1, (k - 3) // 2, 1 - par)
                        if tail and k == 6:
                            heads(b - 2, 0)
                        if nxt and k == 5:
                            transposed(b + 1)
                        if tail and k == 8:
                            heads(b - 2, 1)
                        if tail and k == 11:
                            outputs_transposed(b - 2)
                        if front and k == 10:
                            maxima(b, 0, nxt)
                        if isinstance(b, int) and b == 1 and k == 15:
                            pe.wait_ge(later["wo_b"], 1)
                        if tail and k == 13:
                            project_out(b - 2)
                        if isinstance(b, int) and b >= B:
                            late(16 * (b - B) + k)

                transposed(0)
                pe.wait_ge(s["ht"], 1)
                project(0, 0)
                project(0, 1)
                windows(pe, window)


def experts(nc, T, sems):
    with ExitStack() as own:
        def tmp(name, shape, dt=F32):
            return own.enter_context(nc.sbuf_tensor("e_" + name, shape, dt))

        NP = EP + 1
        NT = TB * SB
        STEPS = B // SB
        h2_hi = tmp("h2_hi", [P, B * S], F32R)
        h2_lo = tmp("h2_lo", [P, B * S], F32R)
        ct_r = tmp("ct_r", [2 * E, B * S], F32R)
        N, h0 = T["norm"], T["norm"]["h0"]
        ht = tmp("ht", [P, N2])
        score = tmp("score", [P, NT, E])
        gsum = tmp("gsum", [P, NT, GROUPS + TOPG])
        best = tmp("best", [P, NT, GROUPS])
        seek = tmp("seek", [P, NT, GROUPS])
        left = tmp("left", [P, NT, GROUPS + TOPG])
        gmask = tmp("gmask", [P, NT, GROUPS])
        masked = tmp("masked", [P, NT, E])
        top = tmp("top", [P, NT, TOPK])
        rest = tmp("rest", [P, NT, E])
        w = tmp("w", [P, NT, E])
        total = tmp("total", [P, NT])
        tmax = tmp("tmax", [P, NT])
        inv = tmp("inv", [P, NT])
        cw = tmp("cw", [P, NT, E])
        c2 = tmp("c2", [P, NT, 2, E])
        sg = tmp("sg", [P, 3, N2])
        su = tmp("su", [P, 2, N2])
        act_w = tmp("act_w", [P, 3, N2])
        yts = tmp("yts", [P, N2])
        g_ps = [own.enter_context(nc.psum_tensor(f"e_g{i}", [P, N2], F32)) for i in range(2)]
        u_ps = [own.enter_context(nc.psum_tensor(f"e_u{i}", [P, N2], F32)) for i in range(2)]
        w_ps = [own.enter_context(nc.psum_tensor(f"e_w{i}", [P, N2], F32)) for i in range(2)]
        y_ps = own.enter_context(nc.psum_tensor("e_y", [P, N2], F32))
        o_ps = own.enter_context(nc.psum_tensor("e_o", [P, N2], F32))
        s = sems("e", [c + "_" + n for c in "nf" for n in NORM_SEMS] +
                 ["ht_ps", "ht", "hi", "lo", "lg", "score", "fill", "gsum", "best", "seek", "left", "gmask", "masked", "top", "rest",
                  "w", "total", "tmax", "inv", "cw", "c_hi", "c_lo", "ct_ps", "ct",
                  "g", "u", "wb", "silu", "sg_free", "su", "act", "act_free", "y", "yts", "o", "o_free"], own)

        def bank(p):
            return (g_ps[p % 2], u_ps[p % 2]) if p < EP else (w_ps[0], o_ps)

        def slot(p):
            return p % 2 if p < EP else 2

        def steps(eng, first, step):
            first()
            with eng.Fori(0, STEPS - 1) as q:
                step(q, True)
            step(STEPS - 1, False)

        with nc.Block() as block:
            @block.gpsimd
            def _(pool):
                with pool.Fori(1, STEPS) as n:
                    norm_pool_rstd(nc, pool, s, "n", NT, T, N, n)
                norm_pool_rstd(nc, pool, s, "f", NT, T, N, 1)

            @block.vector
            def _(dve):
                def route(n, p):
                    xt = [T["x"][:, at(NT * n + t), :].rearrange("p a d -> p (a d)") for t in range(NT)]
                    if p == 1 and not (isinstance(n, int) and n == 0):
                        norm_vector_stats(nc, dve, s, "n", xt, N, n)
                    if p == 2 and not (isinstance(n, int) and n == 0):
                        dve.wait_ge(s["ht_ps"], n)
                        norm_vector_apply(nc, dve, s, "n", xt, N, n)
                    if p == 5:
                        dve.wait_ge(s["hi"], n + 1)
                        nc.vector.tensor_tensor(h2_lo[:, at(N2 * n, N2)], ht[:, :], h2_hi[:, at(N2 * n, N2)].bitcast(F32),
                                                ALU.subtract).then_inc(s["lo"], 1)
                    if p == 7:
                        dve.wait_ge(s["score"], n + 1)
                        nc.vector.tensor_reduce(gsum[:, :, 0:GROUPS], score[:, :, :].rearrange("p t (g k) -> p t g k", k=EPG),
                                                AX.X, ALU.add).then_inc(s["gsum"], 1)
                        dve.wait_ge(s["gsum"], n + 1)
                    if p == 8:
                        for t in range(NT):
                            nc.vector.max(best[:, t, :], gsum[:, t, 0:GROUPS]).then_inc(s["best"], 1)
                        dve.wait_ge(s["best"], NT * (n + 1))
                        nc.vector.tensor_copy(seek[:, :, 0:TOPG], best[:, :, 0:TOPG]).then_inc(s["seek"], 1)
                        dve.wait_ge(s["seek"], n + 1)
                    if p == 9:
                        for t in range(NT):
                            nc.vector.match_replace(left[:, t, :], seek[:, t, :], gsum[:, t, :], -1.0).then_inc(s["left"], 1)
                        dve.wait_ge(s["left"], NT * (n + 1))
                        nc.vector.tensor_scalar(gmask[:, :, :], left[:, :, 0:GROUPS], 0.0, None, ALU.is_lt).then_inc(s["gmask"], 1)
                        dve.wait_ge(s["gmask"], n + 1)
                        nc.vector.tensor_tensor(masked[:, :, :].rearrange("p t (g k) -> p (t g) k", k=EPG),
                                                score[:, :, :].rearrange("p t (g k) -> p (t g) k", k=EPG),
                                                gmask[:, :, :].rearrange("p t g -> p (t g)").unsqueeze(2).to_broadcast([P, NT * GROUPS, EPG]),
                                                ALU.mult).then_inc(s["masked"], 1)
                        dve.wait_ge(s["masked"], n + 1)
                    if p == 10:
                        for t in range(NT):
                            nc.vector.max(top[:, t, :], masked[:, t, :]).then_inc(s["top"], 1)
                        dve.wait_ge(s["top"], NT * (n + 1))
                    if p == 11:
                        for t in range(NT):
                            nc.vector.match_replace(rest[:, t, :], top[:, t, :], masked[:, t, :], -1.0).then_inc(s["rest"], 1)
                        dve.wait_ge(s["rest"], NT * (n + 1))
                        nc.vector.scalar_tensor_tensor(w[:, :, :].rearrange("p t e -> p (t e)"), rest[:, :, :].rearrange("p t e -> p (t e)"), 0.0,
                                                       masked[:, :, :].rearrange("p t e -> p (t e)"), ALU.is_lt, ALU.mult).then_inc(s["w"], 1)
                        dve.wait_ge(s["w"], n + 1)
                        nc.vector.tensor_reduce(total[:, :], w[:, :, :], AX.X, ALU.add).then_inc(s["total"], 1)
                        dve.wait_ge(s["total"], n + 1)
                        nc.vector.tensor_scalar(tmax[:, :], total[:, :], 1e-12, None, ALU.max).then_inc(s["tmax"], 1)
                        dve.wait_ge(s["tmax"], n + 1)
                        nc.vector.reciprocal(inv[:, :], tmax[:, :]).then_inc(s["inv"], 1)
                    if p == 12:
                        dve.wait_ge(s["inv"], n + 1)
                        nc.vector.tensor_tensor(cw[:, :, :], w[:, :, :], inv[:, :].unsqueeze(2).to_broadcast([P, NT, E]),
                                                ALU.mult).then_inc(s["cw"], 1)
                        dve.wait_ge(s["cw"], n + 1)
                        nc.vector.tensor_copy(c2[:, :, 0, :].bitcast(F32R), cw[:, :, :]).then_inc(s["c_hi"], 1)
                        dve.wait_ge(s["c_hi"], n + 1)
                        nc.vector.tensor_tensor(c2[:, :, 1, :].bitcast(F32R), cw[:, :, :], c2[:, :, 0, :], ALU.subtract).then_inc(s["c_lo"], 1)

                def weigh(q, p):
                    dve.wait_ge(s["silu"], NP * q + p + 1)
                    dve.wait_ge(s["u"], NP * q + p + 1)
                    g, u = bank(p)
                    if p < EP:
                        nc.vector.tensor_tensor(su[:, p % 2, :], sg[:, slot(p), :], u[:, :], ALU.mult).then_inc(s["sg_free"], 1)
                        dve.wait_ge(s["sg_free"], EP * q + p + 3)
                        dve.wait_ge(s["wb"], EP * q + p + 1)
                        dve.wait_ge(s["act_free"], EP * q + p + 1)
                        nc.vector.tensor_tensor(act_w[:, slot(p), :], su[:, p % 2, :], w_ps[p % 2][:, :], ALU.mult).then_inc(s["act"], 1)
                    else:
                        nc.vector.tensor_tensor(act_w[0:I, slot(p), :], sg[0:I, slot(p), :], u[0:I, :], ALU.mult).then_inc(s["act"], 1)

                def first():
                    dve.sem_inc(s["o_free"], 1)
                    dve.sem_inc(s["sg_free"], 2)
                    nc.vector.memset(gsum[:, :, GROUPS:], -5.0).then_inc(s["fill"], 1)
                    nc.vector.memset(seek[:, :, TOPG:], -5.0).then_inc(s["fill"], 1)
                    dve.wait_ge(s["fill"], 2)
                    for p in range(EP):
                        route(0, p)
                    weigh(0, 0)

                def step(q, nxt):
                    for p in range(1, NP):
                        if nxt:
                            route(q + 1, p)
                        elif p in (2, 5):
                            first = [T["x"][:, t, :] for t in range(NT)]
                            if p == 2:
                                dve.wait_ge(s["o_free"], 2)
                                norm_vector_stats(nc, dve, s, "f", first, N, 1)
                            else:
                                dve.wait_ge(s["ht_ps"], STEPS)
                                norm_vector_apply(nc, dve, s, "f", first, N, 1)
                        weigh(q, p)
                    if nxt:
                        weigh(q + 1, 0)
                    dve.wait_ge(s["o"], q + 1)
                    xq = T["x"][:, at(NT * q, NT), :].rearrange("p a d -> p (a d)")
                    nc.vector.tensor_tensor(xq, xq, o_ps[:, :], ALU.add).then_inc(s["o_free"], 1)

                steps(dve, first, step)

            @block.scalar
            def _(act):
                def route(n, p):
                    if p == 4:
                        act.wait_ge(s["ht_ps"], n + 1)
                        for k in range(SB):
                            b = SB * n + k
                            nc.scalar.activation(ht[:, k * S:(k + 1) * S], o_ps[:, k * S:(k + 1) * S], ACT.Identity,
                                                 scale=T["mod"][:, L0F, 1, at(b)], bias=T["mod"][:, L0F, 0, at(b)]).then_inc(s["ht"], 1)
                        act.wait_ge(s["ht"], SB * (n + 1))
                        nc.scalar.activation(h2_hi[:, at(N2 * n, N2)], ht[:, :], ACT.Copy).then_inc(s["hi"], 1)
                    if p == 6:
                        act.wait_ge(s["lg"], n + 1)
                        nc.scalar.activation(score[:, :, :].rearrange("p a e -> p (a e)"), o_ps[:, 0:NT * E],
                                             ACT.Sigmoid).then_inc(s["score"], 1)
                    if p == 14:
                        act.wait_ge(s["ct_ps"], n + 1)
                        nc.scalar.activation(ct_r[:, at(N2 * n, N2)], o_ps[0:2 * E, :], ACT.Copy).then_inc(s["ct"], 1)

                def silu(q, p):
                    m = P if p < EP else I
                    act.wait_ge(s["g"], NP * q + p + 1)
                    if p < EP:
                        act.wait_ge(s["sg_free"], EP * q + p + 1)
                    nc.scalar.activation(sg[0:m, slot(p), :], bank(p)[0][0:m, :], ACT.Silu).then_inc(s["silu"], 1)

                def first():
                    for p in range(EP):
                        route(0, p)
                    silu(0, 0)

                def step(q, nxt):
                    for p in range(1, NP):
                        if nxt:
                            route(q + 1, p)
                        silu(q, p)
                    if nxt:
                        silu(q + 1, 0)
                    act.wait_ge(s["y"], q + 1)
                    nc.scalar.activation(yts[:, :], y_ps[:, :], ACT.Copy).then_inc(s["yts"], 1)

                steps(act, first, step)

            @block.tensor
            def _(pe):
                def route(n, p):
                    if p == 3:
                        need(pe, s["n_h0"], NT * n)
                        need(pe, s["o_free"], n)
                        for t in range(NT):
                            last = nc.tensor.transpose(o_ps[:, t * P:(t + 1) * P], h0[:, t, :], T["ident"][:, :])
                        last.then_inc(s["ht_ps"], 1)
                    if p == 5:
                        pe.wait_ge(s["ht"], SB * (n + 1))
                        for t in range(NT):
                            last = nc.tensor.matmul(o_ps[:, t * E:(t + 1) * E], ht[:, t * P:(t + 1) * P], T["gate_t"][:, :],
                                                    start=True, stop=True)
                        last.then_inc(s["lg"], 1)
                    if p == 13:
                        for t in range(NT):
                            last = nc.tensor.transpose(o_ps[0:2 * E, t * P:(t + 1) * P], c2[:, t, :, :].rearrange("p l e -> p (l e)"),
                                                       T["ident"][:, :])
                        last.then_inc(s["ct_ps"], 1)

                def project(q, p):
                    m = P if p < EP else I
                    w_hi = [T["gu_hi"][:, j, p, :] if p < EP else T["sh_hi"][:, j, :] for j in range(2)]
                    w_lo = [T["gu_lo"][:, j, p, :] if p < EP else T["sh_lo"][:, j, :] for j in range(2)]
                    cols = at(N2 * q, N2)
                    for j, dst in enumerate(bank(p)):
                        nc.tensor.matmul(dst[0:m, :], w_hi[j], h2_hi[:, cols], start=True, stop=False)
                        nc.tensor.matmul(dst[0:m, :], w_hi[j], h2_lo[:, cols], start=False, stop=False)
                        nc.tensor.matmul(dst[0:m, :], w_lo[j], h2_hi[:, cols], start=False, stop=True).then_inc(s[("g", "u")[j]], 1)

                def weights(q, p):
                    nc.tensor.matmul(w_ps[p % 2][:, :], T["sel"][:, p, :], ct_r[:, at(N2 * q, N2)], start=True, stop=True).then_inc(s["wb"], 1)

                def down(q, p):
                    pe.wait_ge(s["act"], NP * q + p + 1)
                    if p < EP:
                        nc.tensor.matmul(y_ps[:, :], T["down"][:, p, :], act_w[:, slot(p), :], start=(p == 0), stop=False).then_inc(s["act_free"], 1)
                    else:
                        nc.tensor.matmul(y_ps[:, :], T["sh_down"][:, :], act_w[0:I, slot(p), :], start=False, stop=True).then_inc(s["y"], 1)

                def begin(q):
                    weights(q, 0)
                    project(q, 1)
                    weights(q, 1)

                def first():
                    pe.sem_inc(s["act_free"], 2)
                    for p in range(6):
                        route(0, p)
                    pe.wait_ge(s["lo"], 1)
                    project(0, 0)
                    pe.wait_ge(s["c_lo"], 1)
                    route(0, 13)
                    pe.wait_ge(s["ct"], 1)
                    begin(0)

                def step(q, nxt):
                    down(q, 0)
                    for p in range(1, NP):
                        if nxt and p < 13:
                            route(q + 1, p)
                        if p + 1 == EP - 1:
                            if nxt:
                                pe.wait_ge(s["ct"], q + 2)
                            else:
                                pe.wait_ge(s["o_free"], q + 1)
                        if nxt and p == 13:
                            pe.wait_ge(s["c_lo"], q + 2)
                        if p + 1 < EP:
                            project(q, p + 1)
                            weights(q, p + 1)
                            if nxt and p == 13:
                                route(q + 1, p)
                        elif p + 1 == EP:
                            project(q, EP)
                        elif nxt:
                            pe.wait_ge(s["lo"], q + 2)
                            project(q + 1, 0)
                        down(q, p)
                    if nxt:
                        begin(q + 1)
                    pe.wait_ge(s["yts"], q + 1)
                    for t in range(NT):
                        last = nc.tensor.matmul(o_ps[:, t * P:(t + 1) * P], yts[:, t * P:(t + 1) * P],
                                                T["diag"][:, at(SB * q + t // TB), :].rearrange("p a n -> p (a n)"), start=True, stop=True)
                    last.then_inc(s["o"], 1)

                steps(pe, first, step)


def linear_attention(nc, T, sems):
    with ExitStack() as own:
        def tmp(name, shape, dt=F32):
            return own.enter_context(nc.sbuf_tensor("l_" + name, shape, dt))

        NT = TB * SB
        STEPS = B // SB
        N, h0 = T["norm"], T["norm"]["h0"]
        ht = tmp("ht", [P, N2])
        sq = tmp("sq", [P, NT, 2, D])
        ssum = tmp("ssum", [P, NT, 2])
        den = tmp("den", [P, NT, 2])
        r1 = tmp("r1", [P, NT, 2])
        q4 = tmp("q4", [P, NT, D])
        q4s = tmp("q4s", [P, NT])
        r1q = tmp("r1q", [P, NT])
        n2 = tmp("n2", [P, NT])
        nq = tmp("nq", [P, NT])
        nqm = tmp("nqm", [P, NT])
        rq = tmp("rq", [P, NT])
        rq2 = tmp("rq2", [P, NT])
        q2n = tmp("q2n", [P, NT, D])
        k2 = tmp("k2", [P, NT, D])
        k4 = tmp("k4", [P, NT, D])
        v = tmp("v", [P, NT, D])
        q2t = tmp("q2t", [P, N2])
        kn = tmp("kn", [P, SB])
        knr = tmp("knr", [P, SB])
        knm = tmp("knm", [P, SB])
        rk = tmp("rk", [P, SB])
        kvs = tmp("kvs", [P, SB, D])
        zts = tmp("zts", [P, N2])
        ht_ps = own.enter_context(nc.psum_tensor("l_ht_ps", [P, 512], F32))
        qk_ps = own.enter_context(nc.psum_tensor("l_qk", [P, NT, 2 * D], F32))
        v_ps = own.enter_context(nc.psum_tensor("l_v_ps", [P, NT, D], F32))
        kv_ps = own.enter_context(nc.psum_tensor("l_kv", [P, 512], F32))
        qt_ps = own.enter_context(nc.psum_tensor("l_qt", [P, 512], F32))
        z_ps = own.enter_context(nc.psum_tensor("l_z", [P, 512], F32))
        y_ps = own.enter_context(nc.psum_tensor("l_y", [P, 512], F32))
        s = sems("l", [c + "_" + n for c in "nf" for n in NORM_SEMS] +
                 ["ht_ps", "ht", "qk", "v_ps", "v", "ssum", "den", "r1", "sq", "q4", "q4s", "r1q", "n2", "nq",
                  "nqm", "rq", "rq2", "q2n", "k2", "k4", "kv", "kn", "knr", "knm", "rk", "kvs", "qt", "q2t", "zv", "z", "zts", "y",
                  "y_free"], own)

        def windows(eng, window):
            window(0, True, False, True)
            with eng.Fori(1, STEPS - 1) as q:
                window(q, True, True, True)
            window(STEPS - 1, True, True, False)
            window(STEPS, False, True, False)

        with nc.Block() as block:
            @block.gpsimd
            def _(pool):
                def window(q, front, back, nxt):
                    if back:
                        pool.wait_ge(s["kn"], q)
                        nc.gpsimd.tensor_tensor(knr[:, :], kn[:, :], T["half"][:, 0:SB], ALU.pow).then_inc(s["knr"], 1)
                    if nxt:
                        norm_pool_rstd(nc, pool, s, "n", NT, T, N, q + 1)
                    if front:
                        pool.wait_ge(s["n2"], q + 1)
                        nc.gpsimd.tensor_tensor(nq[:, :], n2[:, :], T["half"][:, 0:NT], ALU.pow).then_inc(s["nq"], 1)

                windows(pool, window)
                norm_pool_rstd(nc, pool, s, "f", TB, T, N, 1)

            @block.vector
            def _(dve):
                def tiles(q):
                    if isinstance(q, int):
                        return [T["x"][:, NT * q + t, :] for t in range(NT)]
                    return [T["x"][:, bass.ds(NT * q + t, 1), :].rearrange("p a d -> p (a d)") for t in range(NT)]

                def window(q, front, back, nxt):
                    if back:
                        dve.wait_ge(s["kv"], q)
                        nc.vector.tensor_copy(kn[:, :], kv_ps[:, SB * D:SB * D + SB]).then_inc(s["kn"], 1)
                    if nxt:
                        norm_vector_stats(nc, dve, s, "n", tiles(q + 1), N, q + 1)
                    if back:
                        dve.wait_ge(s["knr"], q)
                        nc.vector.tensor_scalar(knm[:, :], knr[:, :], 1e-12, float(S) ** 0.5, ALU.max, ALU.mult).then_inc(s["knm"], 1)
                        dve.wait_ge(s["knm"], q)
                        nc.vector.reciprocal(rk[:, :], knm[:, :]).then_inc(s["rk"], 1)
                        dve.wait_ge(s["rk"], q)
                        for k in range(SB):
                            nc.vector.tensor_scalar(kvs[:, k, :], kv_ps[:, k * D:(k + 1) * D], rk[:, k:k + 1], None,
                                                    ALU.mult).then_inc(s["kvs"], 1)
                    if front:
                        dve.wait_ge(s["sq"], q + 1)
                        nc.vector.tensor_reduce(ssum[:, :, :].rearrange("p t j -> p (t j)"),
                                                sq[:, :, :, :].rearrange("p t j d -> p (t j) d"), AX.X, ALU.add).then_inc(s["ssum"], 1)
                        dve.wait_ge(s["ssum"], q + 1)
                        nc.vector.tensor_scalar(den[:, :, :], ssum[:, :, :], 1e-7, None, ALU.add).then_inc(s["den"], 1)
                        dve.wait_ge(s["den"], q + 1)
                        nc.vector.reciprocal(r1[:, :, :], den[:, :, :]).then_inc(s["r1"], 1)
                        dve.wait_ge(s["q4"], q + 1)
                        nc.vector.tensor_reduce(q4s[:, :], q4[:, :, :], AX.X, ALU.add).then_inc(s["q4s"], 1)
                        dve.wait_ge(s["r1"], q + 1)
                        nc.vector.tensor_tensor(r1q[:, :], r1[:, :, 0], r1[:, :, 0], ALU.mult).then_inc(s["r1q"], 1)
                        dve.wait_ge(s["q4s"], q + 1)
                        dve.wait_ge(s["r1q"], q + 1)
                        nc.vector.tensor_tensor(n2[:, :], q4s[:, :], r1q[:, :], ALU.mult).then_inc(s["n2"], 1)
                        nc.vector.tensor_tensor(k2[:, :, :], sq[:, :, 1, :], r1[:, :, 1].unsqueeze(2).to_broadcast([P, NT, D]),
                                                ALU.mult).then_inc(s["k2"], 1)
                    if nxt:
                        dve.wait_ge(s["ht_ps"], q + 1)
                        norm_vector_apply(nc, dve, s, "n", tiles(q + 1), N, q + 1)
                    if front:
                        dve.wait_ge(s["nq"], q + 1)
                        nc.vector.tensor_scalar(nqm[:, :], nq[:, :], 1e-12, None, ALU.max).then_inc(s["nqm"], 1)
                        dve.wait_ge(s["nqm"], q + 1)
                        nc.vector.reciprocal(rq[:, :], nqm[:, :]).then_inc(s["rq"], 1)
                        dve.wait_ge(s["rq"], q + 1)
                        nc.vector.tensor_tensor(rq2[:, :], rq[:, :], r1[:, :, 0], ALU.mult).then_inc(s["rq2"], 1)
                        dve.wait_ge(s["rq2"], q + 1)
                        need(dve, s["qt"], q)
                        nc.vector.tensor_tensor(q2n[:, :, :], sq[:, :, 0, :], rq2[:, :].unsqueeze(2).to_broadcast([P, NT, D]),
                                                ALU.mult).then_inc(s["q2n"], 1)
                    if not front:
                        first = [T["x"][:, t, :] for t in range(TB)]
                        dve.wait_ge(s["y_free"], 2)
                        norm_vector_stats(nc, dve, s, "f", first, N, 1)
                        dve.wait_ge(s["ht_ps"], STEPS)
                        norm_vector_apply(nc, dve, s, "f", first, N, 1)
                    if back:
                        dve.wait_ge(s["y"], q)
                        xq = T["x"][:, NT * (q - 1):NT * q, :] if isinstance(q, int) else T["x"][:, bass.ds(NT * q - NT, NT), :]
                        xq = xq.rearrange("p a d -> p (a d)")
                        nc.vector.tensor_tensor(xq, xq, y_ps[:, :], ALU.add).then_inc(s["y_free"], 1)

                dve.sem_inc(s["y_free"], 1)
                windows(dve, window)

            @block.scalar
            def _(act):
                def window(q, front, back, nxt):
                    if front:
                        act.wait_ge(s["ht_ps"], q + 1)
                        need(act, s["zv"], q)
                        for k in range(SB):
                            nc.scalar.activation(ht[:, k * S:(k + 1) * S], ht_ps[:, k * S:(k + 1) * S], ACT.Identity,
                                                 scale=T["mod"][:, L1A, 1, at(SB * q + k)],
                                                 bias=T["mod"][:, L1A, 0, at(SB * q + k)]).then_inc(s["ht"], 1)
                    if back:
                        act.wait_ge(s["qt"], q)
                        nc.scalar.activation(q2t[:, :], qt_ps[:, :], ACT.Copy).then_inc(s["q2t"], 1)
                    if front:
                        act.wait_ge(s["qk"], q + 1)
                        need(act, s["q2n"], q)
                        nc.scalar.activation(sq[:, :, :, :].rearrange("p t j d -> p t (j d)"), qk_ps[:, :, :], ACT.Square).then_inc(s["sq"], 1)
                        act.wait_ge(s["sq"], q + 1)
                        nc.scalar.activation(q4[:, :, :], sq[:, :, 0, :], ACT.Square).then_inc(s["q4"], 1)
                        act.wait_ge(s["v_ps"], q + 1)
                        nc.scalar.activation(v[:, :, :], v_ps[:, :, :], ACT.Copy).then_inc(s["v"], 1)
                    if back:
                        act.wait_ge(s["z"], q)
                        nc.scalar.activation(zts[:, :], z_ps[:, :], ACT.Identity, bias=T["bv"][:, 0:1]).then_inc(s["zts"], 1)
                    if front:
                        act.wait_ge(s["k2"], q + 1)
                        nc.scalar.activation(k4[:, :, :], k2[:, :, :], ACT.Square).then_inc(s["k4"], 1)

                windows(act, window)

            @block.tensor
            def _(pe):
                def window(q, front, back, nxt):
                    if front:
                        need(pe, s["n_h0"], NT * q)
                        need(pe, s["ht"], SB * q)
                        for t in range(NT):
                            last = nc.tensor.transpose(ht_ps[:, t * P:(t + 1) * P], h0[:, t, :], T["ident"][:, :])
                        last.then_inc(s["ht_ps"], 1)
                    if back:
                        pe.wait_ge(s["v"], q)
                        pe.wait_ge(s["k4"], q)
                        for k in range(SB):
                            for t in range(TB):
                                last = nc.tensor.matmul(kv_ps[:, SB * D + k:SB * D + k + 1], k4[:, TB * k + t, :], T["ones"][:, 0:1],
                                                        start=(t == 0), stop=(t == TB - 1))
                        for k in range(SB):
                            for t in range(TB):
                                last = nc.tensor.matmul(kv_ps[:, k * D:(k + 1) * D], k2[:, TB * k + t, :], v[:, TB * k + t, :],
                                                        start=(t == 0), stop=(t == TB - 1))
                        last.then_inc(s["kv"], 1)
                        pe.wait_ge(s["q2n"], q)
                        for t in range(NT):
                            last = nc.tensor.transpose(qt_ps[:, t * P:(t + 1) * P], q2n[:, t, :], T["ident"][:, :])
                        last.then_inc(s["qt"], 1)
                    if front:
                        pe.wait_ge(s["ht"], SB * (q + 1))
                        need(pe, s["sq"], q)
                        need(pe, s["v"], q)
                        for t in range(NT):
                            nc.tensor.matmul(qk_ps[:, t, :], ht[:, t * P:(t + 1) * P], T["wqkv"][:, 0:2 * D], start=True, stop=False)
                            for part in T["bqkv_hi"], T["bqkv_lo"]:
                                last = nc.tensor.matmul(qk_ps[:, t, :], T["ones_r"][0:1, :], part[:, 0:2 * D],
                                                        start=False, stop=part is T["bqkv_lo"])
                        last.then_inc(s["qk"], 1)
                        for t in range(NT):
                            nc.tensor.matmul(v_ps[:, t, :], ht[:, t * P:(t + 1) * P], T["wqkv"][:, 2 * D:3 * D], start=True, stop=False)
                            for part in T["bqkv_hi"], T["bqkv_lo"]:
                                last = nc.tensor.matmul(v_ps[:, t, :], T["ones_r"][0:1, :], part[:, 2 * D:3 * D],
                                                        start=False, stop=part is T["bqkv_lo"])
                        last.then_inc(s["v_ps"], 1)
                    if back:
                        pe.wait_ge(s["kvs"], SB * q)
                        pe.wait_ge(s["q2t"], q)
                        for k in range(SB):
                            last = nc.tensor.matmul(z_ps[:, k * S:(k + 1) * S], kvs[:, k, :], q2t[:, k * S:(k + 1) * S],
                                                    start=False, stop=True, skip_group_check=True)
                        last.then_inc(s["z"], 1)
                        pe.wait_ge(s["zts"], q)
                        pe.wait_ge(s["y_free"], q)
                    if front:
                        nc.tensor.matmul(z_ps[:, :], T["wqkv"][:, 2 * D:3 * D], ht[:, :], start=True, stop=False,
                                         skip_group_check=True).then_inc(s["zv"], 1)
                    if back:
                        for t in range(NT):
                            w, hi, lo = [r[:, at(SB * q - SB + t // TB), :].rearrange("p a n -> p (a n)")
                                         for r in (T["wln_b"], T["bln_hi"], T["bln_lo"])]
                            dst = y_ps[:, t * P:(t + 1) * P]
                            nc.tensor.matmul(dst, zts[:, t * P:(t + 1) * P], w, start=True, stop=False)
                            nc.tensor.matmul(dst, T["ones_r"][0:1, :], hi, start=False, stop=False)
                            last = nc.tensor.matmul(dst, T["ones_r"][0:1, :], lo, start=False, stop=True)
                        last.then_inc(s["y"], 1)

                windows(pe, window)


def slots(nc, T, out, sems):
    with ExitStack() as own:
        def tmp(name, shape, dt=F32):
            return own.enter_context(nc.sbuf_tensor("s_" + name, shape, dt))

        N, h0 = T["norm"], T["norm"]["h0"]
        ht = tmp("ht", [P, S])
        hsq = tmp("hsq", [P, S])
        gdiag = tmp("gdiag", [P, P])
        ssum = tmp("ssum", [P, TB])
        norm = tmp("norm", [P, TB])
        norm_m = tmp("norm_m", [P, TB])
        rnorm = tmp("rnorm", [P, TB])
        xns = [tmp(f"xn{i}", [P, TB, D + 1]) for i in range(2)]
        xnt_hi = tmp("xnt_hi", [P, S], F32R)
        xnt_lo = tmp("xnt_lo", [P, S], F32R)
        m_slot = tmp("m_slot", [P, SC])
        m_tok = tmp("m_tok", [P, TB])
        d_slot = tmp("d_slot", [P, SC, P], F32R)
        d_tok = tmp("d_tok", [P, TB, P], F32R)
        disp = tmp("disp", [P, TB, SLOTS])
        comb = [tmp(f"comb{i}", [P, SC, S]) for i in range(2)]
        rz = tmp("rz", [P, SC])
        sl = tmp("sl", [P, SC, D])
        slt_hi = tmp("slt_hi", [P, SLOTS], F32R)
        slt_lo = tmp("slt_lo", [P, SLOTS], F32R)
        hid = tmp("hid", [P, HC, SLOTS])
        proc = tmp("proc", [P, SC, D + 1])
        ru = tmp("ru", [P, TB])
        yo = tmp("yo", [P, TB, D])
        pa = own.enter_context(nc.psum_tensor("s_a", [P, TB, SLOTS], F32))
        pb = own.enter_context(nc.psum_tensor("s_b", [P, SC, S], F32))
        ma = own.enter_context(nc.psum_tensor("s_ma", [P, 512], F32))
        pc = own.enter_context(nc.psum_tensor("s_c", [P, 2, 512], F32))
        mb = own.enter_context(nc.psum_tensor("s_mb", [P, 512], F32))
        s = sems("s", ["n_" + n for n in NORM_SEMS] +
                 ["one", "gdiag", "ht_ps", "ht", "hsq", "ss", "ssum", "norm", "nm", "rn", "xt_ps", "xn", "xnt_ps", "xnt_hi", "xnt_lo",
                  "la", "lb", "m_tok", "m_slot", "d", "fa", "fb", "disp", "comb", "sl_ps", "rz", "sl", "slt_ps", "slt_hi", "slt_lo",
                  "h_ps", "hid", "pr_ps", "proc", "u_ps", "ru", "yo", "res", "stored0", "stored1"], own)
        slot_out = lambda c, n: pc[:, c // 2, c % 2 * (D + 1):c % 2 * (D + 1) + n]

        def windows(eng, window):
            for b in (0, 1):
                window(b, b % 2)
            with eng.Fori(0, (B - 4) // 2) as turn:
                window(2 * turn + 2, 0, True)
                window(2 * turn + 3, 1, True)
            for b in range(B - 2, B + 2):
                window(b, b % 2)

        def parts(b, inner):
            return (True, True, True, True) if inner else (b < B, 1 <= b <= B, 2 <= b, b + 1 < B)

        with nc.Block() as block:
            @block.gpsimd
            def _(pool):
                for xn in xns:
                    nc.gpsimd.memset(xn[:, :, D:D + 1], 1.0).then_inc(s["one"], 1)
                nc.gpsimd.memset(proc[:, :, D:D + 1], 1.0).then_inc(s["one"], 1)
                def norms(b):
                    pool.wait_ge(s["ssum"], b + 1)
                    nc.gpsimd.tensor_tensor(norm[:, :], ssum[:, :], T["half"][:, 0:TB], ALU.pow).then_inc(s["norm"], 1)

                with pool.Fori(0, B - 1) as b:
                    norms(b)
                    norm_pool_rstd(nc, pool, s, "n", TB, T, N, b + 1)
                norms(B - 1)

            @block.sync
            def _(sp):
                for done, b0 in ((B - 1, 0), (B, B - 1)):
                    sp.wait_ge(s["res"], done)
                    sp.dma_start(out[b0:done].rearrange("b (t p) d -> p (b t) d", p=P),
                                 T["x"][:, TB * b0:TB * done, :]).then_inc(s[f"stored{b0 > 0:d}"], 16)
                sp.wait_ge(s["stored0"], 16)
                sp.wait_ge(s["stored1"], 16)

            @block.vector
            def _(dve):
                def tiles(b):
                    if isinstance(b, int):
                        return [T["x"][:, TB * b + t, :] for t in range(TB)]
                    return [T["x"][:, bass.ds(TB * b + t, 1), :].rearrange("p a d -> p (a d)") for t in range(TB)]

                def window(b, par, inner=False):
                    front, back, tail, nxt = parts(b, inner)
                    xn = xns[par]
                    if front:
                        dve.wait_ge(s["ss"], b + 1)
                        nc.vector.tensor_copy(ssum[:, :], ma[:, 256:256 + TB]).then_inc(s["ssum"], 1)
                        dve.wait_ge(s["norm"], b + 1)
                        nc.vector.tensor_scalar(norm_m[:, :], norm[:, :], 1e-12, None, ALU.max).then_inc(s["nm"], 1)
                        dve.wait_ge(s["nm"], b + 1)
                        nc.vector.reciprocal(rnorm[:, :], norm_m[:, :]).then_inc(s["rn"], 1)
                    if tail:
                        dve.wait_ge(s["pr_ps"], b - 1)
                        nc.vector.tensor_copy(proc[:, :, 0:D], mb[:, :].rearrange("p (c d) -> p c d", c=SC)).then_inc(s["proc"], 1)
                    if front:
                        dve.wait_ge(s["rn"], b + 1)
                        dve.wait_ge(s["xt_ps"], b + 1)
                        nc.vector.tensor_tensor(xn[:, :, 0:D], ma[:, 0:S].rearrange("p (t d) -> p t d", t=TB),
                                                rnorm[:, :].unsqueeze(2).to_broadcast([P, TB, D]), ALU.mult).then_inc(s["xn"], 1)
                    if back:
                        dve.wait_ge(s["sl_ps"], b)
                        for k in range(SC):
                            nc.vector.reciprocal(rz[:, k:k + 1], slot_out(k, D + 1)[:, D:D + 1]).then_inc(s["rz"], 1)
                        dve.wait_ge(s["rz"], SC * b)
                        for k in range(SC):
                            nc.vector.tensor_scalar(sl[:, k, :], slot_out(k, D), rz[:, k:k + 1], None, ALU.mult).then_inc(s["sl"], 1)
                    if front:
                        dve.wait_ge(s["xnt_hi"], b + 1)
                        nc.vector.tensor_tensor(xnt_lo[:, :], ma[:, S:2 * S], xnt_hi[:, :].bitcast(F32), ALU.subtract).then_inc(s["xnt_lo"], 1)
                    if tail:
                        dve.wait_ge(s["u_ps"], b - 1)
                        uo = mb[:, 0:TB * (D + 1)].rearrange("p (t d) -> p t d", t=TB)
                        nc.vector.reciprocal(ru[:, :], uo[:, :, D]).then_inc(s["ru"], 1)
                        dve.wait_ge(s["ru"], b - 1)
                        for t in range(TB):
                            nc.vector.scalar_tensor_tensor(yo[:, t, :], uo[:, t, 0:D], ru[:, t:t + 1],
                                                           T["gb"][:, at(b - 2), :].rearrange("p a d -> p (a d)"),
                                                           ALU.mult, ALU.mult).then_inc(s["yo"], 1)
                    if nxt:
                        norm_vector_stats(nc, dve, s, "n", tiles(b + 1), N, b + 1)
                    if tail:
                        dve.wait_ge(s["yo"], TB * (b - 1))
                        xb = T["x"][:, at(TB * (b - 2), TB), :]
                        nc.vector.tensor_tensor(xb, xb, yo[:, :, :], ALU.add).then_inc(s["res"], 1)
                    if back:
                        dve.wait_ge(s["slt_hi"], b)
                        nc.vector.tensor_tensor(slt_lo[:, :], mb[:, :], slt_hi[:, :].bitcast(F32), ALU.subtract).then_inc(s["slt_lo"], 1)
                    if front:
                        dve.wait_ge(s["la"], b + 1)
                        nc.vector.tensor_reduce(m_tok[:, :], pa[:, :, :], AX.X, ALU.max).then_inc(s["m_tok"], 1)
                    if front:
                        dve.wait_ge(s["lb"], b + 1)
                        nc.vector.tensor_reduce(m_slot[:, :], pb[:, :, :], AX.X, ALU.max).then_inc(s["m_slot"], 1)
                        dve.wait_ge(s["m_tok"], b + 1)
                        for t in range(TB):
                            nc.vector.tensor_scalar(d_tok[:, t, :], T["ident"][:, :], m_tok[:, t:t + 1], -1.0,
                                                    ALU.mult, ALU.mult).then_inc(s["d"], 1)
                        dve.wait_ge(s["m_slot"], b + 1)
                        for k in range(SC):
                            nc.vector.tensor_scalar(d_slot[:, k, :], T["ident"][:, :], m_slot[:, k:k + 1], -1.0,
                                                    ALU.mult, ALU.mult).then_inc(s["d"], 1)
                    if nxt:
                        norm_vector_apply(nc, dve, s, "n", tiles(b + 1), N, b + 1)

                nc.vector.tensor_scalar(gdiag[:, :], T["ident"][:, :], T["gx"][:, 0:1], float(D) ** 0.5,
                                        ALU.mult, ALU.mult).then_inc(s["gdiag"], 1)
                windows(dve, window)

            @block.scalar
            def _(act):
                def window(b, par, inner=False):
                    front, back, tail, nxt = parts(b, inner)
                    if front:
                        act.wait_ge(s["ht_ps"], b + 1)
                        nc.scalar.activation(ht[:, :], ma[:, 0:S], ACT.Identity, scale=T["mod"][:, L1F, 1, at(b)],
                                             bias=T["mod"][:, L1F, 0, at(b)]).then_inc(s["ht"], 1)
                        act.wait_ge(s["ht"], b + 1)
                        nc.scalar.activation(hsq[:, :], ht[:, :], ACT.Square).then_inc(s["hsq"], 1)
                        act.wait_ge(s["xnt_ps"], b + 1)
                        nc.scalar.activation(xnt_hi[:, :], ma[:, S:2 * S], ACT.Copy).then_inc(s["xnt_hi"], 1)
                    if back:
                        act.wait_ge(s["slt_ps"], b)
                        nc.scalar.activation(slt_hi[:, :], mb[:, :], ACT.Copy).then_inc(s["slt_hi"], 1)
                        for j in range(HC):
                            act.wait_ge(s["h_ps"], HC * (b - 1) + j + 1)
                            nc.scalar.activation(hid[:, j, :], pc[:, j % 2, :], ACT.Gelu).then_inc(s["hid"], 1)
                    if front:
                        act.wait_ge(s["fa"], b + 1)
                        nc.scalar.activation(disp[:, :, :], pa[:, :, :], ACT.Exp).then_inc(s["disp"], 1)
                        act.wait_ge(s["fb"], b + 1)
                        nc.scalar.activation(comb[par][:, :, :], pb[:, :, :], ACT.Exp).then_inc(s["comb"], 1)

                windows(act, window)

            @block.tensor
            def _(pe):
                def exact(dst, w, x, skip=False):
                    nc.tensor.matmul(dst, w[0], x[0], start=True, stop=False, skip_group_check=skip)
                    nc.tensor.matmul(dst, w[0], x[1], start=False, stop=False, skip_group_check=skip)
                    return nc.tensor.matmul(dst, w[1], x[0], start=False, stop=not skip, skip_group_check=skip)

                def token_logits(t):
                    cols = slice(t * P, (t + 1) * P)
                    return exact(pa[:, t, :], (xnt_hi[:, cols], xnt_lo[:, cols]), (T["se_hi"][:, :], T["se_lo"][:, :]), True)

                def window(b, par, inner=False):
                    front, back, tail, nxt = parts(b, inner)
                    if front:
                        need(pe, s["n_h0"], TB * b)
                        need(pe, s["xnt_lo"], b)
                        for t in range(TB):
                            last = nc.tensor.transpose(ma[:, t * P:(t + 1) * P], h0[:, t, :], T["ident"][:, :])
                        last.then_inc(s["ht_ps"], 1)
                    if tail:
                        pe.wait_ge(s["hid"], HC * (b - 1))
                        pe.wait_ge(s["slt_lo"], b - 1)
                        for k in range(SC):
                            for j in range(HC):
                                last = nc.tensor.matmul(mb[:, k * P:(k + 1) * P], hid[:, j, k * P:(k + 1) * P], T["w2"][:, j, :],
                                                        start=(j == 0), stop=(j == HC - 1))
                        last.then_inc(s["pr_ps"], 1)
                    if front:
                        pe.wait_ge(s["hsq"], b + 1)
                        for t in range(TB):
                            last = nc.tensor.matmul(ma[:, 256 + t:257 + t], hsq[:, t * P:(t + 1) * P], T["ones"][:, 0:1], start=True, stop=True)
                        last.then_inc(s["ss"], 1)
                    if front:
                        pe.wait_ge(s["ssum"], b + 1)
                        for t in range(TB):
                            last = nc.tensor.matmul(ma[:, t * P:(t + 1) * P], ht[:, t * P:(t + 1) * P], gdiag[:, :],
                                                    start=True, stop=True)
                        last.then_inc(s["xt_ps"], 1)
                    if back:
                        pe.wait_ge(s["disp"], b)
                        need(pe, s["hid"], HC * (b - 1))
                        for k in range(SC):
                            for t in range(TB):
                                last = nc.tensor.matmul(slot_out(k, D + 1), disp[:, t, k * P:(k + 1) * P], xns[1 - par][:, t, :],
                                                        start=(t == 0), stop=(t == TB - 1), skip_group_check=True)
                        last.then_inc(s["sl_ps"], 1)
                    if front:
                        pe.wait_ge(s["xn"], b + 1)
                        for t in range(TB):
                            last = nc.tensor.transpose(ma[:, S + t * P:S + (t + 1) * P], xns[par][:, t, 0:D], T["ident"][:, :])
                        last.then_inc(s["xnt_ps"], 1)
                    if tail:
                        pe.wait_ge(s["comb"], b - 1)
                        pe.wait_ge(s["proc"], b - 1)
                        for t in range(TB):
                            for k in range(SC):
                                last = nc.tensor.matmul(mb[:, t * (D + 1):(t + 1) * (D + 1)], comb[par][:, k, t * P:(t + 1) * P],
                                                        proc[:, k, :], start=(k == 0), stop=(k == SC - 1))
                        last.then_inc(s["u_ps"], 1)
                    if front:
                        pe.wait_ge(s["xnt_lo"], b + 1)
                        need(pe, s["disp"], b)
                        token_logits(0)
                    if back:
                        pe.wait_ge(s["sl"], SC * b)
                        if tail:
                            pe.wait_ge(s["yo"], TB * (b - 1))
                        for k in range(SC):
                            last = nc.tensor.transpose(mb[:, k * P:(k + 1) * P], sl[:, k, :], T["ident"][:, :])
                        last.then_inc(s["slt_ps"], 1)
                    if front:
                        token_logits(1).then_inc(s["la"], 1)
                        need(pe, s["comb"], b)
                        for k in range(SC):
                            w = T["se_hi"][:, k * P:(k + 1) * P], T["se_lo"][:, k * P:(k + 1) * P]
                            nc.tensor.matmul(pb[:, k, :], w[0], xnt_hi[:, :], start=(k % 2 == 0), stop=False, skip_group_check=True)
                            nc.tensor.matmul(pb[:, k, :], w[0], xnt_lo[:, :], start=False, stop=False, skip_group_check=True)
                            last = nc.tensor.matmul(pb[:, k, :], w[1], xnt_hi[:, :], start=False, stop=False, skip_group_check=True)
                        last.then_inc(s["lb"], 1)
                    if back:
                        for j in range(HC):
                            if j == 0:
                                pe.wait_ge(s["slt_lo"], b)
                            if j >= 2:
                                pe.wait_ge(s["hid"], HC * (b - 1) + j - 1)
                            cols = slice(j * P, (j + 1) * P)
                            exact(pc[:, j % 2, :], (T["w1_hi"][:, cols], T["w1_lo"][:, cols]), (slt_hi[:, :], slt_lo[:, :])).then_inc(s["h_ps"], 1)
                    if front:
                        pe.wait_ge(s["d"], (SC + TB) * (b + 1))
                        for t in range(TB):
                            last = nc.tensor.matmul(pa[:, t, :], T["ones_r"][:, :], d_slot[:, :, :].rearrange("p c n -> p (c n)"),
                                                    start=False, stop=True, skip_group_check=True)
                        last.then_inc(s["fa"], 1)
                        for k in range(SC):
                            last = nc.tensor.matmul(pb[:, k, :], T["ones_r"][:, :], d_tok[:, :, :].rearrange("p t n -> p (t n)"),
                                                    start=False, stop=True, skip_group_check=True)
                        last.then_inc(s["fb"], 1)

                pe.wait_ge(s["one"], 3)
                pe.wait_ge(s["gdiag"], 1)
                windows(pe, window)


_INS = ['L0_attn_q', 'L0_attn_W_query', 'L0_attn_W_key', 'L0_attn_W_val', 'L0_attn_W_out', 'L0_ffn_gate_w',
        'L0_ffn_expert_gate', 'L0_ffn_expert_up', 'L0_ffn_expert_down', 'L0_ffn_shared_gate_w', 'L0_ffn_shared_up_w',
        'L0_ffn_shared_down_w', 'L0_c', 'L0_wmod', 'L1_attn_Wqkv', 'L1_attn_bqkv', 'L1_attn_Wln', 'L1_attn_bln',
        'L1_ffn_gamma_x', 'L1_ffn_gamma_slot', 'L1_ffn_slot_embeds', 'L1_ffn_w1', 'L1_ffn_w2', 'L1_c', 'L1_wmod']


def kernel(**inputs):
    import numpy as _np
    import concourse.bacc as _bacc
    from concourse import mybir as _mybir
    from concourse.bass_utils import run_bass_kernel_spmd as _run

    nc = _bacc.Bacc("TRN2", target_bir_lowering=False, num_devices=1)
    arrays, aps = {}, {}
    for name in _INS:
        a = _np.ascontiguousarray(inputs[name])
        arrays[f"in_{name}_dram"] = a
        aps[name] = nc.dram_tensor(f"in_{name}_dram", a.shape, _mybir.dt.from_np(a.dtype), kind="ExternalInput").ap()
    rows = row_constants()
    arrays["rows_dram"] = rows
    aps["rows"] = nc.dram_tensor("rows_dram", rows.shape, _mybir.dt.from_np(rows.dtype), kind="ExternalInput").ap()
    out = nc.dram_tensor("out_dram", (B, S, D), F32, kind="ExternalOutput").ap()
    network(nc, aps, out)
    r = _run(nc, [arrays], core_ids=[0])
    return r.results[0]["out_dram"]
```
